# Optimizing a Trainium2 kernel written in Bass

```python
import numpy as np
import jax
import jax.numpy as jnp

def _softmax(x, axis=-1):
    return jax.nn.softmax(x, axis=axis)

def _gelu(x):
    return jax.nn.gelu(x, approximate=True)

def _silu(x):
    return jax.nn.silu(x)

def _sigmoid(x):
    return jax.nn.sigmoid(x)

def _layernorm(x, axis=-1, eps=1e-05):
    m = jnp.mean(x, axis=axis, keepdims=True)
    v = jnp.var(x, axis=axis, keepdims=True)
    return (x - m) / jnp.sqrt(v + eps)

def _scatter_add(tgt, idx, src, axis=0):
    return tgt.at[idx].add(src)

def _segment_sum(src, seg, n):
    return jax.ops.segment_sum(src, seg, n)
kernel_name = 'mk_seq_preln_d1_jaxref_r8_d5b1f8'

def setup_inputs(seed: int=0):
    np.random.seed(seed)
    _w = jnp.asarray

    def _L0_attn_setup():
        import jax, jax.numpy as jnp
        import numpy as np
        D, H, DK, DV, F, R = (128, 16, 64, 64, 512, 64)
        B, T = (4, 256)
        KCONV = 4
        EPS = 1e-06

        def rmsnorm(x, w):
            return x * jax.lax.rsqrt(jnp.mean(x * x, axis=-1, keepdims=True) + EPS) * w

        def _reference_tuple_inner(x, norm_in_w, conv_w, conv_b, q_w, k_w, v_w, out_w, alpha_w, alpha_b, beta_w, beta_b, head_norm_w, u1_w, u1_b, u2_w, u2_b, ff_norm_w, ff_w1, ff_w3, ff_w2):
            bsz, seq, _ = x.shape
            h = rmsnorm(x, norm_in_w)
            hc = jax.lax.conv_general_dilated(h.transpose(0, 2, 1), conv_w, (1,), [(KCONV - 1, 0)], dimension_numbers=('NCH', 'OIH', 'NCH'), feature_group_count=D)
            h = jax.nn.silu((hc + conv_b[None, :, None]).transpose(0, 2, 1))
            q = (h @ q_w).reshape(bsz, seq, H, DK)
            k = (h @ k_w).reshape(bsz, seq, H, DK)
            v = (h @ v_w).reshape(bsz, seq, H, DV)
            q = q / (jnp.linalg.norm(q, axis=-1, keepdims=True) + EPS)
            k = k / (jnp.linalg.norm(k, axis=-1, keepdims=True) + EPS)
            alpha = jax.nn.sigmoid(h @ alpha_w + alpha_b).reshape(bsz, seq, H, DK)
            beta = jax.nn.sigmoid(h @ beta_w + beta_b)

            def step(s, inp):
                qt, kt, vt, at, bt = inp
                s = s * at[..., None]
                u = jnp.einsum('bhd,bhdv->bhv', kt, s)
                s = s + bt[..., None, None] * (kt[..., None] * (vt - u)[..., None, :])
                out = jnp.einsum('bhdv,bhd->bhv', s, qt)
                return (s, out)
            tm = lambda a: jnp.swapaxes(a, 0, 1)
            s0 = jnp.zeros((bsz, H, DK, DV), x.dtype)
            s_final, outs = jax.lax.scan(step, s0, (tm(q), tm(k), tm(v), tm(alpha), tm(beta)))
            y = tm(outs)
            y = y * jax.lax.rsqrt(jnp.mean(y * y, axis=-1, keepdims=True) + EPS) * head_norm_w
            y = y.reshape(bsz, seq, H * DV)
            gate = jax.nn.sigmoid(jax.nn.silu(x @ u1_w + u1_b) @ u2_w + u2_b)
            y = x + y @ out_w * gate
            y2 = rmsnorm(y, ff_norm_w)
            y = y + jax.nn.silu(y2 @ ff_w1) * (y2 @ ff_w3) @ ff_w2
            return (y, s_final)
        key = jax.random.key(seed)
        ks = jax.random.split(key, 16)
        n = lambda k, shape: jax.random.normal(k, shape, jnp.float32) * 0.02
        return dict(x=jax.random.normal(ks[0], (B, T, D), jnp.float32), norm_in_w=jnp.ones((D,), jnp.float32), conv_w=n(ks[1], (D, 1, KCONV)), conv_b=jnp.zeros((D,), jnp.float32), q_w=n(ks[2], (D, H * DK)), k_w=n(ks[3], (D, H * DK)), v_w=n(ks[4], (D, H * DV)), out_w=n(ks[5], (H * DV, D)), alpha_w=n(ks[6], (D, H * DK)), alpha_b=jnp.zeros((H * DK,), jnp.float32), beta_w=n(ks[7], (D, H)), beta_b=jnp.zeros((H,), jnp.float32), head_norm_w=jnp.ones((H, DV), jnp.float32), u1_w=n(ks[8], (D, R)), u1_b=jnp.zeros((R,), jnp.float32), u2_w=n(ks[9], (R, D)), u2_b=jnp.zeros((D,), jnp.float32), ff_norm_w=jnp.ones((D,), jnp.float32), ff_w1=n(ks[10], (D, F)), ff_w3=n(ks[11], (D, F)), ff_w2=n(ks[12], (F, D)))
    _L0_attn_in = _L0_attn_setup()

    def _L0_ffn_setup():
        import jax, jax.numpy as jnp
        import numpy as np
        DIM = 128
        DEPTH = 2
        HEADS = 8
        DIM_HEAD = 64
        WINDOW = 64
        INNER = HEADS * DIM_HEAD
        HID = int(DIM * 4 * 2 / 3)
        B, N = (2, 1024)
        QK_SCALE = 8.0

        def shift_token(t):
            t1, t2 = jnp.split(t, 2, axis=-1)
            t2 = jnp.pad(t2, ((0, 0), (1, 0), (0, 0)))[:, :-1]
            return jnp.concatenate([t1, t2], axis=-1)

        def l2norm(t):
            return t / jnp.clip(jnp.linalg.norm(t, axis=-1, keepdims=True), 1e-12)

        def rotate_half(x):
            x1, x2 = jnp.split(x, 2, axis=-1)
            return jnp.concatenate([-x2, x1], axis=-1)

        def rotary_xpos(q, k):
            n = q.shape[-2]
            half_idx = jnp.arange(0, DIM_HEAD, 2, dtype=jnp.float32)
            inv_freq = 1.0 / 10000.0 ** (half_idx / DIM_HEAD)
            t = jnp.arange(n, dtype=jnp.float32)
            freqs = t[:, None] * inv_freq[None, :]
            freqs = jnp.concatenate([freqs, freqs], axis=-1)
            base = (half_idx + 0.4 * DIM_HEAD) / (1.4 * DIM_HEAD)
            power = (t - n // 2) / float(WINDOW // 2)
            scale = base[None, :] ** power[:, None]
            scale = jnp.concatenate([scale, scale], axis=-1)
            cos, sin = (jnp.cos(freqs), jnp.sin(freqs))
            q = q * cos * scale + rotate_half(q) * sin * scale
            k = k * cos / scale + rotate_half(k) * sin / scale
            return (q, k)

        def local_attention(q, k, v):
            b, h, n, d = q.shape
            w = n // WINDOW
            bq = q.reshape(b, h, w, WINDOW, d) * QK_SCALE
            bk = k.reshape(b, h, w, WINDOW, d)
            bv = v.reshape(b, h, w, WINDOW, d)

            def look_around(t):
                p = jnp.pad(t, ((0, 0), (0, 0), (1, 0), (0, 0), (0, 0)))
                return jnp.concatenate([p[:, :, :w], p[:, :, 1:]], axis=3)
            bk, bv = (look_around(bk), look_around(bv))
            bt = jnp.arange(n).reshape(w, WINDOW)
            btp = jnp.pad(bt, ((1, 0), (0, 0)), constant_values=-1)
            btk = jnp.concatenate([btp[:w], btp[1:]], axis=1)
            sim = jnp.einsum('bhwid,bhwjd->bhwij', bq, bk)
            i = bt[:, :, None]
            j = btk[:, None, :]
            mask = (i < j) | (i > j + WINDOW) | (j == -1)
            sim = jnp.where(mask, -jnp.finfo(sim.dtype).max, sim)
            attn = jax.nn.softmax(sim, axis=-1)
            out = jnp.einsum('bhwij,bhwjd->bhwid', attn, bv)
            return out.reshape(b, h, n, d)

        def _layer(x, wqkv, qs, ksc, wo, lg, lb, w1, b1, w2, b2):
            b, n, _ = x.shape
            h = shift_token(x)
            qkv = h @ wqkv
            q, k, v = jnp.split(qkv, 3, axis=-1)
            to_heads = lambda t: t.reshape(b, n, HEADS, DIM_HEAD).transpose(0, 2, 1, 3)
            q, k, v = (to_heads(q), to_heads(k), to_heads(v))
            q = l2norm(q) * qs
            k = l2norm(k) * ksc
            q, k = rotary_xpos(q, k)
            o = local_attention(q, k, v)
            o = o.transpose(0, 2, 1, 3).reshape(b, n, INNER)
            x = x + o @ wo
            h = shift_token(x)
            mu = h.mean(-1, keepdims=True)
            var = h.var(-1, keepdims=True)
            h = (h - mu) / jnp.sqrt(var + 1e-05) * lg + lb
            h = h @ w1 + b1
            a, g = jnp.split(h, 2, axis=-1)
            h = a * jax.nn.gelu(g, approximate=False)
            x = x + h @ w2 + b2
            return x
        key = jax.random.key(seed)
        ks = jax.random.split(key, 6)
        return {'x': jax.random.normal(ks[0], (B, N, DIM), jnp.float32), 'wqkv': jax.random.normal(ks[1], (DEPTH, DIM, 3 * INNER), jnp.float32) * 0.02, 'q_scale': jnp.ones((DEPTH, DIM_HEAD), jnp.float32), 'k_scale': jnp.ones((DEPTH, DIM_HEAD), jnp.float32), 'wo': jax.random.normal(ks[2], (DEPTH, INNER, DIM), jnp.float32) * 0.02, 'ln_g': jnp.ones((DEPTH, DIM), jnp.float32), 'ln_b': jnp.zeros((DEPTH, DIM), jnp.float32), 'w1': jax.random.normal(ks[3], (DEPTH, DIM, 2 * HID), jnp.float32) * 0.02, 'b1': jnp.zeros((DEPTH, 2 * HID), jnp.float32), 'w2': jax.random.normal(ks[4], (DEPTH, HID, DIM), jnp.float32) * 0.02, 'b2': jnp.zeros((DEPTH, DIM), jnp.float32)}
    _L0_ffn_in = _L0_ffn_setup()
    _d = {'L0_attn_x': _L0_attn_in['x'], 'L0_attn_norm_in_w': _L0_attn_in['norm_in_w'], 'L0_attn_conv_w': _L0_attn_in['conv_w'], 'L0_attn_conv_b': _L0_attn_in['conv_b'], 'L0_attn_q_w': _L0_attn_in['q_w'], 'L0_attn_k_w': _L0_attn_in['k_w'], 'L0_attn_v_w': _L0_attn_in['v_w'], 'L0_attn_out_w': _L0_attn_in['out_w'], 'L0_attn_alpha_w': _L0_attn_in['alpha_w'], 'L0_attn_alpha_b': _L0_attn_in['alpha_b'], 'L0_attn_beta_w': _L0_attn_in['beta_w'], 'L0_attn_beta_b': _L0_attn_in['beta_b'], 'L0_attn_head_norm_w': _L0_attn_in['head_norm_w'], 'L0_attn_u1_w': _L0_attn_in['u1_w'], 'L0_attn_u1_b': _L0_attn_in['u1_b'], 'L0_attn_u2_w': _L0_attn_in['u2_w'], 'L0_attn_u2_b': _L0_attn_in['u2_b'], 'L0_attn_ff_norm_w': _L0_attn_in['ff_norm_w'], 'L0_attn_ff_w1': _L0_attn_in['ff_w1'], 'L0_attn_ff_w3': _L0_attn_in['ff_w3'], 'L0_attn_ff_w2': _L0_attn_in['ff_w2'], 'L0_ffn_wqkv': _L0_ffn_in['wqkv'], 'L0_ffn_q_scale': _L0_ffn_in['q_scale'], 'L0_ffn_k_scale': _L0_ffn_in['k_scale'], 'L0_ffn_wo': _L0_ffn_in['wo'], 'L0_ffn_ln_g': _L0_ffn_in['ln_g'], 'L0_ffn_ln_b': _L0_ffn_in['ln_b'], 'L0_ffn_w1': _L0_ffn_in['w1'], 'L0_ffn_b1': _L0_ffn_in['b1'], 'L0_ffn_w2': _L0_ffn_in['w2'], 'L0_ffn_b2': _L0_ffn_in['b2']}
    _x0 = _d['L0_attn_x']
    _d['L0_attn_x'] = jax.random.normal(jax.random.fold_in(jax.random.key(seed), 1), (4, 512, 128), dtype=_x0.dtype)
    del _x0
    return _d

def reference(L0_attn_x, L0_attn_norm_in_w, L0_attn_conv_w, L0_attn_conv_b, L0_attn_q_w, L0_attn_k_w, L0_attn_v_w, L0_attn_out_w, L0_attn_alpha_w, L0_attn_alpha_b, L0_attn_beta_w, L0_attn_beta_b, L0_attn_head_norm_w, L0_attn_u1_w, L0_attn_u1_b, L0_attn_u2_w, L0_attn_u2_b, L0_attn_ff_norm_w, L0_attn_ff_w1, L0_attn_ff_w3, L0_attn_ff_w2, L0_ffn_wqkv, L0_ffn_q_scale, L0_ffn_k_scale, L0_ffn_wo, L0_ffn_ln_g, L0_ffn_ln_b, L0_ffn_w1, L0_ffn_b1, L0_ffn_w2, L0_ffn_b2):

    def _L0_attn_ref(x, norm_in_w, conv_w, conv_b, q_w, k_w, v_w, out_w, alpha_w, alpha_b, beta_w, beta_b, head_norm_w, u1_w, u1_b, u2_w, u2_b, ff_norm_w, ff_w1, ff_w3, ff_w2):
        import jax, jax.numpy as jnp
        import numpy as np
        D, H, DK, DV, F, R = (128, 16, 64, 64, 512, 64)
        B, T = (4, 256)
        KCONV = 4
        EPS = 1e-06

        def rmsnorm(x, w):
            return x * jax.lax.rsqrt(jnp.mean(x * x, axis=-1, keepdims=True) + EPS) * w

        def _reference_tuple_inner(x, norm_in_w, conv_w, conv_b, q_w, k_w, v_w, out_w, alpha_w, alpha_b, beta_w, beta_b, head_norm_w, u1_w, u1_b, u2_w, u2_b, ff_norm_w, ff_w1, ff_w3, ff_w2):
            bsz, seq, _ = x.shape
            h = rmsnorm(x, norm_in_w)
            hc = jax.lax.conv_general_dilated(h.transpose(0, 2, 1), conv_w, (1,), [(KCONV - 1, 0)], dimension_numbers=('NCH', 'OIH', 'NCH'), feature_group_count=D)
            h = jax.nn.silu((hc + conv_b[None, :, None]).transpose(0, 2, 1))
            q = (h @ q_w).reshape(bsz, seq, H, DK)
            k = (h @ k_w).reshape(bsz, seq, H, DK)
            v = (h @ v_w).reshape(bsz, seq, H, DV)
            q = q / (jnp.linalg.norm(q, axis=-1, keepdims=True) + EPS)
            k = k / (jnp.linalg.norm(k, axis=-1, keepdims=True) + EPS)
            alpha = jax.nn.sigmoid(h @ alpha_w + alpha_b).reshape(bsz, seq, H, DK)
            beta = jax.nn.sigmoid(h @ beta_w + beta_b)

            def step(s, inp):
                qt, kt, vt, at, bt = inp
                s = s * at[..., None]
                u = jnp.einsum('bhd,bhdv->bhv', kt, s)
                s = s + bt[..., None, None] * (kt[..., None] * (vt - u)[..., None, :])
                out = jnp.einsum('bhdv,bhd->bhv', s, qt)
                return (s, out)
            tm = lambda a: jnp.swapaxes(a, 0, 1)
            s0 = jnp.zeros((bsz, H, DK, DV), x.dtype)
            s_final, outs = jax.lax.scan(step, s0, (tm(q), tm(k), tm(v), tm(alpha), tm(beta)))
            y = tm(outs)
            y = y * jax.lax.rsqrt(jnp.mean(y * y, axis=-1, keepdims=True) + EPS) * head_norm_w
            y = y.reshape(bsz, seq, H * DV)
            gate = jax.nn.sigmoid(jax.nn.silu(x @ u1_w + u1_b) @ u2_w + u2_b)
            y = x + y @ out_w * gate
            y2 = rmsnorm(y, ff_norm_w)
            y = y + jax.nn.silu(y2 @ ff_w1) * (y2 @ ff_w3) @ ff_w2
            return (y, s_final)
        return _reference_tuple_inner(x, norm_in_w, conv_w, conv_b, q_w, k_w, v_w, out_w, alpha_w, alpha_b, beta_w, beta_b, head_norm_w, u1_w, u1_b, u2_w, u2_b, ff_norm_w, ff_w1, ff_w3, ff_w2)[0]

    def _L0_ffn_ref(x, wqkv, q_scale, k_scale, wo, ln_g, ln_b, w1, b1, w2, b2):
        import jax, jax.numpy as jnp
        import numpy as np
        DIM = 128
        DEPTH = 2
        HEADS = 8
        DIM_HEAD = 64
        WINDOW = 64
        INNER = HEADS * DIM_HEAD
        HID = int(DIM * 4 * 2 / 3)
        B, N = (2, 1024)
        QK_SCALE = 8.0

        def shift_token(t):
            t1, t2 = jnp.split(t, 2, axis=-1)
            t2 = jnp.pad(t2, ((0, 0), (1, 0), (0, 0)))[:, :-1]
            return jnp.concatenate([t1, t2], axis=-1)

        def l2norm(t):
            return t / jnp.clip(jnp.linalg.norm(t, axis=-1, keepdims=True), 1e-12)

        def rotate_half(x):
            x1, x2 = jnp.split(x, 2, axis=-1)
            return jnp.concatenate([-x2, x1], axis=-1)

        def rotary_xpos(q, k):
            n = q.shape[-2]
            half_idx = jnp.arange(0, DIM_HEAD, 2, dtype=jnp.float32)
            inv_freq = 1.0 / 10000.0 ** (half_idx / DIM_HEAD)
            t = jnp.arange(n, dtype=jnp.float32)
            freqs = t[:, None] * inv_freq[None, :]
            freqs = jnp.concatenate([freqs, freqs], axis=-1)
            base = (half_idx + 0.4 * DIM_HEAD) / (1.4 * DIM_HEAD)
            power = (t - n // 2) / float(WINDOW // 2)
            scale = base[None, :] ** power[:, None]
            scale = jnp.concatenate([scale, scale], axis=-1)
            cos, sin = (jnp.cos(freqs), jnp.sin(freqs))
            q = q * cos * scale + rotate_half(q) * sin * scale
            k = k * cos / scale + rotate_half(k) * sin / scale
            return (q, k)

        def local_attention(q, k, v):
            b, h, n, d = q.shape
            w = n // WINDOW
            bq = q.reshape(b, h, w, WINDOW, d) * QK_SCALE
            bk = k.reshape(b, h, w, WINDOW, d)
            bv = v.reshape(b, h, w, WINDOW, d)

            def look_around(t):
                p = jnp.pad(t, ((0, 0), (0, 0), (1, 0), (0, 0), (0, 0)))
                return jnp.concatenate([p[:, :, :w], p[:, :, 1:]], axis=3)
            bk, bv = (look_around(bk), look_around(bv))
            bt = jnp.arange(n).reshape(w, WINDOW)
            btp = jnp.pad(bt, ((1, 0), (0, 0)), constant_values=-1)
            btk = jnp.concatenate([btp[:w], btp[1:]], axis=1)
            sim = jnp.einsum('bhwid,bhwjd->bhwij', bq, bk)
            i = bt[:, :, None]
            j = btk[:, None, :]
            mask = (i < j) | (i > j + WINDOW) | (j == -1)
            sim = jnp.where(mask, -jnp.finfo(sim.dtype).max, sim)
            attn = jax.nn.softmax(sim, axis=-1)
            out = jnp.einsum('bhwij,bhwjd->bhwid', attn, bv)
            return out.reshape(b, h, n, d)

        def _layer(x, wqkv, qs, ksc, wo, lg, lb, w1, b1, w2, b2):
            b, n, _ = x.shape
            h = shift_token(x)
            qkv = h @ wqkv
            q, k, v = jnp.split(qkv, 3, axis=-1)
            to_heads = lambda t: t.reshape(b, n, HEADS, DIM_HEAD).transpose(0, 2, 1, 3)
            q, k, v = (to_heads(q), to_heads(k), to_heads(v))
            q = l2norm(q) * qs
            k = l2norm(k) * ksc
            q, k = rotary_xpos(q, k)
            o = local_attention(q, k, v)
            o = o.transpose(0, 2, 1, 3).reshape(b, n, INNER)
            x = x + o @ wo
            h = shift_token(x)
            mu = h.mean(-1, keepdims=True)
            var = h.var(-1, keepdims=True)
            h = (h - mu) / jnp.sqrt(var + 1e-05) * lg + lb
            h = h @ w1 + b1
            a, g = jnp.split(h, 2, axis=-1)
            h = a * jax.nn.gelu(g, approximate=False)
            x = x + h @ w2 + b2
            return x
        for l in range(DEPTH):
            x = _layer(x, wqkv[l], q_scale[l], k_scale[l], wo[l], ln_g[l], ln_b[l], w1[l], b1[l], w2[l], b2[l])
        return x
    x = L0_attn_x
    x = x + _L0_attn_ref(_layernorm(x, axis=-1), L0_attn_norm_in_w, L0_attn_conv_w, L0_attn_conv_b, L0_attn_q_w, L0_attn_k_w, L0_attn_v_w, L0_attn_out_w, L0_attn_alpha_w, L0_attn_alpha_b, L0_attn_beta_w, L0_attn_beta_b, L0_attn_head_norm_w, L0_attn_u1_w, L0_attn_u1_b, L0_attn_u2_w, L0_attn_u2_b, L0_attn_ff_norm_w, L0_attn_ff_w1, L0_attn_ff_w3, L0_attn_ff_w2)
    x = x + _L0_ffn_ref(_layernorm(x, axis=-1), L0_ffn_wqkv, L0_ffn_q_scale, L0_ffn_k_scale, L0_ffn_wo, L0_ffn_ln_g, L0_ffn_ln_b, L0_ffn_w1, L0_ffn_b1, L0_ffn_w2, L0_ffn_b2)
    return x

_drawn_inputs = setup_inputs


def setup_inputs(seed=0):
    import zlib

    import numpy as np

    out = dict(_drawn_inputs(seed))
    spreads = {'L0_attn_norm_in_w': (1.0, 0.6),
     'L0_attn_conv_b': (0.0, 0.1),
     'L0_attn_alpha_b': (0.0, 0.8),
     'L0_attn_beta_b': (0.0, 0.8),
     'L0_attn_head_norm_w': (1.0, 0.6),
     'L0_attn_u1_b': (0.0, 0.8),
     'L0_attn_u2_b': (0.0, 0.8),
     'L0_attn_ff_norm_w': (1.0, 0.6),
     'L0_ffn_q_scale': (1.0, 0.6),
     'L0_ffn_k_scale': (1.0, 0.6),
     'L0_ffn_ln_g': (1.0, 0.6),
     'L0_ffn_ln_b': (0.0, 0.8),
     'L0_ffn_b1': (0.0, 0.8),
     'L0_ffn_b2': (0.0, 0.8)}
    factors = {'L0_attn_alpha_w': 8.0,
     'L0_attn_beta_w': 8.0,
     'L0_attn_u1_w': 8.0,
     'L0_attn_u2_w': 8.0,
     'L0_attn_ff_w1': 8.0,
     'L0_attn_ff_w3': 8.0,
     'L0_attn_ff_w2': 8.0,
     'L0_ffn_wqkv': 5.357,
     'L0_ffn_wo': 5.308,
     'L0_ffn_w1': 8.0,
     'L0_ffn_w2': 8.0}
    for name, (base, spread) in spreads.items():
        noise = np.random.default_rng([zlib.crc32(name.encode()), seed]).standard_normal(out[name].shape)
        drawn = base * np.exp(spread * noise) if base else spread * noise
        out[name] = jnp.asarray(drawn.astype(out[name].dtype))
    for name, factor in factors.items():
        out[name] = (out[name] * factor).astype(out[name].dtype)
    return out
```

```python
from contextlib import ExitStack

import numpy as np

import concourse.bass as bass
from concourse import mybir

F32 = mybir.dt.float32
ALU = mybir.AluOpType
ACT = mybir.ActivationFunctionType
AX = mybir.AxisListType

P = 128
B, T, D = 4, 512, 128
C = 128
NC = T // C
TOK = B * T
H, DK = 16, 64
HP = H // 2
LEVELS = 7
HALF = C // 2
KCONV = 4
R = 64
RMS_EPS = 1e-6
LN_EPS = 1e-5


class Signal:

    def __init__(self, ctx, nc, name, per=1):
        self.sem = ctx.enter_context(nc.semaphore(name))
        self.per = per

    def at(self, hp, b, k=None):
        k = self.per if k is None else k
        return hp * (B * self.per) + ((b + 1) * self.per + k)


def view(t, offset, dims, parts=P, part0=0):
    row = 1
    for s in t.shape[1:]:
        row *= s
    return bass.AP(tensor=t, offset=part0 * row + offset, ap=[[row, parts]] + [list(d) for d in dims])


def halves(t, offset, n, second, count, outer=None, parts=P, part0=0):
    dims = [[2 * n, count // (2 * n)], [1, n]] if n > 1 else [[2, count // 2]]
    return view(t, offset + (n if second else 0), ([outer] if outer else []) + dims, parts, part0)


def level_consts():
    j = np.arange(C)[:, None]
    masks = np.zeros((C, LEVELS, NC * HALF), np.float32)
    for l in range(LEVELS):
        n = 1 << l
        i = np.arange(HALF)[None, :]
        block = i // n
        one = ((j // (2 * n)) == block) & ((j % (2 * n)) < n)
        masks[:, l, :] = np.tile(one.astype(np.float32), (1, NC))
    return masks


def stage_a(nc, io, keep, per_batch):
    with ExitStack() as ctx:
        sb = lambda n, s: ctx.enter_context(nc.sbuf_tensor("a_" + n, s, F32))
        ps = lambda n, s: ctx.enter_context(nc.psum_tensor("a_" + n, s, F32))
        sig = lambda n, per=1: Signal(ctx, nc, "a_" + n, per)
        ident, mean_w = keep["ident"], keep["mean_w"]
        xT, xnT, hT, gateT, beta = (keep[k] for k in ("xT", "xnT", "hT", "gateT", "beta"))

        norm_w = sb("norm_w", [P, 1]); conv_w = sb("conv_w", [P, KCONV]); conv_b = sb("conv_b", [P, 1])
        u1_w = sb("u1_w", [P, R]); u1_b = sb("u1_b", [R, 1]); u2_w = sb("u2_w", [R, D]); u2_b = sb("u2_b", [P, 1])
        beta_w = sb("beta_w", [P, H]); beta_b = sb("beta_b", [P, H])
        xs = sb("xs", [P, NC, D])
        xc = sb("xc", [P, T]); xm = sb("xm", [P, T]); sq = sb("sq", [P, T]); sd = sb("sd", [P, T])
        rs = sb("rs", [P, T]); xn = sb("xn", [P, T]); hpad = sb("hpad", [P, KCONV - 1 + T])
        cv = sb("cv", [P, T]); hs = sb("hs", [P, T]); g1 = sb("g1", [R, T]); bz = sb("bz", [P, NC, H])
        pX = ps("pX", [P, T]); pM = ps("pM", [P, T]); pV = ps("pV", [P, T]); pR = ps("pR", [P, T])
        pG = ps("pG", [P, T]); pU = ps("pU", [P, T]); pB = ps("pB", [P, NC * H])

        weights_in = ctx.enter_context(nc.semaphore("a_weights_in"))
        x_in = ctx.enter_context(nc.semaphore("a_x_in"))
        pad_zero = ctx.enter_context(nc.semaphore("a_pad_zero"))
        transposed, mean_mm, var_mm, ms_mm = sig("transposed"), sig("mean_mm"), sig("var_mm"), sig("ms_mm")
        u1_mm, u2_mm, beta_mm = sig("u1_mm"), sig("u2_mm"), sig("beta_mm")
        x_copied, sq_var, sd_var, sq_ms, sd_ms = sig("x_copied"), sig("sq_var"), sig("sd_var"), sig("sq_ms"), sig("sd_ms")
        silu_h, silu_g, gate_done, beta_done = sig("silu_h"), sig("silu_g"), sig("gate_done"), sig("beta_done")
        centred, r_var, normed, r_ms, scaled, conv, beta_sum = (
            sig("centred"), sig("r_var"), sig("normed"), sig("r_ms"), sig("scaled"), sig("conv", KCONV), sig("beta_sum"))
        kept = sig("kept", 3)
        x_view = io["x"].rearrange("b (c p) d -> b p c d", p=P)
        loads = [(norm_w[:, :], io["norm_in_w"].rearrange("(p o) -> p o", o=1)),
                 (conv_w[:, :], io["conv_w"].rearrange("p o k -> p (o k)")),
                 (conv_b[:, :], io["conv_b"].rearrange("(p o) -> p o", o=1)),
                 (u1_w[:, :], io["u1_w"]), (u1_b[:, :], io["u1_b"].rearrange("(p o) -> p o", o=1)),
                 (u2_w[:, :], io["u2_w"]), (u2_b[:, :], io["u2_b"].rearrange("(p o) -> p o", o=1)),
                 (beta_w[:, :], io["beta_w"]),
                 (beta_b[:, :], io["beta_b"].rearrange("(o h) -> o h", o=1).to_broadcast([P, H])),
                 (ident[:, :], io["ident"]), (mean_w[:, :], io["mean_w"])]
        block = ctx.enter_context(nc.Block())

        def at(s, b, k=None):
            return s.at(0, 0, k) if isinstance(b, int) and b == 0 else b * s.per + (s.per + (k or s.per))

        def before(s, b, k=None):
            return b * s.per + (k or s.per)

        @block.sync
        def _(sp):
            for dst, src in loads:
                sp.dma_start(dst, src).then_inc(weights_in, 16)
            with sp.Fori(0, B) as b:
                sp.wait_ge(transposed.sem, before(transposed, b))
                sp.dma_start(xs[:, :, :], x_view[b]).then_inc(x_in, 16)

        @block.tensor
        def _(pe):
            pe.sem_inc(transposed.sem, 1)
            pe.sem_inc(mean_mm.sem, 1); pe.sem_inc(var_mm.sem, 1); pe.sem_inc(ms_mm.sem, 1)
            pe.sem_inc(u1_mm.sem, 1); pe.sem_inc(u2_mm.sem, 1); pe.sem_inc(beta_mm.sem, 1)
            pe.wait_ge(weights_in, 16 * len(loads))
            with pe.Fori(0, B) as b:
                pe.wait_ge(x_in, b * 16 + 16)
                pe.wait_ge(x_copied.sem, before(x_copied, b))
                for c in range(NC):
                    last = nc.tensor.transpose(pX[:, c * C:(c + 1) * C], xs[:, c, :], ident[:, :])
                last.then_inc(transposed.sem, 1)
                pe.wait_ge(x_copied.sem, at(x_copied, b))
                pe.wait_ge(centred.sem, before(centred, b))
                nc.tensor.matmul(pM[:, :], mean_w[:, :], xc[:, :], start=True, stop=True).then_inc(mean_mm.sem, 1)
                pe.wait_ge(sq_var.sem, at(sq_var, b))
                pe.wait_ge(sd_var.sem, before(sd_var, b))
                nc.tensor.matmul(pV[:, :], mean_w[:, :], sq[:, :], start=True, stop=True).then_inc(var_mm.sem, 1)
                pe.wait_ge(normed.sem, at(normed, b))
                pe.wait_ge(silu_g.sem, before(silu_g, b))
                nc.tensor.matmul(pG[0:R, :], u1_w[:, :], xn[:, :], start=True, stop=True).then_inc(u1_mm.sem, 1)
                pe.wait_ge(sq_ms.sem, at(sq_ms, b))
                pe.wait_ge(sd_ms.sem, before(sd_ms, b))
                nc.tensor.matmul(pR[:, :], mean_w[:, :], sq[:, :], start=True, stop=True).then_inc(ms_mm.sem, 1)
                pe.wait_ge(silu_g.sem, at(silu_g, b))
                pe.wait_ge(gate_done.sem, before(gate_done, b))
                nc.tensor.matmul(pU[:, :], u2_w[:, :], g1[:, :], start=True, stop=True).then_inc(u2_mm.sem, 1)
                pe.wait_ge(silu_h.sem, at(silu_h, b))
                pe.wait_ge(beta_sum.sem, before(beta_sum, b))
                for c in range(NC):
                    last = nc.tensor.matmul(pB[:, c * H:(c + 1) * H], hs[:, c * C:(c + 1) * C], beta_w[:, :],
                                            start=True, stop=True)
                last.then_inc(beta_mm.sem, 1)

        @block.scalar
        def _(act):
            for s in (x_copied, sq_var, sd_var, sq_ms, sd_ms, silu_h, silu_g, gate_done, beta_done):
                act.sem_inc(s.sem, 1)
            act.wait_ge(weights_in, 16 * len(loads))
            with act.Fori(0, B) as b:
                act.wait_ge(transposed.sem, at(transposed, b))
                act.wait_ge(centred.sem, before(centred, b))
                act.wait_ge(kept.sem, before(kept, b))
                nc.scalar.activation(xc[:, :], pX[:, :], ACT.Copy).then_inc(x_copied.sem, 1)
                act.wait_ge(centred.sem, at(centred, b))
                nc.scalar.activation(sq[:, :], xm[:, :], ACT.Square).then_inc(sq_var.sem, 1)
                act.wait_ge(var_mm.sem, at(var_mm, b))
                nc.scalar.activation(sd[:, :], pV[:, :], ACT.Sqrt, bias=keep["ln_eps"][:, :]).then_inc(sd_var.sem, 1)
                act.wait_ge(normed.sem, at(normed, b))
                nc.scalar.activation(sq[:, :], xn[:, :], ACT.Square).then_inc(sq_ms.sem, 1)
                act.wait_ge(ms_mm.sem, at(ms_mm, b))
                act.wait_ge(r_var.sem, at(r_var, b))
                nc.scalar.activation(sd[:, :], pR[:, :], ACT.Sqrt, bias=keep["rms_eps"][:, :]).then_inc(sd_ms.sem, 1)
                act.wait_ge(u1_mm.sem, at(u1_mm, b))
                act.wait_ge(u2_mm.sem, before(u2_mm, b))
                nc.scalar.activation(g1[:, :], pG[0:R, :], ACT.Silu, bias=u1_b[:, :]).then_inc(silu_g.sem, 1)
                act.wait_ge(conv.sem, at(conv, b))
                act.wait_ge(beta_mm.sem, before(beta_mm, b))
                nc.scalar.activation(hs[:, :], cv[:, :], ACT.Silu).then_inc(silu_h.sem, 1)
                act.wait_ge(u2_mm.sem, at(u2_mm, b))
                nc.scalar.activation(gateT[:, b, :], pU[:, :], ACT.Sigmoid, bias=u2_b[:, :]).then_inc(gate_done.sem, 1)
                act.wait_ge(beta_sum.sem, at(beta_sum, b))
                nc.scalar.activation(beta[:, b], bz[:, :, :], ACT.Sigmoid).then_inc(beta_done.sem, 1)

        @block.vector
        def _(dve):
            for s in (centred, r_var, normed, r_ms, scaled, conv, beta_sum):
                dve.sem_inc(s.sem, s.per)
            nc.vector.memset(hpad[:, 0:KCONV - 1], 0.0).then_inc(pad_zero, 1)
            dve.wait_ge(pad_zero, 1)
            dve.wait_ge(weights_in, 16 * len(loads))
            with dve.Fori(0, B) as b:
                dve.wait_ge(mean_mm.sem, at(mean_mm, b))
                dve.wait_ge(x_copied.sem, at(x_copied, b))
                nc.vector.tensor_tensor(xm[:, :], xc[:, :], pM[:, :], ALU.subtract).then_inc(centred.sem, 1)
                dve.wait_ge(sd_var.sem, at(sd_var, b))
                nc.vector.reciprocal(rs[:, :], sd[:, :]).then_inc(r_var.sem, 1)
                dve.wait_ge(r_var.sem, at(r_var, b))
                dve.wait_ge(kept.sem, before(kept, b))
                dve.wait_ge(u1_mm.sem, before(u1_mm, b))
                dve.wait_ge(centred.sem, at(centred, b))
                nc.vector.tensor_tensor(xn[:, :], xm[:, :], rs[:, :], ALU.mult).then_inc(normed.sem, 1)
                dve.wait_ge(sd_ms.sem, at(sd_ms, b))
                dve.wait_ge(normed.sem, at(normed, b))
                nc.vector.reciprocal(rs[:, :], sd[:, :]).then_inc(r_ms.sem, 1)
                dve.wait_ge(r_ms.sem, at(r_ms, b))
                dve.wait_ge(conv.sem, before(conv, b))
                nc.vector.scalar_tensor_tensor(out=hpad[:, KCONV - 1:], in0=xn[:, :], scalar=norm_w[:, 0:1],
                                               in1=rs[:, :], op0=ALU.mult, op1=ALU.mult).then_inc(scaled.sem, 1)
                dve.wait_ge(scaled.sem, at(scaled, b))
                dve.wait_ge(silu_h.sem, before(silu_h, b))
                nc.vector.tensor_scalar(cv[:, :], hpad[:, 0:T], conv_w[:, 0:1], conv_b[:, 0:1],
                                        ALU.mult, ALU.add).then_inc(conv.sem, 1)
                for k in range(1, KCONV):
                    dve.wait_ge(conv.sem, at(conv, b, k))
                    nc.vector.scalar_tensor_tensor(out=cv[:, :], in0=hpad[:, k:k + T], scalar=conv_w[:, k:k + 1],
                                                   in1=cv[:, :], op0=ALU.mult, op1=ALU.add).then_inc(conv.sem, 1)
                dve.wait_ge(beta_mm.sem, at(beta_mm, b))
                dve.wait_ge(beta_done.sem, before(beta_done, b))
                nc.vector.tensor_tensor(bz[:, :, :], pB[:, :].rearrange("p (c h) -> p c h", c=NC),
                                        view(beta_b, 0, [[0, NC], [1, H]]), ALU.add).then_inc(beta_sum.sem, 1)

        @block.gpsimd
        def _(pool):
            pool.sem_inc(kept.sem, 3)
            with pool.Fori(0, B) as b:
                pool.wait_ge(x_copied.sem, at(x_copied, b))
                nc.gpsimd.tensor_copy(xT[:, b, :], xc[:, :]).then_inc(kept.sem, 1)
                pool.wait_ge(normed.sem, at(normed, b))
                nc.gpsimd.tensor_copy(xnT[:, b, :], xn[:, :]).then_inc(kept.sem, 1)
                pool.wait_ge(silu_h.sem, at(silu_h, b))
                nc.gpsimd.tensor_copy(hT[:, b, :], hs[:, :]).then_inc(kept.sem, 1)


def stage_b(nc, io, keep):
    with ExitStack() as ctx:
        sb = lambda n, s: ctx.enter_context(nc.sbuf_tensor("b_" + n, s, F32))
        ps = lambda n, s: ctx.enter_context(nc.psum_tensor("b_" + n, s, F32))
        sig = lambda n, per=1: Signal(ctx, nc, "b_" + n, per)
        ident, hT, beta, acc = keep["ident"], keep["hT"], keep["beta"], keep["acc"]

        wqka = sb("wqka", [P, 3, HP, P]); wv = sb("wv", [P, HP, P]); wo = sb("wo", [P, HP, D])
        hn = sb("hn", [P, HP]); ab = sb("ab", [P, HP])
        wc = sb("wc", [P, 3, P]); abc = sb("abc", [P, 1]); woc = sb("woc", [P, D])
        masks = sb("masks", [P, LEVELS, NC * HALF]); ident4 = sb("ident4", [P, NC * C]); sel = sb("sel", [P, 2])
        sqb = sb("sqb", [P, 2, T]); qs = sb("qs", [P, T]); kr = sb("kr", [P, T]); al = sb("al", [P, T])
        ka = sb("ka", [P, T])
        kq = [sb(f"kq{i}", [P, 2, T]) for i in range(2)]
        tot = sb("tot", [P, T]); totc = [sb(f"totc{i}", [P, NC]) for i in range(2)]
        nrm = sb("nrm", [P, 2, NC, 2]); nre = sb("nre", [P, 2, NC, 2])
        rn = [sb(f"rn{i}", [P, 2, NC, 2]) for i in range(2)]
        bk = sb("bk", [P, NC, 2]); bk2 = sb("bk2", [P, NC, 2 * DK])
        bv = [sb(f"bv{i}", [P, NC, 2, DK]) for i in range(2)]
        em = sb("em", [P, 2 * LEVELS + 4, T])
        yz = [None] + [sb(f"yz{l}", [P, 2, NC * C]) for l in range(1, LEVELS)]
        tt = [sb(f"tt{i}", [P, 2, 2, NC * C]) for i in range(2)]
        mt = [sb(f"mt{i}", [P, 2, NC * C]) for i in range(2)]
        kh = [sb(f"kh{i}", [P, NC, P]) for i in range(2)]
        st = sb("st", [P, 2 * DK]); xsb = sb("xsb", [P, 2, DK]); us = sb("us", [P, 2, DK])
        yt = sb("yt", [P, NC, 2, DK]); ysq = sb("ysq", [P, NC, 2, DK]); yss = sb("yss", [P, NC * 2])
        ysd = sb("ysd", [P, NC * 2]); yr = sb("yr", [P, NC * 2]); yn = sb("yn", [P, NC, 2 * DK])
        yT = sb("yT", [P, T])

        pj = ps("pj", [P, 512]); lv = ps("lv", [P, 2, 512]); wk = ps("wk", [P, 3, 512])
        cx = ps("cx", [P, 512]); cu = ps("cu", [P, 512])

        weights_in = ctx.enter_context(nc.semaphore("b_weights_in"))
        scaled_wo = ctx.enter_context(nc.semaphore("b_scaled_wo"))
        loads = [(wqka[:, 0], io["q_w"].rearrange("d (h n) -> d h n", h=HP)),
                 (wqka[:, 1], io["k_w"].rearrange("d (h n) -> d h n", h=HP)),
                 (wqka[:, 2], io["alpha_w"].rearrange("d (h n) -> d h n", h=HP)),
                 (wv[:, :, :], io["v_w"].rearrange("d (h n) -> d h n", h=HP)),
                 (wo[:, :, :], io["out_w"].rearrange("(h p) d -> p h d", p=P)),
                 (hn[:, :], io["head_norm_w"].rearrange("(a b) d -> (b d) a", b=2)),
                 (ab[:, :], io["alpha_b"].rearrange("(h p) -> p h", p=P)),
                 (masks[:, :, :], io["masks"]),
                 (sel[:, :], io["sel"])]
        with nc.Block() as block:
            @block.sync
            def _(sp):
                with nc.allow_non_contiguous_dma(reason="small per-channel vectors"):
                    for dst, src in loads:
                        sp.dma_start(dst, src).then_inc(weights_in, 16)

            @block.vector
            def _(dve):
                for t in [em, *tt, *mt]:
                    nc.vector.memset(t[:], 0.0)
                for c in range(NC):
                    nc.vector.tensor_copy(ident4[:, c * C:(c + 1) * C], ident[:, :])
                dve.wait_ge(weights_in, 16 * len(loads))
                nc.vector.tensor_tensor(wo[:, :, :], wo[:, :, :], view(hn, 0, [[1, HP], [0, D]]),
                                        ALU.mult).then_inc(scaled_wo, 1)

            @block.gpsimd
            def _(pool):
                for t in [*yz[1:], *kq, *bv, *kh, *rn, *totc, woc, acc, st]:
                    nc.gpsimd.memset(t[:], 0.0)

        def z_step(l, h, transposed=1):
            return 4 * (l - 1) + (2 * h + transposed + 1 if l < LEVELS - 1 else h + 1)

        q_mm, k_mm, a_mm, v_mm, ssq_mm, bb_mm = (sig(n) for n in ("q_mm", "k_mm", "a_mm", "v_mm", "ssq_mm", "bb_mm"))
        diag_mm, lvl_mm, tr_mm = sig("diag_mm", 2), sig("lvl_mm", 2 * LEVELS), sig("tr_mm", 2)
        y_mm, z_mm = sig("y_mm", 2 * (LEVELS - 1)), sig("z_mm", z_step(LEVELS - 1, 1))
        kh_mm, x_mm, u_mm, o_mm, su_mm = sig("kh_mm"), sig("x_mm", NC - 1), sig("u_mm", NC), sig("o_mm", NC), sig("su_mm", NC - 1)
        yT_mm, out_mm = sig("yT_mm"), sig("out_mm")
        pe_signals = (q_mm, k_mm, a_mm, v_mm, ssq_mm, bb_mm, diag_mm, lvl_mm, tr_mm, y_mm, z_mm, kh_mm, x_mm, u_mm,
                      o_mm, su_mm, yT_mm, out_mm)
        q_read, k_read, alpha_done, norm_sqrt = sig("q_read", 2), sig("k_read", 2), sig("alpha_done"), sig("norm_sqrt")
        u_copy, y_copy, kh_copy, rms_sqrt, yT_copy = (sig("u_copy", NC), sig("y_copy", 2 * (LEVELS - 1)), sig("kh_copy"),
                                                      sig("rms_sqrt"), sig("yT_copy"))
        act_signals = (q_read, k_read, alpha_done, norm_sqrt, u_copy, y_copy, kh_copy, rms_sqrt, yT_copy)
        norm_steps, bv_done, kab_done, kq_start = sig("norm_steps", 4), sig("bv_done"), sig("kab_done"), sig("kq_start", 2)
        diag_done, lvl_done, kq_up = sig("diag_done", 2), sig("lvl_done", 2 * LEVELS), sig("kq_up", LEVELS)
        t_start, t_up, x_done, o_done, s_done = (sig("t_start", 2), sig("t_up", z_step(LEVELS - 1, 1)), sig("x_done", NC - 1),
                                                 sig("o_done", NC), sig("s_done", 2 * (NC - 1)))
        y_sum, y_recip, acc_done = sig("y_sum"), sig("y_recip"), sig("acc_done")
        dve_signals = (norm_steps, bv_done, kab_done, kq_start, diag_done, lvl_done, kq_up, t_start, t_up, x_done,
                       o_done, s_done, y_sum, y_recip, acc_done)
        kr_up, tot_up, tT_start, mt_up, y_sq, y_norm = (sig("kr_up", LEVELS), sig("tot_up", LEVELS), sig("tT_start", 2),
                                                       sig("mt_up", 2 * LEVELS), sig("y_sq"), sig("y_norm"))
        pool_signals = (kr_up, tot_up, tT_start, mt_up, y_sq, y_norm)
        wc_ready = ctx.enter_context(nc.semaphore("b_wc_ready"))
        woc_ready = ctx.enter_context(nc.semaphore("b_woc_ready"))

        def tile(c):
            return slice(c * C, (c + 1) * C)

        def m_slot(l, h):
            return 2 * LEVELS + 2 * (l % 2) + h

        def rows(h):
            return slice(h * DK, (h + 1) * DK)

        def zt_bank(l, h):
            return h if l == LEVELS - 1 else 2 * h

        tot_at = [None] + [T - (T >> (l - 1)) for l in range(1, LEVELS)]

        def block_products(l, par, second, outer, n_rep):
            t, off = (al, 0) if l == 0 else (tot, tot_at[l])
            dims = [[2, T >> (l + 1)]] + ([[0, n_rep]] if n_rep > 1 else [])
            return view(t, off + (1 if second else 0), ([[0, outer]] if outer else []) + dims)

        block = ctx.enter_context(nc.Block())

        @block.tensor
        def _(pe):
            for s in pe_signals:
                pe.sem_inc(s.sem, s.per)

            def chain_x(hp, b, c):
                p = 1 - b % 2
                pe.wait_ge(s_done.sem, s_done.at(hp, b, 2 * c))
                pe.wait_ge(o_done.sem, o_done.at(hp, b, c))
                if c == 1:
                    pe.wait_ge(kq_up.sem, kq_up.at(hp, b - 1))
                nc.tensor.matmul(cx[:, 0:P], kq[p][:, 0, tile(c)], st[:, :], start=True, stop=True).then_inc(x_mm.sem, 1)

            def chain_u(hp, b, c):
                p = 1 - b % 2
                if c == 0:
                    pe.wait_ge(t_up.sem, t_up.at(hp, b - 1))
                    pe.wait_ge(bv_done.sem, bv_done.at(hp, b - 1))
                else:
                    pe.wait_ge(x_done.sem, x_done.at(hp, b, c))
                for h in range(2):
                    rhs = bv[p][:, 0, h, :] if c == 0 else xsb[:, h, :]
                    mm = nc.tensor.matmul(cu[:, h * DK:(h + 1) * DK], tt[p][:, h, 1, tile(c)], rhs,
                                          start=True, stop=True)
                mm.then_inc(u_mm.sem, 1)

            def chain_o(hp, b, c):
                p = 1 - b % 2
                pe.wait_ge(u_copy.sem, u_copy.at(hp, b, c + 1))
                if c == 0:
                    pe.wait_ge(mt_up.sem, mt_up.at(hp, b - 1))
                    pe.wait_ge(kh_copy.sem, kh_copy.at(hp, b - 1))
                    pe.wait_ge(o_done.sem, o_done.at(hp, b - 1))
                if c > 0:
                    nc.tensor.matmul(cx[:, P:2 * P], kq[p][:, 1, tile(c)], st[:, :], start=True, stop=False)
                if c < NC - 1:
                    nc.tensor.matmul(cu[:, P:2 * P], kh[p][:, c, :], us[:, :, :], start=True,
                                     stop=True).then_inc(su_mm.sem, 1)
                for h in range(2):
                    mm = nc.tensor.matmul(cx[:, P + h * DK:P + (h + 1) * DK], mt[p][:, h, tile(c)], us[:, h, :],
                                          start=(c == 0), stop=(c == 0 or h == 1))
                mm.then_inc(o_mm.sem, 1)

            def level(hp, b, l):
                n, q = 1 << l, kq[b % 2]
                if l == 0:
                    pe.wait_ge(kq_start.sem, kq_start.at(hp, b))
                else:
                    pe.wait_ge(kq_up.sem, kq_up.at(hp, b, l))
                    pe.wait_ge(kr_up.sem, kr_up.at(hp, b, l))
                for h in range(2):
                    if l == 0:
                        pe.wait_ge(diag_done.sem, diag_done.at(hp, b, h + 1))
                    else:
                        pe.wait_ge(lvl_done.sem, lvl_done.at(hp, b, 2 * (l - 1) + h + 1))
                    for c in range(NC):
                        mm = nc.tensor.matmul(
                            view(lv, h * 512 + c * HALF, [[NC * HALF, 2], [1, HALF]]), kr[rows(h), tile(c)],
                            halves(q, c * C, n, True, C, [T, 2], DK, h * DK), start=True, stop=True)
                    mm.then_inc(lvl_mm.sem, 1)

            def times_t(hp, b, l):
                t = tt[b % 2]
                for h in range(2):
                    pe.wait_ge(lvl_done.sem, lvl_done.at(hp, b, 2 * l + h + 1))
                    if l == 1:
                        pe.wait_ge(t_start.sem, t_start.at(hp, b, h + 1))
                        pe.wait_ge(tT_start.sem, tT_start.at(hp, b, h + 1))
                    else:
                        pe.wait_ge(t_up.sem, t_up.at(hp, b, z_step(l - 1, h, 1 - h)))
                    for c in range(NC):
                        mm = nc.tensor.matmul(wk[:, h, tile(c)], em[:, 2 * l + h, tile(c)], t[:, h, 0, tile(c)],
                                              start=True, stop=True)
                    mm.then_inc(y_mm.sem, 1)

            def t_times(hp, b, l):
                t = tt[b % 2]
                for h in range(2):
                    pe.wait_ge(y_copy.sem, y_copy.at(hp, b, 2 * (l - 1) + h + 1))
                    if l > 1 and h == (0 if l < LEVELS - 1 else 1):
                        pe.wait_ge(t_up.sem, t_up.at(hp, b, z_step(l - 1, 1)))
                    if l < LEVELS - 1:
                        for c in range(NC):
                            mm = nc.tensor.matmul(wk[:, 2 - h, tile(c)], t[:, h, 1, tile(c)], yz[l][:, h, tile(c)],
                                                  start=True, stop=True)
                        mm.then_inc(z_mm.sem, 1)
                        if h == 1:
                            pe.wait_ge(t_up.sem, t_up.at(hp, b, z_step(l, 0, 0)))
                    for c in range(NC):
                        mm = nc.tensor.matmul(wk[:, zt_bank(l, h), tile(c)], yz[l][:, h, tile(c)], t[:, h, 1, tile(c)],
                                              start=True, stop=True)
                    mm.then_inc(z_mm.sem, 1)

            def step(hp, b):
                hb = hT[:, b, :]
                if b == 0:
                    pe.wait_ge(wc_ready, hp * 2 + 2)
                pe.wait_ge(kh_copy.sem, kh_copy.at(hp, b - 1))
                nc.tensor.matmul(pj[:, :], wc[:, 0, :], hb, start=True, stop=True).then_inc(q_mm.sem, 1)
                pe.wait_ge(lvl_done.sem, lvl_done.at(hp, b - 1))
                nc.tensor.matmul(lv[:, 0, :], wc[:, 1, :], hb, start=True, stop=True).then_inc(k_mm.sem, 1)
                nc.tensor.matmul(lv[:, 1, :], wc[:, 2, :], hb, start=True, stop=True).then_inc(a_mm.sem, 1)
                chain_u(hp, b, 0)
                pe.wait_ge(q_read.sem, q_read.at(hp, b))
                for c in range(NC):
                    mm = nc.tensor.matmul(pj[:, tile(c)], hT[:, b, tile(c)], wv[:, hp, :], start=True, stop=True)
                mm.then_inc(v_mm.sem, 1)
                chain_o(hp, b, 0)
                pe.wait_ge(k_read.sem, k_read.at(hp, b))
                for i in range(2):
                    for c in range(NC):
                        mm = nc.tensor.matmul(lv[:, 0, (i * NC + c) * 2:(i * NC + c) * 2 + 2], sqb[:, i, tile(c)],
                                              sel[:, :], start=True, stop=True)
                mm.then_inc(ssq_mm.sem, 1)
                chain_x(hp, b, 1)
                pe.wait_ge(norm_steps.sem, norm_steps.at(hp, b))
                pe.wait_ge(alpha_done.sem, alpha_done.at(hp, b))
                for c in range(NC):
                    mm = nc.tensor.matmul(lv[:, 1, tile(c)], bk2[:, c, :], ident[:, :],
                                          start=True, stop=True)
                mm.then_inc(bb_mm.sem, 1)
                chain_u(hp, b, 1)
                chain_o(hp, b, 1)
                for h in range(2):
                    if h == 0:
                        pe.wait_ge(norm_sqrt.sem, norm_sqrt.at(hp, b))
                    else:
                        pe.wait_ge(kab_done.sem, kab_done.at(hp, b))
                    for c in range(NC):
                        mm = nc.tensor.matmul(lv[:, h, tile(c)], kr[rows(h), tile(c)], qs[rows(h), tile(c)],
                                              start=True, stop=True)
                    mm.then_inc(diag_mm.sem, 1)
                chain_x(hp, b, 2)
                level(hp, b, 0)
                chain_u(hp, b, 2)
                for h in range(2):
                    pe.wait_ge(lvl_done.sem, lvl_done.at(hp, b, h + 1))
                    for c in range(NC):
                        mm = nc.tensor.transpose(wk[:, h, tile(c)], em[:, h, tile(c)], ident[:, :])
                    mm.then_inc(tr_mm.sem, 1)
                chain_o(hp, b, 2)
                level(hp, b, 1)
                chain_x(hp, b, 3)
                times_t(hp, b, 1)
                chain_u(hp, b, 3)
                level(hp, b, 2)
                t_times(hp, b, 1)
                chain_o(hp, b, 3)
                for l in range(2, LEVELS - 1):
                    times_t(hp, b, l)
                    level(hp, b, l + 1)
                    t_times(hp, b, l)
                    if l == 4:
                        pe.wait_ge(y_norm.sem, y_norm.at(hp, b))
                        pe.wait_ge(bv_done.sem, bv_done.at(hp, b))
                        for c in range(NC):
                            mm = nc.tensor.transpose(pj[:, tile(c)], yn[:, c, :], ident[:, :])
                        mm.then_inc(yT_mm.sem, 1)
                    if l == 5:
                        project(hp, b)
                times_t(hp, b, LEVELS - 1)
                pe.wait_ge(kr_up.sem, kr_up.at(hp, b))
                pe.wait_ge(acc_done.sem, acc_done.at(hp, b))
                for c in range(NC):
                    mm = nc.tensor.transpose(pj[:, tile(c)], kr[:, tile(c)], ident[:, :])
                mm.then_inc(kh_mm.sem, 1)
                t_times(hp, b, LEVELS - 1)

            def project(hp, b):
                pe.wait_ge(yT_copy.sem, yT_copy.at(hp, b))
                if b <= 1:
                    pe.wait_ge(woc_ready, hp + 1 + b)
                nc.tensor.matmul(pj[:, :], woc[:, :], yT[:, :], start=True, stop=True).then_inc(out_mm.sem, 1)

            with pe.Fori(0, HP) as hp:
                for b in range(B):
                    step(hp, b)
            hp, b = HP, 0
            chain_u(hp, b, 0)
            chain_o(hp, b, 0)
            for c in range(1, NC):
                chain_x(hp, b, c)
                chain_u(hp, b, c)
                chain_o(hp, b, c)
            pe.wait_ge(y_norm.sem, y_norm.at(hp, b))
            for c in range(NC):
                mm = nc.tensor.transpose(pj[:, tile(c)], yn[:, c, :], ident[:, :])
            mm.then_inc(yT_mm.sem, 1)
            project(hp, b)

        @block.scalar
        def _(act):
            for s in act_signals:
                act.sem_inc(s.sem, s.per)

            def copy_u(hp, b, c):
                act.wait_ge(u_mm.sem, u_mm.at(hp, b, c + 1))
                act.wait_ge(o_mm.sem, o_mm.at(hp, b, c))
                nc.scalar.activation(us[:, :, :], cu[:, 0:P].rearrange("p (h d) -> p h d", h=2),
                                     ACT.Copy).then_inc(u_copy.sem, 1)

            def copy_y(hp, b, l):
                n = 1 << l
                for h in range(2):
                    act.wait_ge(y_mm.sem, y_mm.at(hp, b, 2 * (l - 1) + h + 1))
                    nc.scalar.activation(halves(yz[l], h * T, n, False, T),
                                         halves(wk, h * 512, n, False, T),
                                         ACT.Copy).then_inc(y_copy.sem, 1)

            def rms(hp, b):
                act.wait_ge(y_sum.sem, y_sum.at(hp, b))
                nc.scalar.activation(ysd[:, :], yss[:, :], ACT.Sqrt, bias=keep["rms_eps"][:, :],
                                     scale=1.0 / DK).then_inc(rms_sqrt.sem, 1)

            def copy_yT(hp, b):
                act.wait_ge(yT_mm.sem, yT_mm.at(hp, b))
                act.wait_ge(out_mm.sem, out_mm.at(hp, b - 1))
                nc.scalar.activation(yT[:, :], pj[:, :], ACT.Copy).then_inc(yT_copy.sem, 1)

            def step(hp, b):
                act.wait_ge(q_mm.sem, q_mm.at(hp, b))
                act.wait_ge(ssq_mm.sem, ssq_mm.at(hp, b - 1))
                nc.scalar.activation(sqb[:, 0, :], pj[:, :], ACT.Square).then_inc(q_read.sem, 1)
                act.wait_ge(kq_start.sem, kq_start.at(hp, b - 1))
                act.wait_ge(diag_mm.sem, diag_mm.at(hp, b - 1))
                nc.scalar.activation(qs[:, :], pj[:, :], ACT.Copy).then_inc(q_read.sem, 1)
                act.wait_ge(k_mm.sem, k_mm.at(hp, b))
                nc.scalar.activation(sqb[:, 1, :], lv[:, 0, :], ACT.Square).then_inc(k_read.sem, 1)
                act.wait_ge(kh_mm.sem, kh_mm.at(hp, b - 1))
                nc.scalar.activation(kr[:, :], lv[:, 0, :], ACT.Copy).then_inc(k_read.sem, 1)
                copy_u(hp, b, 0)
                act.wait_ge(a_mm.sem, a_mm.at(hp, b))
                act.wait_ge(kq_up.sem, kq_up.at(hp, b - 1))
                act.wait_ge(tot_up.sem, tot_up.at(hp, b - 1))
                nc.scalar.activation(al[:, :], lv[:, 1, :], ACT.Sigmoid, bias=abc[:, :]).then_inc(alpha_done.sem, 1)
                act.wait_ge(ssq_mm.sem, ssq_mm.at(hp, b))
                act.wait_ge(norm_steps.sem, norm_steps.at(hp, b - 1))
                nc.scalar.activation(nrm[:, :, :, :].rearrange("p i c h -> p (i c h)"), lv[:, 0, 0:4 * NC],
                                     ACT.Sqrt).then_inc(norm_sqrt.sem, 1)
                copy_u(hp, b, 1)
                copy_u(hp, b, 2)
                copy_y(hp, b, 1)
                copy_u(hp, b, 3)
                copy_y(hp, b, 2)
                rms(hp, b)
                copy_y(hp, b, 3)
                copy_y(hp, b, 4)
                copy_yT(hp, b)
                copy_y(hp, b, 5)
                copy_y(hp, b, 6)
                act.wait_ge(kh_mm.sem, kh_mm.at(hp, b))
                nc.scalar.activation(kh[b % 2][:, :, :], pj[:, :].rearrange("p (c d) -> p c d", c=NC),
                                     ACT.Copy).then_inc(kh_copy.sem, 1)

            with act.Fori(0, HP) as hp:
                for b in range(B):
                    step(hp, b)
            for c in range(NC):
                copy_u(HP, 0, c)
            rms(HP, 0)
            copy_yT(HP, 0)

        @block.vector
        def _(dve):
            for s in dve_signals:
                dve.sem_inc(s.sem, s.per)

            def take_o(hp, b, c):
                p = 1 - b % 2
                dve.wait_ge(o_mm.sem, o_mm.at(hp, b, c + 1))
                if c == 0:
                    dve.wait_ge(y_norm.sem, y_norm.at(hp, b - 1))
                nc.vector.tensor_tensor(yt[:, c], cx[:, P:2 * P].rearrange("p (h d) -> p h d", h=2),
                                        view(rn[p], c * 2, [[1, 2], [0, DK]]), ALU.mult).then_inc(o_done.sem, 1)

            def take_s(hp, b, c):
                p = 1 - b % 2
                dve.wait_ge(su_mm.sem, su_mm.at(hp, b, c + 1))
                if c == 0:
                    dve.wait_ge(o_mm.sem, o_mm.at(hp, b - 1))
                    dve.wait_ge(tot_up.sem, tot_up.at(hp, b - 1))
                for h in range(2):
                    add = cu[rows(h), P + h * DK:P + (h + 1) * DK]
                    if c == 0:
                        nc.vector.tensor_copy(st[rows(h), rows(h)], add).then_inc(s_done.sem, 1)
                    else:
                        nc.vector.scalar_tensor_tensor(out=st[rows(h), rows(h)], in0=st[rows(h), rows(h)],
                                                       scalar=totc[p][rows(h), c:c + 1], in1=add,
                                                       op0=ALU.mult, op1=ALU.add).then_inc(s_done.sem, 1)

            def take_x(hp, b, c):
                p = 1 - b % 2
                dve.wait_ge(x_mm.sem, x_mm.at(hp, b, c))
                dve.wait_ge(u_mm.sem, u_mm.at(hp, b, c))
                nc.vector.tensor_tensor(xsb[:, :, :], bv[p][:, c], cx[:, 0:P].rearrange("p (h d) -> p h d", h=2), ALU.subtract).then_inc(x_done.sem, 1)

            def take_level(hp, b, l):
                n = 1 << l
                mask = view(masks, l * NC * HALF, [[0, 2], [n, T // 2 // n], [1, n]])
                for h in range(2):
                    dve.wait_ge(lvl_mm.sem, lvl_mm.at(hp, b, 2 * l + h + 1))
                    if h == 0:
                        if l == 0:
                            dve.wait_ge(tr_mm.sem, tr_mm.at(hp, b - 1))
                            dve.wait_ge(tT_start.sem, tT_start.at(hp, b - 1))
                        else:
                            dve.wait_ge(y_mm.sem, y_mm.at(hp, b - 1, 2 * l))
                        if l < 2:
                            dve.wait_ge(mt_up.sem, mt_up.at(hp, b - 1))
                        else:
                            dve.wait_ge(mt_up.sem, mt_up.at(hp, b, 2 * l - 2))
                    nc.vector.tensor_tensor(
                        halves(em, (2 * l + h) * T, n, True, T, [(m_slot(l, h) - 2 * l - h) * T, 2]),
                        view(lv, h * 512, [[NC * HALF, 2], [n, T // 2 // n], [1, n]]), mask,
                        ALU.mult).then_inc(lvl_done.sem, 1)

            def grow_kq(hp, b, l):
                n, q = 1 << l, kq[b % 2]
                dve.wait_ge(lvl_mm.sem, lvl_mm.at(hp, b, 2 * l + 2))
                if l == 0:
                    dve.wait_ge(kq_start.sem, kq_start.at(hp, b))
                else:
                    dve.wait_ge(kq_up.sem, kq_up.at(hp, b, l))
                    dve.wait_ge(tot_up.sem, tot_up.at(hp, b, l))
                v = halves(q, 0, n, True, T, [T, 2])
                nc.vector.tensor_tensor(v, v, block_products(l, b % 2, False, 2, n), ALU.mult).then_inc(kq_up.sem, 1)

            def take_t(hp, b, l):
                n, t = 1 << l, tt[b % 2]
                for h in range(2):
                    for transposed in range(0 if l < LEVELS - 1 else 1, 2):
                        dve.wait_ge(z_mm.sem, z_mm.at(hp, b, z_step(l, h, transposed)))
                        bank = zt_bank(l, h) if transposed else 2 - h
                        v = halves(t, (h * 2 + transposed) * T, n, bool(transposed), T)
                        z = halves(wk, bank * 512, n, bool(transposed), T)
                        nc.vector.tensor_tensor(v, v, z, ALU.subtract).then_inc(t_up.sem, 1)

            def sum_y(hp, b):
                dve.wait_ge(y_sq.sem, y_sq.at(hp, b))
                dve.wait_ge(rms_sqrt.sem, rms_sqrt.at(hp, b - 1))
                nc.vector.tensor_reduce(yss[:, :], ysq[:, :, :, :].rearrange("p c h d -> p (c h) d"), AX.X,
                                        ALU.add).then_inc(y_sum.sem, 1)

            def invert_y(hp, b):
                dve.wait_ge(rms_sqrt.sem, rms_sqrt.at(hp, b))
                dve.wait_ge(y_norm.sem, y_norm.at(hp, b - 1))
                nc.vector.reciprocal(yr[:, :], ysd[:, :]).then_inc(y_recip.sem, 1)

            def add_out(hp, b):
                dve.wait_ge(out_mm.sem, out_mm.at(hp, b))
                a = acc[:, (b - 1) % B, :]
                nc.vector.tensor_tensor(a, a, pj[:, :], ALU.add).then_inc(acc_done.sem, 1)

            def step(hp, b):
                q = kq[b % 2]
                take_s(hp, b, 0)
                take_o(hp, b, 0)
                take_x(hp, b, 1)
                r = rn[b % 2]
                dve.wait_ge(norm_sqrt.sem, norm_sqrt.at(hp, b))
                nc.vector.tensor_scalar(nre[:], nrm[:], RMS_EPS, None, ALU.add).then_inc(norm_steps.sem, 1)
                dve.wait_ge(norm_steps.sem, norm_steps.at(hp, b, 1))
                nc.vector.reciprocal(r[:], nre[:]).then_inc(norm_steps.sem, 1)
                dve.wait_ge(norm_steps.sem, norm_steps.at(hp, b, 2))
                nc.vector.tensor_tensor(bk[:, :, :], beta[:, b, :, bass.ds(hp * 2, 2)], r[:, 1], ALU.mult).then_inc(norm_steps.sem, 1)
                dve.wait_ge(norm_steps.sem, norm_steps.at(hp, b, 3))
                dve.wait_ge(bb_mm.sem, bb_mm.at(hp, b - 1))
                nc.vector.tensor_tensor(
                    bk2[:, :, :].rearrange("p c (h d) -> p (c h) d", h=2), view(bk, 0, [[1, 2 * NC], [0, DK]]),
                    view(r, 2 * NC, [[1, 2 * NC], [0, DK]]), ALU.mult).then_inc(norm_steps.sem, 1)
                dve.wait_ge(v_mm.sem, v_mm.at(hp, b))
                nc.vector.tensor_tensor(
                    bv[b % 2][:, :, :, :].rearrange("p c h d -> p (c h) d"),
                    pj[:, :].rearrange("p (c d) -> p c d", d=DK), view(bk, 0, [[1, 2 * NC], [0, DK]]),
                    ALU.mult).then_inc(bv_done.sem, 1)
                dve.wait_ge(bb_mm.sem, bb_mm.at(hp, b))
                dve.wait_ge(alpha_done.sem, alpha_done.at(hp, b))
                nc.vector.tensor_tensor(ka[:, :], lv[:, 1, :], al[:, :], ALU.mult).then_inc(kab_done.sem, 1)
                dve.wait_ge(kab_done.sem, kab_done.at(hp, b))
                dve.wait_ge(k_read.sem, k_read.at(hp, b))
                nc.vector.tensor_tensor(q[:, 0, :], ka[:, :], kr[:, :], ALU.mult).then_inc(kq_start.sem, 1)
                dve.wait_ge(q_read.sem, q_read.at(hp, b))
                nc.vector.tensor_tensor(q[:, 1, :], qs[:, :], al[:, :], ALU.mult).then_inc(kq_start.sem, 1)
                take_s(hp, b, 1)
                take_o(hp, b, 1)
                for h in range(2):
                    dve.wait_ge(diag_mm.sem, diag_mm.at(hp, b, h + 1))
                    nc.vector.tensor_tensor(mt[b % 2][:, h, :], lv[:, h, :], ident4[:, :],
                                            ALU.mult).then_inc(diag_done.sem, 1)
                take_x(hp, b, 2)
                take_level(hp, b, 0)
                grow_kq(hp, b, 0)
                for h in range(2):
                    dve.wait_ge(tr_mm.sem, tr_mm.at(hp, b, h + 1))
                    nc.vector.tensor_tensor(tt[b % 2][:, h, 0, :], ident4[:, :], wk[:, h, :],
                                            ALU.subtract).then_inc(t_start.sem, 1)
                take_s(hp, b, 2)
                take_o(hp, b, 2)
                take_level(hp, b, 1)
                grow_kq(hp, b, 1)
                take_x(hp, b, 3)
                take_level(hp, b, 2)
                grow_kq(hp, b, 2)
                take_t(hp, b, 1)
                take_o(hp, b, 3)
                for l in range(2, LEVELS - 1):
                    take_level(hp, b, l + 1)
                    grow_kq(hp, b, l + 1)
                    if l == 3:
                        invert_y(hp, b)
                    take_t(hp, b, l)
                    if l == 2:
                        sum_y(hp, b)
                    if l == 5:
                        add_out(hp, b)
                take_t(hp, b, LEVELS - 1)

            with dve.Fori(0, HP) as hp:
                for b in range(B):
                    step(hp, b)
            for c in range(NC):
                if c > 0:
                    take_x(HP, 0, c)
                if c < NC - 1:
                    take_s(HP, 0, c)
                take_o(HP, 0, c)
            sum_y(HP, 0)
            invert_y(HP, 0)
            add_out(HP, 0)

        @block.gpsimd
        def _(pool):
            for s in pool_signals:
                pool.sem_inc(s.sem, s.per)
            pool.sem_inc(woc_ready, 1)

            def add_m(hp, b, l):
                n, m = 1 << l, mt[b % 2]
                for h in range(2):
                    pool.wait_ge(lvl_done.sem, lvl_done.at(hp, b, 2 * l + h + 1))
                    if l > 0:
                        pool.wait_ge(mt_up.sem, mt_up.at(hp, b, 2 * (l - 1) + h + 1))
                    v = halves(m, h * T, n, True, T)
                    nc.gpsimd.tensor_tensor(v, v, halves(em, m_slot(l, h) * T, n, True, T),
                                            ALU.add).then_inc(mt_up.sem, 1)

            def grow_kr(hp, b, l):
                n = 1 << l
                pool.wait_ge(lvl_mm.sem, lvl_mm.at(hp, b, 2 * l + 2))
                if l == 0:
                    pool.wait_ge(alpha_done.sem, alpha_done.at(hp, b))
                    pool.wait_ge(kq_start.sem, kq_start.at(hp, b))
                else:
                    pool.wait_ge(kr_up.sem, kr_up.at(hp, b, l))
                    pool.wait_ge(tot_up.sem, tot_up.at(hp, b, l))
                v = halves(kr, 0, n, False, T)
                nc.gpsimd.tensor_tensor(v, v, block_products(l, b % 2, True, None, n), ALU.mult).then_inc(kr_up.sem, 1)
                if l > 0:
                    pass
                out = view(tot, tot_at[l + 1], [[1, T >> (l + 1)]]) if l < LEVELS - 1 else totc[b % 2][:, :]
                pool.wait_ge(kq_up.sem, kq_up.at(hp, b - 1))
                nc.gpsimd.tensor_tensor(out, block_products(l, b % 2, False, None, 1),
                                        block_products(l, b % 2, True, None, 1), ALU.mult).then_inc(tot_up.sem, 1)

            def square_y(hp, b):
                pool.wait_ge(o_done.sem, o_done.at(hp, b))
                pool.wait_ge(y_sum.sem, y_sum.at(hp, b - 1))
                nc.gpsimd.tensor_tensor(ysq[:], yt[:], yt[:], ALU.mult).then_inc(y_sq.sem, 1)

            def norm_y(hp, b):
                pool.wait_ge(y_recip.sem, y_recip.at(hp, b))
                pool.wait_ge(yT_mm.sem, yT_mm.at(hp, b - 1))
                nc.gpsimd.tensor_tensor(yn[:, :, :].rearrange("p c (h d) -> p (c h) d", h=2),
                                        yt[:, :, :, :].rearrange("p c h d -> p (c h) d"),
                                        view(yr, 0, [[1, 2 * NC], [0, DK]]), ALU.mult).then_inc(y_norm.sem, 1)

            def step(hp, b):
                if b == 0:
                    pool.wait_ge(a_mm.sem, a_mm.at(hp, b - 1))
                    pool.wait_ge(alpha_done.sem, alpha_done.at(hp, b - 1))
                    nc.gpsimd.tensor_copy(wc[:, :, :], wqka[:, :, hp, :]).then_inc(wc_ready, 1)
                    nc.gpsimd.tensor_copy(abc[:, :], ab[:, bass.ds(hp, 1)]).then_inc(wc_ready, 1)
                grow_kr(hp, b, 0)
                for h in range(2):
                    pool.wait_ge(lvl_done.sem, lvl_done.at(hp, b, h + 1))
                    nc.gpsimd.tensor_tensor(tt[b % 2][:, h, 1, :], ident4[:, :], em[:, h, :],
                                            ALU.subtract).then_inc(tT_start.sem, 1)
                add_m(hp, b, 0)
                grow_kr(hp, b, 1)
                add_m(hp, b, 1)
                grow_kr(hp, b, 2)
                add_m(hp, b, 2)
                square_y(hp, b)
                grow_kr(hp, b, 3)
                add_m(hp, b, 3)
                grow_kr(hp, b, 4)
                add_m(hp, b, 4)
                norm_y(hp, b)
                grow_kr(hp, b, 5)
                add_m(hp, b, 5)
                grow_kr(hp, b, 6)
                add_m(hp, b, 6)
                if b == 0:
                    pool.wait_ge(out_mm.sem, out_mm.at(hp, b))
                    nc.gpsimd.tensor_copy(woc[:, :], wo[:, hp, :]).then_inc(woc_ready, 1)

            with pool.Fori(0, HP) as hp:
                for b in range(B):
                    step(hp, b)
            square_y(HP, 0)
            norm_y(HP, 0)


def loop_at(s, b, k=None):
    return b * s.per + (s.per + (s.per if k is None else k))


def stage_c(nc, io, keep):
    with ExitStack() as ctx:
        sb = lambda n, s: ctx.enter_context(nc.sbuf_tensor("c_" + n, s, F32))
        ps = lambda n, s: ctx.enter_context(nc.psum_tensor("c_" + n, s, F32))
        sig = lambda n, per=1: Signal(ctx, nc, "c_" + n, per)
        at = loop_at
        xT, xnT, gateT, acc, mean_w = (keep[k] for k in ("xT", "xnT", "gateT", "acc", "mean_w"))
        NF = 512 // P
        ffn_w = sb("ffn_w", [P, 1]); w1 = sb("w1", [P, NF, P]); w3 = sb("w3", [P, NF, P]); w2 = sb("w2", [P, NF, D])
        tg = sb("tg", [P, T]); y1 = sb("y1", [P, T]); sq = sb("sq", [P, T]); sd = sb("sd", [P, T]); rs = sb("rs", [P, T])
        y2 = sb("y2", [P, T]); sl = sb("sl", [P, 2, T]); g = sb("g", [P, 2, T]); y3 = sb("y3", [P, T])
        x2 = sb("x2", [P, T]); xm = sb("xm", [P, T])
        pM = ps("pM", [P, T]); p1 = ps("p1", [P, 2, T]); p3 = ps("p3", [P, 2, T]); pO = ps("pO", [P, T]); pV = ps("pV", [P, T])
        weights_in = ctx.enter_context(nc.semaphore("c_weights_in"))
        ms_mm, w1_mm, w3_mm, w2_mm, mean_mm, var_mm = (
            sig("ms_mm"), sig("w1_mm", NF), sig("w3_mm", NF), sig("w2_mm", NF), sig("mean_mm"), sig("var_mm"))
        sq_ms, sd_ms, silu_done, sq_var, sd_var = sig("sq_ms"), sig("sd_ms"), sig("silu_done", NF), sig("sq_var"), sig("sd_var")
        y_sum, r_ms, y_norm, g_done, y_ff, x_sum, centred, r_var, x_norm = (
            sig("y_sum"), sig("r_ms"), sig("y_norm"), sig("g_done", NF), sig("y_ff"), sig("x_sum"), sig("centred"),
            sig("r_var"), sig("x_norm"))
        gated, kept = sig("gated"), sig("kept")
        loads = [(ffn_w[:, :], io["ff_norm_w"].rearrange("(p o) -> p o", o=1)),
                 (w1[:, :, :], io["ff_w1"].rearrange("d (m n) -> d m n", n=P)),
                 (w3[:, :, :], io["ff_w3"].rearrange("d (m n) -> d m n", n=P)),
                 (w2[:, :, :], io["ff_w2"].rearrange("(m p) d -> p m d", p=P))]
        block = ctx.enter_context(nc.Block())

        @block.sync
        def _(sp):
            for dst, src in loads:
                sp.dma_start(dst, src).then_inc(weights_in, 16)

        @block.gpsimd
        def _(pool):
            for s in (gated, kept):
                pool.sem_inc(s.sem, s.per)
            with pool.Fori(0, B) as b:
                pool.wait_ge(y_sum.sem, at(y_sum, b, 0))
                nc.gpsimd.tensor_tensor(tg[:, :], acc[:, b, :], gateT[:, b, :], ALU.mult).then_inc(gated.sem, 1)
                pool.wait_ge(x_sum.sem, at(x_sum, b))
                nc.gpsimd.tensor_copy(xT[:, b, :], x2[:, :]).then_inc(kept.sem, 1)

        @block.tensor
        def _(pe):
            for s in (ms_mm, w1_mm, w3_mm, w2_mm, mean_mm, var_mm):
                pe.sem_inc(s.sem, s.per)
            pe.wait_ge(weights_in, 16 * len(loads))
            with pe.Fori(0, B) as b:
                pe.wait_ge(sq_ms.sem, at(sq_ms, b))
                pe.wait_ge(centred.sem, at(centred, b, 0))
                nc.tensor.matmul(pM[:, :], mean_w[:, :], sq[:, :], start=True, stop=True).then_inc(ms_mm.sem, 1)
                pe.wait_ge(y_norm.sem, at(y_norm, b))

                def ff_in(m):
                    pe.wait_ge(g_done.sem, at(g_done, b, m - 1) if m else at(g_done, b, 0))
                    nc.tensor.matmul(p1[:, m % 2, :], w1[:, m, :], y2[:, :], start=True, stop=True).then_inc(w1_mm.sem, 1)
                    nc.tensor.matmul(p3[:, m % 2, :], w3[:, m, :], y2[:, :], start=True, stop=True).then_inc(w3_mm.sem, 1)

                ff_in(0)
                for m in range(NF):
                    if m + 1 < NF:
                        ff_in(m + 1)
                    pe.wait_ge(g_done.sem, at(g_done, b, m + 1))
                    if m == 0:
                        pe.wait_ge(y_ff.sem, at(y_ff, b, 0))
                    nc.tensor.matmul(pO[:, :], w2[:, m, :], g[:, m % 2, :], start=(m == 0),
                                     stop=(m == NF - 1)).then_inc(w2_mm.sem, 1)
                pe.wait_ge(x_sum.sem, at(x_sum, b))
                pe.wait_ge(sd_ms.sem, at(sd_ms, b))
                nc.tensor.matmul(pM[:, :], mean_w[:, :], x2[:, :], start=True, stop=True).then_inc(mean_mm.sem, 1)
                pe.wait_ge(sq_var.sem, at(sq_var, b))
                nc.tensor.matmul(pV[:, :], mean_w[:, :], sq[:, :], start=True, stop=True).then_inc(var_mm.sem, 1)

        @block.scalar
        def _(act):
            for s in (sq_ms, sd_ms, silu_done, sq_var, sd_var):
                act.sem_inc(s.sem, s.per)
            with act.Fori(0, B) as b:
                act.wait_ge(y_sum.sem, at(y_sum, b))
                nc.scalar.activation(sq[:, :], y1[:, :], ACT.Square).then_inc(sq_ms.sem, 1)
                act.wait_ge(ms_mm.sem, at(ms_mm, b))
                nc.scalar.activation(sd[:, :], pM[:, :], ACT.Sqrt, bias=keep["rms_eps"][:, :]).then_inc(sd_ms.sem, 1)
                for m in range(NF):
                    act.wait_ge(w1_mm.sem, at(w1_mm, b, m + 1))
                    act.wait_ge(g_done.sem, at(g_done, b, max(m - 1, 0)))
                    nc.scalar.activation(sl[:, m % 2, :], p1[:, m % 2, :], ACT.Silu).then_inc(silu_done.sem, 1)
                act.wait_ge(centred.sem, at(centred, b))
                nc.scalar.activation(sq[:, :], xm[:, :], ACT.Square).then_inc(sq_var.sem, 1)
                act.wait_ge(var_mm.sem, at(var_mm, b))
                act.wait_ge(r_ms.sem, at(r_ms, b))
                nc.scalar.activation(sd[:, :], pV[:, :], ACT.Sqrt, bias=keep["ln_eps"][:, :]).then_inc(sd_var.sem, 1)

        @block.vector
        def _(dve):
            for s in (y_sum, r_ms, y_norm, g_done, y_ff, x_sum, centred, r_var, x_norm):
                dve.sem_inc(s.sem, s.per)
            dve.wait_ge(weights_in, 16 * len(loads))
            with dve.Fori(0, B) as b:
                dve.wait_ge(gated.sem, at(gated, b))
                nc.vector.tensor_tensor(y1[:, :], tg[:, :], xnT[:, b, :], ALU.add).then_inc(y_sum.sem, 1)
                dve.wait_ge(sd_ms.sem, at(sd_ms, b))
                dve.wait_ge(x_norm.sem, at(x_norm, b, 0))
                nc.vector.reciprocal(rs[:, :], sd[:, :]).then_inc(r_ms.sem, 1)
                dve.wait_ge(r_ms.sem, at(r_ms, b))
                dve.wait_ge(w3_mm.sem, at(w3_mm, b, 0))
                dve.wait_ge(y_sum.sem, at(y_sum, b))
                nc.vector.scalar_tensor_tensor(out=y2[:, :], in0=y1[:, :], scalar=ffn_w[:, 0:1], in1=rs[:, :],
                                               op0=ALU.mult, op1=ALU.mult).then_inc(y_norm.sem, 1)
                for m in range(NF):
                    dve.wait_ge(silu_done.sem, at(silu_done, b, m + 1))
                    dve.wait_ge(w3_mm.sem, at(w3_mm, b, m + 1))
                    dve.wait_ge(w2_mm.sem, at(w2_mm, b, max(m - 1, 0)))
                    nc.vector.tensor_tensor(g[:, m % 2, :], sl[:, m % 2, :], p3[:, m % 2, :], ALU.mult).then_inc(g_done.sem, 1)
                dve.wait_ge(w2_mm.sem, at(w2_mm, b))
                nc.vector.tensor_tensor(y3[:, :], y1[:, :], pO[:, :], ALU.add).then_inc(y_ff.sem, 1)
                dve.wait_ge(y_ff.sem, at(y_ff, b))
                dve.wait_ge(kept.sem, at(kept, b, 0))
                nc.vector.tensor_tensor(x2[:, :], y3[:, :], xT[:, b, :], ALU.add).then_inc(x_sum.sem, 1)
                dve.wait_ge(mean_mm.sem, at(mean_mm, b))
                dve.wait_ge(x_sum.sem, at(x_sum, b))
                nc.vector.tensor_tensor(xm[:, :], x2[:, :], pM[:, :], ALU.subtract).then_inc(centred.sem, 1)
                dve.wait_ge(sd_var.sem, at(sd_var, b))
                nc.vector.reciprocal(rs[:, :], sd[:, :]).then_inc(r_var.sem, 1)
                dve.wait_ge(r_var.sem, at(r_var, b))
                dve.wait_ge(centred.sem, at(centred, b))
                nc.vector.tensor_tensor(xnT[:, b, :], xm[:, :], rs[:, :], ALU.mult).then_inc(x_norm.sem, 1)


AH = 8
AP2 = AH // 2
INNER = AH * DK
WINDOW = 64
LAYERS = 2
HID = int(D * 4 * 2 / 3)
HM = [128, 128, HID - 256]
NEG = -3.0e38


def rotary_tables():
    half = np.arange(0, DK, 2, dtype=np.float32)
    inv_freq = (1.0 / 10000.0 ** (half / DK)).astype(np.float32)
    t = np.arange(T, dtype=np.float32)
    fr = (t[:, None] * inv_freq[None, :]).astype(np.float32).astype(np.float64)
    base = ((half + 0.4 * DK) / (1.4 * DK)).astype(np.float64)
    power = (t.astype(np.float64) - T // 2) / (WINDOW // 2)
    scale = base[None, :] ** power[:, None]
    cos, sin = np.cos(fr), np.sin(fr)
    q_scale = 8.0

    def pack(f, signed):
        lo, hi = (-f, f) if signed else (f, f)
        q = np.concatenate([lo * scale, hi * scale], -1) * q_scale
        k = np.concatenate([lo / scale, hi / scale], -1)
        return np.stack([q, k], 1)

    def lay(a):
        return np.ascontiguousarray(a.reshape(NC, C, 2, DK).transpose(1, 0, 2, 3)).astype(np.float32)

    return lay(pack(cos, False)), lay(pack(sin, True))


def attention_mask():
    i = np.arange(C)[:, None] + C
    j = np.arange(2 * C)[None, :]
    window = (i // WINDOW) * WINDOW
    ok = (j <= i) & (j + WINDOW >= i) & (j >= window - WINDOW)
    return np.where(ok, 0.0, NEG).astype(np.float32)


def stage_d(nc, io, keep, out):
    with ExitStack() as ctx:
        nm_ = "d_"
        sb = lambda n, s: ctx.enter_context(nc.sbuf_tensor(nm_ + n, s, F32))
        ps = lambda n, s: ctx.enter_context(nc.psum_tensor(nm_ + n, s, F32))
        signals = {"pe": [], "act": [], "dve": [], "pool": [], "sp": []}

        def sig(by, n, per=1):
            s = Signal(ctx, nc, nm_ + n, per)
            signals[by].append(s)
            return s

        xdT, x2T, ident, mean_w = keep["xnT"], keep["xT"], keep["ident"], keep["mean_w"]
        wqkv = sb("wqkv", [P, 3, INNER]); wo = sb("wo", [P, AP2, D]); w1 = sb("w1", [P, 2, HID]); w2 = sb("w2", [P, 3, D])
        b1 = sb("b1", [P, 2, 3]); b2 = sb("b2", [P, 1]); lg = sb("lg", [P, 1]); lb = sb("lb", [P, 1])
        mask = sb("mask", [P, 2 * C]); tcos = sb("tcos", [P, NC, 2, DK]); tsin = sb("tsin", [P, NC, 2, DK])
        sc = sb("sc", [P, 2, DK])
        xb = sb("xb", [P, T]); hs = sb("hs", [P, T]); sq = sb("sq", [P, 2, INNER]); ssq = sb("ssq", [P, 16])
        nrm = sb("nrm", [P, 16]); nmx = sb("nmx", [P, 16]); rn = sb("rn", [P, 16])
        qn = sb("qn", [P, 2, AH, DK]); qc = sb("qc", [P, 2, AH, DK]); qx = sb("qx", [P, 2, AH, DK]); qr = sb("qr", [P, 2 * INNER])
        vs = sb("vs", [P, NC, INNER]); qT = sb("qT", [P, AP2, C]); kT = sb("kT", [P, AP2, T])
        sm = sb("sm", [P, AH, 2 * C]); mx = sb("mx", [P, AH]); ex = sb("ex", [P, AH, 2 * C]); den = sb("den", [P, AH])
        rd = sb("rd", [P, AH]); pT = sb("pT", [P, AH, 2 * C]); o = sb("o", [P, INNER]); oT = sb("oT", [P, AP2, T])
        x1 = sb("x1", [P, T]); xm = sb("xm", [P, T]); sq1 = sb("sq1", [P, T]); sd = sb("sd", [P, T]); rs = sb("rs", [P, T])
        hn = sb("hn", [P, T]); hf = sb("hf", [P, T]); gl = sb("gl", [P, T]); hm = sb("hm", [P, 2, T]); xo = sb("xo", [P, T])
        pqk = ps("pqk", [P, 2, 512]); pv = ps("pv", [P, 512]); psm = ps("psm", [P, 4, 512]); po = ps("po", [P, 512])

        weights_in = ctx.enter_context(nc.semaphore(nm_ + "weights_in"))
        prepared = ctx.enter_context(nc.semaphore(nm_ + "prepared"))
        stored = ctx.enter_context(nc.semaphore(nm_ + "stored"))
        shifted, kept = sig("dve", "shifted", 2), sig("pool", "kept")
        cos_done = sig("pool", "cos_done", NC)
        q_mm, k_mm, v_mm, qkT_mm, s_mm, pT_mm, o_mm, oT_mm = (
            sig("pe", n, NC) for n in ("q_mm", "k_mm", "v_mm", "qkT_mm", "s_mm", "pT_mm", "o_mm", "oT_mm"))
        wo_mm, mean_mm, var_mm, a_mm, g_mm, w2_mm, out_mm = (
            sig("pe", "wo_mm"), sig("pe", "mean_mm"), sig("pe", "var_mm"), sig("pe", "a_mm", 3), sig("pe", "g_mm", 3),
            sig("pe", "w2_mm", 3), sig("pe", "out_mm"))
        squared, v_copy, norm_sqrt, qT_copy, exped, pT_copy, oT_copy = (
            sig("act", "squared", 2 * NC), sig("act", "v_copy", NC), sig("act", "norm_sqrt", NC), sig("act", "qT_copy", NC),
            sig("act", "exped", NC), sig("act", "pT_copy", NC), sig("act", "oT_copy", NC))
        sq_var, sd_var, gelu_done, out_copy = (sig("act", "sq_var"), sig("act", "sd_var"), sig("act", "gelu_done", 3),
                                               sig("act", "out_copy"))
        q_sum, norm_steps, q_norm, rot, q_rot, kT_copy, masked, maxed, r_den, p_half, o_norm = (
            sig("dve", "q_sum", NC), sig("dve", "norm_steps", 2 * NC), sig("dve", "q_norm", NC), sig("dve", "rot", 2 * NC),
            sig("dve", "q_rot", NC), sig("dve", "kT_copy", NC), sig("dve", "masked", NC), sig("dve", "maxed", NC),
            sig("dve", "r_den", NC), sig("dve", "p_half", NC), sig("dve", "o_norm", NC))
        hf_zero = sig("dve", "hf_zero", 3)
        x_sum, centred, r_var, normed, scaled, mid, x_done, total = (
            sig("dve", "x_sum"), sig("dve", "centred"), sig("dve", "r_var"), sig("dve", "normed"), sig("dve", "scaled"),
            sig("dve", "mid", 3), sig("dve", "x_done"), sig("dve", "total"))
        x_out = sig("sp", "x_out")

        def tile(c):
            return slice(c * C, (c + 1) * C)

        last_only = (out_mm, out_copy, total)

        def credit(eng, by, layer):
            for s in signals[by]:
                if s in last_only and layer == LAYERS - 1:
                    eng.sem_inc(s.sem, B * (LAYERS - 1) * s.per)
                if layer == 0:
                    eng.sem_inc(s.sem, s.per)

        def run_layer(layer):
            last_layer = layer == LAYERS - 1

            def at(s, b, k=None):
                return b * s.per + (layer * B * s.per + s.per + (s.per if k is None else k))

            col = lambda a: a.rearrange("(p o) -> p o", o=1)
            loads = [(wqkv[:, :, :], io["wqkv"][layer].rearrange("d (i n) -> d i n", i=3)),
                     (wo[:, :, :], io["wo"][layer].rearrange("(m p) d -> p m d", p=P)),
                     (w1[:, :, :], io["w1"][layer].rearrange("d (i n) -> d i n", i=2)),
                     (w2[:, 0:2, :], io["w2"][layer][0:256].rearrange("(m p) d -> p m d", p=P)),
                     (w2[0:HM[2], 2, :], io["w2"][layer][256:HID]),
                     (b2[:, :], col(io["b2"][layer])), (lg[:, :], col(io["ln_g"][layer])), (lb[:, :], col(io["ln_b"][layer])),
                     (mask[:, :], io["mask"]), (tcos[:, :, :, :], io["tcos"]), (tsin[:, :, :, :], io["tsin"]),
                     (sc[:, 0, :], io["q_scale"][layer].rearrange("(o d) -> o d", o=1).to_broadcast([P, DK])),
                     (sc[:, 1, :], io["k_scale"][layer].rearrange("(o d) -> o d", o=1).to_broadcast([P, DK]))]
            for i in range(2):
                for m in range(3):
                    lo = i * HID + m * P
                    loads.append((b1[0:HM[m], i, m:m + 1], col(io["b1"][layer][lo:lo + HM[m]])))

            with nc.Block() as block:
                @block.sync
                def _(sp):
                    with nc.allow_non_contiguous_dma(reason="small per-channel vectors"):
                        for dst, src in loads:
                            sp.dma_start(dst, src).then_inc(weights_in, 16)

                @block.vector
                def _(dve):
                    nc.vector.memset(hs[:, :], 0.0)
                    dve.wait_ge(weights_in, 16 * len(loads) * (layer + 1))
                    for c in range(NC):
                        nc.vector.tensor_tensor(tcos[:, c], tcos[:, c], sc[:, :, :], ALU.mult).then_inc(prepared, 1)
                        for d in range(2):
                            a = tsin[:, c, :, d * 32:d * 32 + 32]
                            nc.vector.tensor_tensor(a, a, sc[:, :, 32 - d * 32:64 - d * 32], ALU.mult).then_inc(prepared, 1)

            with nc.Block() as block:

                @block.gpsimd
                def _(pool):
                    credit(pool, "pool", layer)
                    with pool.Fori(0, B) as b:
                        pool.wait_ge(x_sum.sem, at(x_sum, b, 0))
                        nc.gpsimd.tensor_copy(xb[:, :], xdT[:, b, :]).then_inc(kept.sem, 1)
                        for c in range(NC):
                            pool.wait_ge(q_norm.sem, at(q_norm, b, c + 1))
                            pool.wait_ge(q_rot.sem, at(q_rot, b, c))
                            nc.gpsimd.tensor_tensor(qc[:, :, :, :], qn[:, :, :, :],
                                                    view(tcos, c * 2 * DK, [[DK, 2], [0, AH], [1, DK]]), ALU.mult).then_inc(cos_done.sem, 1)

                @block.tensor
                def _(pe):
                    credit(pe, "pe", layer)
                    with pe.Fori(0, B) as b:
                        pe.wait_ge(shifted.sem, at(shifted, b))
                        for c in range(NC):
                            pe.wait_ge(qT_copy.sem, at(qT_copy, b, c))
                            pe.wait_ge(kT_copy.sem, at(kT_copy, b, c))
                            if c == 0:
                                pe.wait_ge(gelu_done.sem, at(gelu_done, b, 0))
                                pe.wait_ge(mid.sem, at(mid, b, 0))
                            nc.tensor.matmul(pqk[:, 0, :], hs[:, tile(c)], wqkv[:, 0, :], start=True, stop=True).then_inc(q_mm.sem, 1)
                            nc.tensor.matmul(pqk[:, 1, :], hs[:, tile(c)], wqkv[:, 1, :], start=True, stop=True).then_inc(k_mm.sem, 1)
                            if c == 0:
                                pe.wait_ge(x_done.sem, at(x_done, b, 0))
                            else:
                                pe.wait_ge(v_copy.sem, at(v_copy, b, c))
                            nc.tensor.matmul(pv[:, :], hs[:, tile(c)], wqkv[:, 2, :], start=True, stop=True).then_inc(v_mm.sem, 1)
                            pe.wait_ge(q_rot.sem, at(q_rot, b, c + 1))
                            for i in range(2):
                                for m in range(AP2):
                                    mm = nc.tensor.transpose(pqk[:, i, tile(m)], qr[:, (i * AP2 + m) * P:(i * AP2 + m + 1) * P], ident[:, :])
                            mm.then_inc(qkT_mm.sem, 1)
                            pe.wait_ge(qT_copy.sem, at(qT_copy, b, c + 1))
                            pe.wait_ge(kT_copy.sem, at(kT_copy, b, c + 1))
                            lo = 0 if c else C
                            pe.wait_ge(pT_copy.sem, at(pT_copy, b, c))
                            pe.wait_ge(p_half.sem, at(p_half, b, c))
                            if c == 0:
                                pe.wait_ge(x_sum.sem, at(x_sum, b, 0))
                                pe.wait_ge(centred.sem, at(centred, b, 0))
                                pe.wait_ge(sd_var.sem, at(sd_var, b, 0))
                            for m in range(AP2):
                                for e in range(2):
                                    r = slice(e * DK, e * DK + DK)
                                    mm = nc.tensor.matmul(psm[:, e * 2 + m // 2, (m % 2) * 256 + lo:(m % 2) * 256 + 256], qT[r, m, :],
                                                          kT[r, m, (c - 1) * C + lo:(c + 1) * C], start=True, stop=True)
                            mm.then_inc(s_mm.sem, 1)
                            pe.wait_ge(exped.sem, at(exped, b, c + 1))
                            for hd in range(AH):
                                for w in range(1 if c == 0 else 0, 2):
                                    mm = nc.tensor.transpose(psm[:, hd // 2, (hd % 2) * 256 + w * C:(hd % 2) * 256 + w * C + C],
                                                             ex[:, hd, w * C:(w + 1) * C], ident[:, :])
                            mm.then_inc(pT_mm.sem, 1)
                            pe.wait_ge(pT_copy.sem, at(pT_copy, b, c + 1))
                            pe.wait_ge(p_half.sem, at(p_half, b, c + 1))
                            pe.wait_ge(v_copy.sem, at(v_copy, b, c + 1))
                            if c == 0:
                                pe.wait_ge(oT_copy.sem, at(oT_copy, b, 0))
                                if last_layer:
                                    pe.wait_ge(out_copy.sem, at(out_copy, b, 0))
                            for hd in range(AH):
                                for w in range(1 if c == 0 else 0, 2):
                                    mm = nc.tensor.matmul(po[:, hd * DK:(hd + 1) * DK], pT[:, hd, w * C:(w + 1) * C],
                                                          vs[:, c - 1 + w, slot_cols(hd)], start=(w == 0 or c == 0), stop=(w == 1))
                            mm.then_inc(o_mm.sem, 1)
                            pe.wait_ge(o_norm.sem, at(o_norm, b, c + 1))
                            for m in range(AP2):
                                mm = nc.tensor.transpose(po[:, tile(m)], o[:, tile(m)], ident[:, :])
                            mm.then_inc(oT_mm.sem, 1)
                            pe.wait_ge(oT_copy.sem, at(oT_copy, b, c + 1))
                        for m in range(AP2):
                            mm = nc.tensor.matmul(psm[:, 0, :], wo[:, m, :], oT[:, m, :], start=(m == 0), stop=(m == AP2 - 1))
                        mm.then_inc(wo_mm.sem, 1)
                        pe.wait_ge(hf_zero.sem, at(hf_zero, b))
                        nc.tensor.matmul(psm[:, 1, :], mean_w[:, :], hf[:, :], start=True, stop=True).then_inc(mean_mm.sem, 1)
                        pe.wait_ge(sq_var.sem, at(sq_var, b))
                        nc.tensor.matmul(psm[:, 2, :], mean_w[:, :], sq1[:, :], start=True, stop=True).then_inc(var_mm.sem, 1)
                        pe.wait_ge(scaled.sem, at(scaled, b))
                        for m in range(3):
                            n = HM[m]
                            if m > 0:
                                pe.wait_ge(gelu_done.sem, at(gelu_done, b, m))
                                pe.wait_ge(mid.sem, at(mid, b, m))
                            nc.tensor.matmul(pqk[0:n, 0, :], w1[:, 0, m * P:m * P + n], hn[:, :], start=True, stop=True).then_inc(a_mm.sem, 1)
                            nc.tensor.matmul(pqk[0:n, 1, :], w1[:, 1, m * P:m * P + n], hn[:, :], start=True, stop=True).then_inc(g_mm.sem, 1)
                            pe.wait_ge(mid.sem, at(mid, b, m + 1))
                            nc.tensor.matmul(pv[:, :], w2[0:n, m, :], hm[0:n, m % 2, :], start=(m == 0), stop=(m == 2)).then_inc(w2_mm.sem, 1)
                        if last_layer:
                            pe.wait_ge(total.sem, at(total, b))
                            for c in range(NC):
                                mm = nc.tensor.transpose(po[:, tile(c)], xo[:, tile(c)], ident[:, :])
                            mm.then_inc(out_mm.sem, 1)

                @block.scalar
                def _(act):
                    credit(act, "act", layer)
                    with act.Fori(0, B) as b:
                        for c in range(NC):
                            act.wait_ge(q_sum.sem, at(q_sum, b, c))
                            for i, s in enumerate((q_mm, k_mm)):
                                act.wait_ge(s.sem, at(s, b, c + 1))
                                nc.scalar.activation(sq[:, i, :], pqk[:, i, :], ACT.Square).then_inc(squared.sem, 1)
                            act.wait_ge(v_mm.sem, at(v_mm, b, c + 1))
                            if c == 0:
                                act.wait_ge(o_mm.sem, at(o_mm, b, 0))
                            nc.scalar.activation(vs[:, c, :], pv[:, :], ACT.Copy).then_inc(v_copy.sem, 1)
                            act.wait_ge(q_sum.sem, at(q_sum, b, c + 1))
                            act.wait_ge(norm_steps.sem, at(norm_steps, b, 2 * c))
                            nc.scalar.activation(nrm[:, :], ssq[:, :], ACT.Sqrt).then_inc(norm_sqrt.sem, 1)
                            act.wait_ge(qkT_mm.sem, at(qkT_mm, b, c + 1))
                            act.wait_ge(s_mm.sem, at(s_mm, b, c))
                            nc.scalar.activation(qT[:, :, :], pqk[:, 0, :].rearrange("p (m t) -> p m t", m=AP2), ACT.Copy).then_inc(qT_copy.sem, 1)
                            act.wait_ge(maxed.sem, at(maxed, b, c + 1))
                            act.wait_ge(pT_mm.sem, at(pT_mm, b, c))
                            act.wait_ge(r_den.sem, at(r_den, b, c))
                            lo = 0 if c else C
                            for hd in range(AH):
                                a = nc.scalar.activation(ex[:, hd, lo:], sm[:, hd, lo:], ACT.Exp, bias=mx[:, hd:hd + 1],
                                                         accum_out=den[:, hd:hd + 1])
                            a.then_inc(exped.sem, 1)
                            act.wait_ge(pT_mm.sem, at(pT_mm, b, c + 1))
                            act.wait_ge(o_mm.sem, at(o_mm, b, c))
                            nc.scalar.activation(pT[:, 0:4, lo:], psm[:, 0:2, :].rearrange("p e (m j) -> p (e m) j", m=2)[:, :, lo:], ACT.Copy).then_inc(pT_copy.sem, 1)
                            act.wait_ge(oT_mm.sem, at(oT_mm, b, c + 1))
                            if c == 0:
                                act.wait_ge(wo_mm.sem, at(wo_mm, b, 0))
                            nc.scalar.activation(oT[:, :, tile(c)], po[:, :].rearrange("p (m t) -> p m t", m=AP2), ACT.Copy).then_inc(oT_copy.sem, 1)
                        act.wait_ge(centred.sem, at(centred, b))
                        act.wait_ge(var_mm.sem, at(var_mm, b, 0))
                        nc.scalar.activation(sq1[:, :], xm[:, :], ACT.Square).then_inc(sq_var.sem, 1)
                        act.wait_ge(var_mm.sem, at(var_mm, b))
                        act.wait_ge(r_var.sem, at(r_var, b, 0))
                        nc.scalar.activation(sd[:, :], psm[:, 2, :], ACT.Sqrt, bias=keep["ln_eps"][:, :]).then_inc(sd_var.sem, 1)
                        for m in range(3):
                            n = HM[m]
                            act.wait_ge(g_mm.sem, at(g_mm, b, m + 1))
                            act.wait_ge(mid.sem, at(mid, b, m))
                            nc.scalar.activation(gl[0:n, :], pqk[0:n, 1, :], ACT.Gelu, bias=b1[0:n, 1, m:m + 1]).then_inc(gelu_done.sem, 1)
                        if last_layer:
                            act.wait_ge(out_mm.sem, at(out_mm, b))
                            act.wait_ge(x_out.sem, b * 16 + 1)
                            nc.scalar.activation(hf[:, :], po[:, :], ACT.Copy).then_inc(out_copy.sem, 1)

                @block.vector
                def _(dve):
                    credit(dve, "dve", layer)
                    with dve.Fori(0, B) as b:
                        dve.wait_ge(v_mm.sem, at(v_mm, b, 0))
                        nc.vector.tensor_copy(hs[0:DK, :], xdT[0:DK, b, :]).then_inc(shifted.sem, 1)
                        nc.vector.tensor_copy(hs[DK:P, 1:T], xdT[DK:P, b, 0:T - 1]).then_inc(shifted.sem, 1)
                        for c in range(NC):
                            dve.wait_ge(squared.sem, at(squared, b, 2 * c + 2))
                            dve.wait_ge(norm_sqrt.sem, at(norm_sqrt, b, c))
                            nc.vector.tensor_reduce(ssq[:, :], sq[:, :, :].rearrange("p i (h d) -> p (i h) d", d=DK), AX.X, ALU.add).then_inc(q_sum.sem, 1)
                            dve.wait_ge(norm_sqrt.sem, at(norm_sqrt, b, c + 1))
                            nc.vector.tensor_scalar(nmx[:, :], nrm[:, :], 1e-12, None, ALU.max).then_inc(norm_steps.sem, 1)
                            dve.wait_ge(norm_steps.sem, at(norm_steps, b, 2 * c + 1))
                            nc.vector.reciprocal(rn[:, :], nmx[:, :]).then_inc(norm_steps.sem, 1)
                            dve.wait_ge(norm_steps.sem, at(norm_steps, b, 2 * c + 2))
                            dve.wait_ge(cos_done.sem, at(cos_done, b, c))
                            dve.wait_ge(k_mm.sem, at(k_mm, b, c + 1))
                            nc.vector.tensor_tensor(qn[:, :, :, :].rearrange("p i h d -> p (i h) d"),
                                                    pqk[:, :, :].rearrange("p i (h d) -> p (i h) d", d=DK),
                                                    view(rn, 0, [[1, 16], [0, DK]]), ALU.mult).then_inc(q_norm.sem, 1)
                            dve.wait_ge(q_norm.sem, at(q_norm, b, c + 1))
                            for d in range(2):
                                nc.vector.tensor_tensor(qx[:, :, :, d * 32:d * 32 + 32], qn[:, :, :, 32 - d * 32:64 - d * 32],
                                                        view(tsin, c * 2 * DK + d * 32, [[DK, 2], [0, AH], [1, 32]]), ALU.mult).then_inc(rot.sem, 1)
                            dve.wait_ge(rot.sem, at(rot, b, 2 * c + 2))
                            dve.wait_ge(cos_done.sem, at(cos_done, b, c + 1))
                            dve.wait_ge(qkT_mm.sem, at(qkT_mm, b, c))
                            nc.vector.tensor_tensor(qr[:, :], qc[:, :, :, :].rearrange("p i h d -> p (i h d)"),
                                                    qx[:, :, :, :].rearrange("p i h d -> p (i h d)"), ALU.add).then_inc(q_rot.sem, 1)
                            dve.wait_ge(qkT_mm.sem, at(qkT_mm, b, c + 1))
                            nc.vector.tensor_copy(kT[:, :, tile(c)], pqk[:, 1, :].rearrange("p (m t) -> p m t", m=AP2)).then_inc(kT_copy.sem, 1)
                            lo = 0 if c else C
                            dve.wait_ge(s_mm.sem, at(s_mm, b, c + 1))
                            dve.wait_ge(exped.sem, at(exped, b, c))
                            nc.vector.tensor_tensor(sm[:, :, lo:], psm[:, :, :].rearrange("p e (m j) -> p (e m) j", m=2)[:, :, lo:],
                                                    view(mask, lo, [[0, AH], [1, 2 * C - lo]]), ALU.add).then_inc(masked.sem, 1)
                            dve.wait_ge(masked.sem, at(masked, b, c + 1))
                            nc.vector.tensor_reduce(mx[:, :], sm[:, :, lo:], AX.X, ALU.max, negate=True).then_inc(maxed.sem, 1)
                            dve.wait_ge(exped.sem, at(exped, b, c + 1))
                            dve.wait_ge(o_norm.sem, at(o_norm, b, c))
                            nc.vector.reciprocal(rd[:, :], den[:, :]).then_inc(r_den.sem, 1)
                            dve.wait_ge(pT_mm.sem, at(pT_mm, b, c + 1))
                            dve.wait_ge(o_mm.sem, at(o_mm, b, c))
                            nc.vector.tensor_copy(pT[:, 4:8, lo:], psm[:, 2:4, :].rearrange("p e (m j) -> p (e m) j", m=2)[:, :, lo:]).then_inc(p_half.sem, 1)
                            dve.wait_ge(o_mm.sem, at(o_mm, b, c + 1))
                            dve.wait_ge(r_den.sem, at(r_den, b, c + 1))
                            dve.wait_ge(oT_mm.sem, at(oT_mm, b, c))
                            for e in range(2):
                                ins = nc.vector.tensor_tensor(
                                    view(o, e * DK, [[2 * DK, AP2], [1, DK]]), view(po, e * 4 * DK, [[DK, AP2], [1, DK]]),
                                    view(rd, e * 4, [[1, AP2], [0, DK]]), ALU.mult)
                            ins.then_inc(o_norm.sem, 1)
                        dve.wait_ge(wo_mm.sem, at(wo_mm, b))
                        dve.wait_ge(kept.sem, at(kept, b))
                        nc.vector.tensor_tensor(x1[:, :], xb[:, :], psm[:, 0, :], ALU.add).then_inc(x_sum.sem, 1)
                        dve.wait_ge(x_sum.sem, at(x_sum, b))
                        if last_layer:
                            dve.wait_ge(x_out.sem, b * 16 + 1)
                        nc.vector.memset(hf[DK:P, 0:1], 0.0).then_inc(hf_zero.sem, 1)
                        nc.vector.tensor_copy(hf[0:DK, :], x1[0:DK, :]).then_inc(hf_zero.sem, 1)
                        nc.vector.tensor_copy(hf[DK:P, 1:T], x1[DK:P, 0:T - 1]).then_inc(hf_zero.sem, 1)
                        dve.wait_ge(mean_mm.sem, at(mean_mm, b))
                        dve.wait_ge(hf_zero.sem, at(hf_zero, b))
                        nc.vector.tensor_tensor(xm[:, :], hf[:, :], psm[:, 1, :], ALU.subtract).then_inc(centred.sem, 1)
                        dve.wait_ge(sd_var.sem, at(sd_var, b))
                        nc.vector.reciprocal(rs[:, :], sd[:, :]).then_inc(r_var.sem, 1)
                        dve.wait_ge(r_var.sem, at(r_var, b))
                        dve.wait_ge(g_mm.sem, at(g_mm, b, 0))
                        dve.wait_ge(centred.sem, at(centred, b))
                        nc.vector.tensor_tensor(rs[:, :], xm[:, :], rs[:, :], ALU.mult).then_inc(normed.sem, 1)
                        dve.wait_ge(normed.sem, at(normed, b))
                        nc.vector.tensor_scalar(hn[:, :], rs[:, :], lg[:, 0:1], lb[:, 0:1], ALU.mult, ALU.add).then_inc(scaled.sem, 1)
                        for m in range(3):
                            n = HM[m]
                            dve.wait_ge(a_mm.sem, at(a_mm, b, m + 1))
                            dve.wait_ge(gelu_done.sem, at(gelu_done, b, m + 1))
                            dve.wait_ge(w2_mm.sem, at(w2_mm, b, max(m - 1, 0)))
                            nc.vector.scalar_tensor_tensor(out=hm[0:n, m % 2, :], in0=pqk[0:n, 0, :], scalar=b1[0:n, 0, m:m + 1],
                                                           in1=gl[0:n, :], op0=ALU.add, op1=ALU.mult).then_inc(mid.sem, 1)
                        dve.wait_ge(w2_mm.sem, at(w2_mm, b))
                        if last_layer:
                            dve.wait_ge(out_mm.sem, at(out_mm, b, 0))
                        xnew = xo[:, :] if last_layer else xdT[:, b, :]
                        nc.vector.scalar_tensor_tensor(out=xnew, in0=pv[:, :], scalar=b2[:, 0:1], in1=x1[:, :],
                                                       op0=ALU.add, op1=ALU.add).then_inc(x_done.sem, 1)
                        if last_layer:
                            dve.wait_ge(x_done.sem, at(x_done, b))
                            nc.vector.tensor_tensor(xo[:, :], xo[:, :], x2T[:, b, :], ALU.add).then_inc(total.sem, 1)

                if last_layer:
                    out_v = out.rearrange("b (c p) d -> b p c d", p=P)

                    @block.sync
                    def _(sp):
                        sp.sem_inc(x_out.sem, 1)
                        with sp.Fori(0, B) as b:
                            sp.wait_ge(out_copy.sem, at(out_copy, b))
                            sp.dma_start(out_v[b], hf[:, :].rearrange("p (c d) -> p c d", c=NC)).then_inc(x_out.sem, 16)
                        sp.wait_ge(x_out.sem, 16 * B + 1)

        for layer in range(LAYERS):
            run_layer(layer)


def slot_cols(slot):
    head = 2 * (slot % 4) + slot // 4
    return slice(head * DK, (head + 1) * DK)


def build(nc, io, outs):
    with ExitStack() as ctx:
        sb = lambda n, s: ctx.enter_context(nc.sbuf_tensor(n, s, F32))
        keep = dict(ident=sb("ident", [P, P]), mean_w=sb("mean_w", [P, P]), xT=sb("xT", [P, B, T]),
                    xnT=sb("xnT", [P, B, T]), hT=sb("hT", [P, B, T]), gateT=sb("gateT", [P, B, T]),
                    acc=sb("acc", [P, B, T]), beta=sb("beta", [P, B, NC, H]),
                    ln_eps=sb("ln_eps", [P, 1]), rms_eps=sb("rms_eps", [P, 1]))
        with nc.Block() as block:
            @block.vector
            def _(dve):
                nc.vector.memset(keep["ln_eps"][:, :], LN_EPS)
                nc.vector.memset(keep["rms_eps"][:, :], RMS_EPS)
        stage_a(nc, io, keep, None)
        stage_b(nc, io, keep)
        stage_c(nc, io, keep)
        stage_d(nc, io, keep, outs)


_INS = {'x': 'L0_attn_x', 'norm_in_w': 'L0_attn_norm_in_w', 'conv_w': 'L0_attn_conv_w', 'conv_b': 'L0_attn_conv_b',
        'q_w': 'L0_attn_q_w', 'k_w': 'L0_attn_k_w', 'v_w': 'L0_attn_v_w', 'out_w': 'L0_attn_out_w',
        'alpha_w': 'L0_attn_alpha_w', 'alpha_b': 'L0_attn_alpha_b', 'beta_w': 'L0_attn_beta_w',
        'beta_b': 'L0_attn_beta_b', 'head_norm_w': 'L0_attn_head_norm_w', 'u1_w': 'L0_attn_u1_w',
        'u1_b': 'L0_attn_u1_b', 'u2_w': 'L0_attn_u2_w', 'u2_b': 'L0_attn_u2_b',
        'ff_norm_w': 'L0_attn_ff_norm_w', 'ff_w1': 'L0_attn_ff_w1', 'ff_w3': 'L0_attn_ff_w3', 'ff_w2': 'L0_attn_ff_w2',
        'wqkv': 'L0_ffn_wqkv', 'q_scale': 'L0_ffn_q_scale', 'k_scale': 'L0_ffn_k_scale', 'wo': 'L0_ffn_wo',
        'ln_g': 'L0_ffn_ln_g', 'ln_b': 'L0_ffn_ln_b', 'w1': 'L0_ffn_w1', 'b1': 'L0_ffn_b1', 'w2': 'L0_ffn_w2',
        'b2': 'L0_ffn_b2'}


def kernel(**inputs):
    import concourse.bacc as _bacc
    from concourse.bass_utils import run_bass_kernel_spmd as _run

    nc = _bacc.Bacc("TRN2", target_bir_lowering=False, num_devices=1)
    arrays, io = {}, {}
    host = {k: np.ascontiguousarray(inputs[v]) for k, v in _INS.items()}
    host["ident"] = np.eye(P, dtype=np.float32)
    host["mean_w"] = np.full((P, P), 1.0 / D, np.float32)
    host["masks"] = level_consts()
    host["tcos"], host["tsin"] = rotary_tables()
    host["mask"] = attention_mask()
    host["sel"] = (np.arange(P)[:, None] // DK == np.arange(2)[None, :]).astype(np.float32)
    for name, a in host.items():
        arrays[f"in_{name}_dram"] = a
        io[name] = nc.dram_tensor(f"in_{name}_dram", a.shape, mybir.dt.from_np(a.dtype), kind="ExternalInput").ap()
    out = nc.dram_tensor("out_0_dram", (B, T, D), F32, kind="ExternalOutput").ap()
    build(nc, io, out)
    r = _run(nc, [arrays], core_ids=[0])
    return r.results[0]["out_0_dram"]
```

```python
from contextlib import ExitStack

import numpy as np

import concourse.bass as bass
from concourse import mybir

F32 = mybir.dt.float32
ALU = mybir.AluOpType
ACT = mybir.ActivationFunctionType
AX = mybir.AxisListType

P = 128
B, T, D = 4, 512, 128
C = 128
NC = T // C
TOK = B * T
H, DK = 16, 64
HP = H // 2
LEVELS = 7
HALF = C // 2
KCONV = 4
R = 64
RMS_EPS = 1e-6
LN_EPS = 1e-5


class Signal:

    def __init__(self, ctx, nc, name, per=1):
        self.sem = ctx.enter_context(nc.semaphore(name))
        self.per = per

    def at(self, hp, b, k=None):
        k = self.per if k is None else k
        return hp * (B * self.per) + ((b + 1) * self.per + k)


def view(t, offset, dims, parts=P, part0=0):
    row = 1
    for s in t.shape[1:]:
        row *= s
    return bass.AP(tensor=t, offset=part0 * row + offset, ap=[[row, parts]] + [list(d) for d in dims])


def halves(t, offset, n, second, count, outer=None, parts=P, part0=0):
    dims = [[2 * n, count // (2 * n)], [1, n]] if n > 1 else [[2, count // 2]]
    return view(t, offset + (n if second else 0), ([outer] if outer else []) + dims, parts, part0)


def level_consts():
    j = np.arange(C)[:, None]
    masks = np.zeros((C, LEVELS, NC * HALF), np.float32)
    for l in range(LEVELS):
        n = 1 << l
        i = np.arange(HALF)[None, :]
        block = i // n
        one = ((j // (2 * n)) == block) & ((j % (2 * n)) < n)
        masks[:, l, :] = np.tile(one.astype(np.float32), (1, NC))
    return masks


def stage_a(nc, io, keep, per_batch):
    with ExitStack() as ctx:
        sb = lambda n, s: ctx.enter_context(nc.sbuf_tensor("a_" + n, s, F32))
        ps = lambda n, s: ctx.enter_context(nc.psum_tensor("a_" + n, s, F32))
        sig = lambda n, per=1: Signal(ctx, nc, "a_" + n, per)
        ident, mean_w = keep["ident"], keep["mean_w"]
        xT, xnT, hT, gateT, beta = (keep[k] for k in ("xT", "xnT", "hT", "gateT", "beta"))

        norm_w = sb("norm_w", [P, 1]); conv_w = sb("conv_w", [P, KCONV]); conv_b = sb("conv_b", [P, 1])
        u1_w = sb("u1_w", [P, R]); u1_b = sb("u1_b", [R, 1]); u2_w = sb("u2_w", [R, D]); u2_b = sb("u2_b", [P, 1])
        beta_w = sb("beta_w", [P, H]); beta_b = sb("beta_b", [P, H])
        xs = sb("xs", [P, NC, D])
        xc = sb("xc", [P, T]); xm = sb("xm", [P, T]); sq = sb("sq", [P, T]); sd = sb("sd", [P, T])
        rs = sb("rs", [P, T]); xn = sb("xn", [P, T]); hpad = sb("hpad", [P, KCONV - 1 + T])
        cv = sb("cv", [P, T]); hs = sb("hs", [P, T]); g1 = sb("g1", [R, T]); bz = sb("bz", [P, NC, H])
        pX = ps("pX", [P, T]); pM = ps("pM", [P, T]); pV = ps("pV", [P, T]); pR = ps("pR", [P, T])
        pG = ps("pG", [P, T]); pU = ps("pU", [P, T]); pB = ps("pB", [P, NC * H])

        weights_in = ctx.enter_context(nc.semaphore("a_weights_in"))
        x_in = ctx.enter_context(nc.semaphore("a_x_in"))
        pad_zero = ctx.enter_context(nc.semaphore("a_pad_zero"))
        transposed, mean_mm, var_mm, ms_mm = sig("transposed"), sig("mean_mm"), sig("var_mm"), sig("ms_mm")
        u1_mm, u2_mm, beta_mm = sig("u1_mm"), sig("u2_mm"), sig("beta_mm")
        x_copied, sq_var, sd_var, sq_ms, sd_ms = sig("x_copied"), sig("sq_var"), sig("sd_var"), sig("sq_ms"), sig("sd_ms")
        silu_h, silu_g, gate_done, beta_done = sig("silu_h"), sig("silu_g"), sig("gate_done"), sig("beta_done")
        centred, r_var, normed, r_ms, scaled, conv, beta_sum = (
            sig("centred"), sig("r_var"), sig("normed"), sig("r_ms"), sig("scaled"), sig("conv", KCONV), sig("beta_sum"))
        kept = sig("kept", 3)
        x_view = io["x"].rearrange("b (c p) d -> b p c d", p=P)
        loads = [(norm_w[:, :], io["norm_in_w"].rearrange("(p o) -> p o", o=1)),
                 (conv_w[:, :], io["conv_w"].rearrange("p o k -> p (o k)")),
                 (conv_b[:, :], io["conv_b"].rearrange("(p o) -> p o", o=1)),
                 (u1_w[:, :], io["u1_w"]), (u1_b[:, :], io["u1_b"].rearrange("(p o) -> p o", o=1)),
                 (u2_w[:, :], io["u2_w"]), (u2_b[:, :], io["u2_b"].rearrange("(p o) -> p o", o=1)),
                 (beta_w[:, :], io["beta_w"]),
                 (beta_b[:, :], io["beta_b"].rearrange("(o h) -> o h", o=1).to_broadcast([P, H])),
                 (ident[:, :], io["ident"]), (mean_w[:, :], io["mean_w"])]
        block = ctx.enter_context(nc.Block())

        def at(s, b, k=None):
            return s.at(0, 0, k) if isinstance(b, int) and b == 0 else b * s.per + (s.per + (k or s.per))

        def before(s, b, k=None):
            return b * s.per + (k or s.per)

        @block.sync
        def _(sp):
            for dst, src in loads:
                sp.dma_start(dst, src).then_inc(weights_in, 16)
            with sp.Fori(0, B) as b:
                sp.wait_ge(transposed.sem, before(transposed, b))
                sp.dma_start(xs[:, :, :], x_view[b]).then_inc(x_in, 16)

        @block.tensor
        def _(pe):
            pe.sem_inc(transposed.sem, 1)
            pe.sem_inc(mean_mm.sem, 1); pe.sem_inc(var_mm.sem, 1); pe.sem_inc(ms_mm.sem, 1)
            pe.sem_inc(u1_mm.sem, 1); pe.sem_inc(u2_mm.sem, 1); pe.sem_inc(beta_mm.sem, 1)
            pe.wait_ge(weights_in, 16 * len(loads))
            with pe.Fori(0, B) as b:
                pe.wait_ge(x_in, b * 16 + 16)
                pe.wait_ge(x_copied.sem, before(x_copied, b))
                for c in range(NC):
                    last = nc.tensor.transpose(pX[:, c * C:(c + 1) * C], xs[:, c, :], ident[:, :])
                last.then_inc(transposed.sem, 1)
                pe.wait_ge(x_copied.sem, at(x_copied, b))
                pe.wait_ge(centred.sem, before(centred, b))
                nc.tensor.matmul(pM[:, :], mean_w[:, :], xc[:, :], start=True, stop=True).then_inc(mean_mm.sem, 1)
                pe.wait_ge(sq_var.sem, at(sq_var, b))
                pe.wait_ge(sd_var.sem, before(sd_var, b))
                nc.tensor.matmul(pV[:, :], mean_w[:, :], sq[:, :], start=True, stop=True).then_inc(var_mm.sem, 1)
                pe.wait_ge(normed.sem, at(normed, b))
                pe.wait_ge(silu_g.sem, before(silu_g, b))
                nc.tensor.matmul(pG[0:R, :], u1_w[:, :], xn[:, :], start=True, stop=True).then_inc(u1_mm.sem, 1)
                pe.wait_ge(sq_ms.sem, at(sq_ms, b))
                pe.wait_ge(sd_ms.sem, before(sd_ms, b))
                nc.tensor.matmul(pR[:, :], mean_w[:, :], sq[:, :], start=True, stop=True).then_inc(ms_mm.sem, 1)
                pe.wait_ge(silu_g.sem, at(silu_g, b))
                pe.wait_ge(gate_done.sem, before(gate_done, b))
                nc.tensor.matmul(pU[:, :], u2_w[:, :], g1[:, :], start=True, stop=True).then_inc(u2_mm.sem, 1)
                pe.wait_ge(silu_h.sem, at(silu_h, b))
                pe.wait_ge(beta_sum.sem, before(beta_sum, b))
                for c in range(NC):
                    last = nc.tensor.matmul(pB[:, c * H:(c + 1) * H], hs[:, c * C:(c + 1) * C], beta_w[:, :],
                                            start=True, stop=True)
                last.then_inc(beta_mm.sem, 1)

        @block.scalar
        def _(act):
            for s in (x_copied, sq_var, sd_var, sq_ms, sd_ms, silu_h, silu_g, gate_done, beta_done):
                act.sem_inc(s.sem, 1)
            act.wait_ge(weights_in, 16 * len(loads))
            with act.Fori(0, B) as b:
                act.wait_ge(transposed.sem, at(transposed, b))
                act.wait_ge(centred.sem, before(centred, b))
                act.wait_ge(kept.sem, before(kept, b))
                nc.scalar.activation(xc[:, :], pX[:, :], ACT.Copy).then_inc(x_copied.sem, 1)
                act.wait_ge(centred.sem, at(centred, b))
                nc.scalar.activation(sq[:, :], xm[:, :], ACT.Square).then_inc(sq_var.sem, 1)
                act.wait_ge(var_mm.sem, at(var_mm, b))
                nc.scalar.activation(sd[:, :], pV[:, :], ACT.Sqrt, bias=keep["ln_eps"][:, :]).then_inc(sd_var.sem, 1)
                act.wait_ge(normed.sem, at(normed, b))
                nc.scalar.activation(sq[:, :], xn[:, :], ACT.Square).then_inc(sq_ms.sem, 1)
                act.wait_ge(ms_mm.sem, at(ms_mm, b))
                act.wait_ge(r_var.sem, at(r_var, b))
                nc.scalar.activation(sd[:, :], pR[:, :], ACT.Sqrt, bias=keep["rms_eps"][:, :]).then_inc(sd_ms.sem, 1)
                act.wait_ge(u1_mm.sem, at(u1_mm, b))
                act.wait_ge(u2_mm.sem, before(u2_mm, b))
                nc.scalar.activation(g1[:, :], pG[0:R, :], ACT.Silu, bias=u1_b[:, :]).then_inc(silu_g.sem, 1)
                act.wait_ge(conv.sem, at(conv, b))
                act.wait_ge(beta_mm.sem, before(beta_mm, b))
                nc.scalar.activation(hs[:, :], cv[:, :], ACT.Silu).then_inc(silu_h.sem, 1)
                act.wait_ge(u2_mm.sem, at(u2_mm, b))
                nc.scalar.activation(gateT[:, b, :], pU[:, :], ACT.Sigmoid, bias=u2_b[:, :]).then_inc(gate_done.sem, 1)
                act.wait_ge(beta_sum.sem, at(beta_sum, b))
                nc.scalar.activation(beta[:, b, :, 0:H], bz[:, :, :], ACT.Sigmoid).then_inc(beta_done.sem, 1)

        @block.vector
        def _(dve):
            for s in (centred, r_var, normed, r_ms, scaled, conv, beta_sum):
                dve.sem_inc(s.sem, s.per)
            nc.vector.memset(hpad[:, 0:KCONV - 1], 0.0).then_inc(pad_zero, 1)
            dve.wait_ge(pad_zero, 1)
            dve.wait_ge(weights_in, 16 * len(loads))
            with dve.Fori(0, B) as b:
                dve.wait_ge(mean_mm.sem, at(mean_mm, b))
                dve.wait_ge(x_copied.sem, at(x_copied, b))
                nc.vector.tensor_tensor(xm[:, :], xc[:, :], pM[:, :], ALU.subtract).then_inc(centred.sem, 1)
                dve.wait_ge(sd_var.sem, at(sd_var, b))
                nc.vector.reciprocal(rs[:, :], sd[:, :]).then_inc(r_var.sem, 1)
                dve.wait_ge(r_var.sem, at(r_var, b))
                dve.wait_ge(kept.sem, before(kept, b))
                dve.wait_ge(u1_mm.sem, before(u1_mm, b))
                dve.wait_ge(centred.sem, at(centred, b))
                nc.vector.tensor_tensor(xn[:, :], xm[:, :], rs[:, :], ALU.mult).then_inc(normed.sem, 1)
                dve.wait_ge(sd_ms.sem, at(sd_ms, b))
                dve.wait_ge(normed.sem, at(normed, b))
                nc.vector.reciprocal(rs[:, :], sd[:, :]).then_inc(r_ms.sem, 1)
                dve.wait_ge(r_ms.sem, at(r_ms, b))
                dve.wait_ge(conv.sem, before(conv, b))
                nc.vector.scalar_tensor_tensor(out=hpad[:, KCONV - 1:], in0=xn[:, :], scalar=norm_w[:, 0:1],
                                               in1=rs[:, :], op0=ALU.mult, op1=ALU.mult).then_inc(scaled.sem, 1)
                dve.wait_ge(scaled.sem, at(scaled, b))
                dve.wait_ge(silu_h.sem, before(silu_h, b))
                nc.vector.tensor_scalar(cv[:, :], hpad[:, 0:T], conv_w[:, 0:1], conv_b[:, 0:1],
                                        ALU.mult, ALU.add).then_inc(conv.sem, 1)
                for k in range(1, KCONV):
                    dve.wait_ge(conv.sem, at(conv, b, k))
                    nc.vector.scalar_tensor_tensor(out=cv[:, :], in0=hpad[:, k:k + T], scalar=conv_w[:, k:k + 1],
                                                   in1=cv[:, :], op0=ALU.mult, op1=ALU.add).then_inc(conv.sem, 1)
                dve.wait_ge(beta_mm.sem, at(beta_mm, b))
                dve.wait_ge(beta_done.sem, before(beta_done, b))
                nc.vector.tensor_tensor(bz[:, :, :], pB[:, :].rearrange("p (c h) -> p c h", c=NC),
                                        view(beta_b, 0, [[0, NC], [1, H]]), ALU.add).then_inc(beta_sum.sem, 1)

        @block.gpsimd
        def _(pool):
            pool.sem_inc(kept.sem, 3)
            with pool.Fori(0, B) as b:
                pool.wait_ge(x_copied.sem, at(x_copied, b))
                nc.gpsimd.tensor_copy(xT[:, b, :], xc[:, :]).then_inc(kept.sem, 1)
                pool.wait_ge(normed.sem, at(normed, b))
                nc.gpsimd.tensor_copy(xnT[:, b, :], xn[:, :]).then_inc(kept.sem, 1)
                pool.wait_ge(silu_h.sem, at(silu_h, b))
                nc.gpsimd.tensor_copy(hT[:, b, :], hs[:, :]).then_inc(kept.sem, 1)


def stage_b(nc, io, keep):
    with ExitStack() as ctx:
        sb = lambda n, s: ctx.enter_context(nc.sbuf_tensor("b_" + n, s, F32))
        ps = lambda n, s: ctx.enter_context(nc.psum_tensor("b_" + n, s, F32))
        sig = lambda n, per=1: Signal(ctx, nc, "b_" + n, per)
        ident, hT, beta, acc = keep["ident"], keep["hT"], keep["beta"], keep["acc"]

        wqka = sb("wqka", [P, 3, HP + 1, P]); wv = sb("wv", [P, HP + 1, P]); wo = sb("wo", [P, HP, D])
        hn = sb("hn", [P, HP]); ab = sb("ab", [P, HP + 1])
        wc = sb("wc", [P, 3, P]); abc = sb("abc", [P, 1]); woc = sb("woc", [P, D])
        masks = sb("masks", [P, LEVELS, NC * HALF]); ident4 = sb("ident4", [P, NC * C]); sel = sb("sel", [P, 2])
        sqb = sb("sqb", [P, 2, T]); qs = sb("qs", [P, T]); kr2 = [sb(f"kr{i}", [P, T]) for i in range(2)]; al = sb("al", [P, T])
        ka = sb("ka", [P, T])
        kq = [sb(f"kq{i}", [P, 2, T]) for i in range(2)]
        tot = sb("tot", [P, T]); totc = [sb(f"totc{i}", [P, NC]) for i in range(2)]
        nrm = sb("nrm", [P, 2, NC, 2]); nre = sb("nre", [P, 2, NC, 2])
        rn = [sb(f"rn{i}", [P, 2, NC, 2]) for i in range(2)]
        bk = sb("bk", [P, NC, 2]); bk2 = sb("bk2", [P, NC, 2 * DK])
        bv = [sb(f"bv{i}", [P, NC, 2, DK]) for i in range(2)]
        em = sb("em", [P, 2 * LEVELS + 4, T])
        ysb = sb("ysb", [P, 2, NC * C])
        tt = [sb(f"tt{i}", [P, 2, 2, NC * C]) for i in range(2)]
        mt = [sb(f"mt{i}", [P, 2, NC * C]) for i in range(2)]
        kh = [sb(f"kh{i}", [P, NC, P]) for i in range(2)]
        st = sb("st", [P, 2 * DK]); xsb = sb("xsb", [P, 2, DK]); us = sb("us", [P, 2, DK])
        yt = sb("yt", [P, NC, 2, DK]); ysq = sb("ysq", [P, NC, 2, DK]); yss = sb("yss", [P, NC * 2])
        ysd = sb("ysd", [P, NC * 2]); yr = sb("yr", [P, NC * 2]); yn = sb("yn", [P, NC, 2 * DK])
        yT = sb("yT", [P, T])

        pj = ps("pj", [P, 512]); lv = ps("lv", [P, 2, 512]); wk = ps("wk", [P, 3, 512])
        cx = ps("cx", [P, 512]); cu = ps("cu", [P, 512])

        weights_in = ctx.enter_context(nc.semaphore("b_weights_in"))
        scaled_wo = ctx.enter_context(nc.semaphore("b_scaled_wo"))
        loads = [(wqka[:, 0, 0:HP], io["q_w"].rearrange("d (h n) -> d h n", h=HP)),
                 (wqka[:, 1, 0:HP], io["k_w"].rearrange("d (h n) -> d h n", h=HP)),
                 (wqka[:, 2, 0:HP], io["alpha_w"].rearrange("d (h n) -> d h n", h=HP)),
                 (wv[:, 0:HP, :], io["v_w"].rearrange("d (h n) -> d h n", h=HP)),
                 (wo[:, :, :], io["out_w"].rearrange("(h p) d -> p h d", p=P)),
                 (hn[:, :], io["head_norm_w"].rearrange("(a b) d -> (b d) a", b=2)),
                 (ab[:, 0:HP], io["alpha_b"].rearrange("(h p) -> p h", p=P)),
                 (masks[:, :, :], io["masks"]),
                 (sel[:, :], io["sel"])]
        with nc.Block() as block:
            @block.sync
            def _(sp):
                with nc.allow_non_contiguous_dma(reason="small per-channel vectors"):
                    for dst, src in loads:
                        sp.dma_start(dst, src).then_inc(weights_in, 16)

            @block.vector
            def _(dve):
                for t in [em, *tt, *mt]:
                    nc.vector.memset(t[:], 0.0)
                for c in range(NC):
                    nc.vector.tensor_copy(ident4[:, c * C:(c + 1) * C], ident[:, :])
                dve.wait_ge(weights_in, 16 * len(loads))
                nc.vector.tensor_tensor(wo[:, :, :], wo[:, :, :], view(hn, 0, [[1, HP], [0, D]]),
                                        ALU.mult).then_inc(scaled_wo, 1)

            @block.gpsimd
            def _(pool):
                nc.gpsimd.memset(wqka[:, :, HP, :], 0.0)
                nc.gpsimd.memset(wv[:, HP, :], 0.0)
                nc.gpsimd.memset(ab[:, HP:], 0.0)
                nc.gpsimd.memset(beta[:, :, :, H:], 0.0)
                for t in [*kq, *bv, *kh, *rn, *totc, woc, acc, st]:
                    nc.gpsimd.memset(t[:], 0.0)

        q_mm, k_mm, a_mm, v_mm, ssq_mm, bb_mm = (sig(n) for n in ("q_mm", "k_mm", "a_mm", "v_mm", "ssq_mm", "bb_mm"))
        diag_mm, lvl_mm, tr_mm = sig("diag_mm", 2), sig("lvl_mm", 2 * LEVELS), sig("tr_mm", 2)
        y_mm, z_mm = sig("y_mm", 2 * (LEVELS - 1)), sig("z_mm", 2 * (LEVELS - 1))
        kh_mm, x_mm, u_mm, o_mm, su_mm = sig("kh_mm"), sig("x_mm", NC - 1), sig("u_mm", NC), sig("o_mm", NC), sig("su_mm", NC - 1)
        yT_mm, out_mm = sig("yT_mm"), sig("out_mm")
        turn_mm = sig("turn_mm", 2 * (LEVELS - 2))
        pe_signals = (turn_mm, q_mm, k_mm, a_mm, v_mm, ssq_mm, bb_mm, diag_mm, lvl_mm, tr_mm, y_mm, z_mm, kh_mm, x_mm, u_mm,
                      o_mm, su_mm, yT_mm, out_mm)
        q_read, k_read, alpha_done, norm_sqrt = sig("q_read", 2), sig("k_read", 2), sig("alpha_done"), sig("norm_sqrt")
        u_copy, y_copy, kh_copy, rms_sqrt, yT_copy = (sig("u_copy", NC), sig("y_copy", 2 * (LEVELS - 1)), sig("kh_copy"),
                                                      sig("rms_sqrt"), sig("yT_copy"))
        tT_copy = sig("tT_copy", 2 * (LEVELS - 2))
        act_signals = (tT_copy, q_read, k_read, alpha_done, norm_sqrt, u_copy, y_copy, kh_copy, rms_sqrt, yT_copy)
        norm_steps, bv_done, kab_done, kq_start = sig("norm_steps", 4), sig("bv_done"), sig("kab_done"), sig("kq_start", 2)
        diag_done, lvl_done, kq_up = sig("diag_done", 2), sig("lvl_done", 2 * LEVELS), sig("kq_up", LEVELS)
        t_start, t_up, x_done, o_done, s_done = (sig("t_start", 2), sig("t_up", 2 * (LEVELS - 1)), sig("x_done", NC - 1),
                                                 sig("o_done", NC), sig("s_done", 2 * (NC - 1)))
        y_sum, y_recip, acc_done = sig("y_sum"), sig("y_recip"), sig("acc_done")
        dve_signals = (norm_steps, bv_done, kab_done, kq_start, diag_done, lvl_done, kq_up, t_start, t_up, x_done,
                       o_done, s_done, y_sum, y_recip, acc_done)
        kr_up, tot_up, tT_start, mt_up, y_sq, y_norm = (sig("kr_up", LEVELS), sig("tot_up", LEVELS), sig("tT_start", 2),
                                                       sig("mt_up", 2 * LEVELS), sig("y_sq"), sig("y_norm"))
        pool_signals = (kr_up, tot_up, tT_start, mt_up, y_sq, y_norm)
        wc_ready = ctx.enter_context(nc.semaphore("b_wc_ready"))
        woc_ready = ctx.enter_context(nc.semaphore("b_woc_ready"))

        def tile(c):
            return slice(c * C, (c + 1) * C)

        def m_slot(l, h):
            return 2 * LEVELS + 2 * (l % 2) + h

        def rows(h):
            return slice(h * DK, (h + 1) * DK)

        tot_at = [None] + [T - (T >> (l - 1)) for l in range(1, LEVELS)]

        def block_products(l, par, second, outer, n_rep):
            t, off = (al, 0) if l == 0 else (tot, tot_at[l])
            dims = [[2, T >> (l + 1)]] + ([[0, n_rep]] if n_rep > 1 else [])
            return view(t, off + (1 if second else 0), ([[0, outer]] if outer else []) + dims)

        block = ctx.enter_context(nc.Block())

        @block.tensor
        def _(pe):
            for s in pe_signals:
                pe.sem_inc(s.sem, s.per)

            def chain_x(hp, b, c):
                p = 1 - b % 2
                pe.wait_ge(s_done.sem, s_done.at(hp, b, 2 * c))
                pe.wait_ge(o_done.sem, o_done.at(hp, b, c))
                if c == 1:
                    pe.wait_ge(kq_up.sem, kq_up.at(hp, b - 1))
                nc.tensor.matmul(cx[:, 0:P], kq[p][:, 0, tile(c)], st[:, :], start=True, stop=True).then_inc(x_mm.sem, 1)

            def chain_u(hp, b, c):
                p = 1 - b % 2
                if c == 0:
                    pe.wait_ge(t_up.sem, t_up.at(hp, b - 1))
                    pe.wait_ge(bv_done.sem, bv_done.at(hp, b - 1))
                else:
                    pe.wait_ge(x_done.sem, x_done.at(hp, b, c))
                for h in range(2):
                    rhs = bv[p][:, 0, h, :] if c == 0 else xsb[:, h, :]
                    mm = nc.tensor.matmul(cu[:, h * DK:(h + 1) * DK], tt[p][:, h, 1, tile(c)], rhs,
                                          start=True, stop=True)
                mm.then_inc(u_mm.sem, 1)

            def chain_o(hp, b, c):
                p = 1 - b % 2
                pe.wait_ge(u_copy.sem, u_copy.at(hp, b, c + 1))
                if c == 0:
                    pe.wait_ge(mt_up.sem, mt_up.at(hp, b - 1))
                    pe.wait_ge(kh_copy.sem, kh_copy.at(hp, b - 1))
                    pe.wait_ge(o_done.sem, o_done.at(hp, b - 1))
                if c > 0:
                    nc.tensor.matmul(cx[:, P:2 * P], kq[p][:, 1, tile(c)], st[:, :], start=True, stop=False)
                if c < NC - 1:
                    nc.tensor.matmul(cu[:, P:2 * P], kh[p][:, c, :], us[:, :, :], start=True,
                                     stop=True).then_inc(su_mm.sem, 1)
                for h in range(2):
                    mm = nc.tensor.matmul(cx[:, P + h * DK:P + (h + 1) * DK], mt[p][:, h, tile(c)], us[:, h, :],
                                          start=(c == 0), stop=(c == 0 or h == 1))
                mm.then_inc(o_mm.sem, 1)

            def level(hp, b, l):
                n, q = 1 << l, kq[b % 2]
                if l == 0:
                    pe.wait_ge(kq_start.sem, kq_start.at(hp, b))
                else:
                    pe.wait_ge(kq_up.sem, kq_up.at(hp, b, l))
                    pe.wait_ge(kr_up.sem, kr_up.at(hp, b, l))
                for h in range(2):
                    if l == 0:
                        pe.wait_ge(diag_done.sem, diag_done.at(hp, b, h + 1))
                    else:
                        pe.wait_ge(lvl_done.sem, lvl_done.at(hp, b, 2 * (l - 1) + h + 1))
                    for c in range(NC):
                        mm = nc.tensor.matmul(
                            view(lv, h * 512 + c * HALF, [[NC * HALF, 2], [1, HALF]]), kr2[b % 2][rows(h), tile(c)],
                            halves(q, c * C, n, True, C, [T, 2], DK, h * DK), start=True, stop=True)
                    mm.then_inc(lvl_mm.sem, 1)

            def times_t(hp, b, l):
                t = tt[b % 2]
                for h in range(2):
                    pe.wait_ge(lvl_done.sem, lvl_done.at(hp, b, 2 * l + h + 1))
                    if l == 1:
                        pe.wait_ge(t_start.sem, t_start.at(hp, b, h + 1))
                        pe.wait_ge(tT_start.sem, tT_start.at(hp, b, h + 1))
                    else:
                        pe.wait_ge(t_up.sem, t_up.at(hp, b, 2 * (l - 1)))
                        if h == 1:
                            pe.wait_ge(tT_copy.sem, tT_copy.at(hp, b, 2 * (l - 2) + 1))
                    for c in range(NC):
                        mm = nc.tensor.matmul(wk[:, h, tile(c)], em[:, 2 * l + h, tile(c)], t[:, h, 0, tile(c)],
                                              start=True, stop=True)
                    mm.then_inc(y_mm.sem, 1)

            def t_times(hp, b, l):
                t = tt[b % 2]
                for h in range(2):
                    pe.wait_ge(y_copy.sem, y_copy.at(hp, b, 2 * (l - 1) + h + 1))
                    if l > 1:
                        pe.wait_ge(tT_copy.sem, tT_copy.at(hp, b, 2 * (l - 1)))
                    for c in range(NC):
                        if l < LEVELS - 1:
                            mm = nc.tensor.matmul(wk[:, 2 - 2 * h, tile(c)], t[:, h, 1, tile(c)], ysb[:, h, tile(c)],
                                                  start=True, stop=True)
                        else:
                            mm = nc.tensor.matmul(wk[:, h, tile(c)], ysb[:, h, tile(c)], t[:, h, 1, tile(c)],
                                                  start=True, stop=True)
                    mm.then_inc(z_mm.sem, 1)

            def turn_t(hp, b, l):
                for h in range(2):
                    pe.wait_ge(t_up.sem, t_up.at(hp, b, 2 * (l - 1) + h + 1))
                    for c in range(NC):
                        mm = nc.tensor.transpose(wk[:, 1 + h, tile(c)], tt[b % 2][:, h, 0, tile(c)], ident[:, :])
                    mm.then_inc(turn_mm.sem, 1)

            def prep_q(hp, b):
                if b == B:
                    pe.wait_ge(wc_ready, hp * 2 + 4)
                if b == 0:
                    pe.wait_ge(wc_ready, 2)
                pe.wait_ge(kh_copy.sem, kh_copy.at(hp, b - 1 if b == 0 else b - 2))
                nc.tensor.matmul(pj[:, :], wc[:, 0, :], hT[:, b % B, :], start=True, stop=True).then_inc(q_mm.sem, 1)

            def prep_k(hp, b):
                pe.wait_ge(q_read.sem, q_read.at(hp, b))
                nc.tensor.matmul(pj[:, :], wc[:, 1, :], hT[:, b % B, :], start=True, stop=True).then_inc(k_mm.sem, 1)

            def prep_a(hp, b):
                pe.wait_ge(k_read.sem, k_read.at(hp, b))
                nc.tensor.matmul(pj[:, :], wc[:, 2, :], hT[:, b % B, :], start=True, stop=True).then_inc(a_mm.sem, 1)

            def prep_ssq(hp, b):
                pe.wait_ge(alpha_done.sem, alpha_done.at(hp, b))
                for i in range(2):
                    for c in range(NC):
                        mm = nc.tensor.matmul(pj[:, (i * NC + c) * 2:(i * NC + c) * 2 + 2], sqb[:, i, tile(c)],
                                              sel[:, :], start=True, stop=True)
                mm.then_inc(ssq_mm.sem, 1)

            def prep_v(hp, b):
                pe.wait_ge(norm_sqrt.sem, norm_sqrt.at(hp, b))
                w = wv[:, hp + b // B, :]
                for c in range(NC):
                    mm = nc.tensor.matmul(pj[:, tile(c)], hT[:, b % B, tile(c)], w, start=True, stop=True)
                mm.then_inc(v_mm.sem, 1)

            def prep_bb(hp, b):
                pe.wait_ge(norm_steps.sem, norm_steps.at(hp, b))
                pe.wait_ge(bv_done.sem, bv_done.at(hp, b))
                for c in range(NC):
                    mm = nc.tensor.matmul(pj[:, tile(c)], bk2[:, c, :], ident[:, :], start=True, stop=True)
                mm.then_inc(bb_mm.sem, 1)

            def step(hp, b):
                kr = kr2[b % 2]
                pe.wait_ge(lvl_done.sem, lvl_done.at(hp, b - 1))
                for h in range(2):
                    for c in range(NC):
                        mm = nc.tensor.matmul(lv[:, h, tile(c)], kr[rows(h), tile(c)], qs[rows(h), tile(c)],
                                              start=True, stop=True)
                    mm.then_inc(diag_mm.sem, 1)
                chain_u(hp, b, 0)
                level(hp, b, 0)
                chain_o(hp, b, 0)
                for h in range(2):
                    pe.wait_ge(lvl_done.sem, lvl_done.at(hp, b, h + 1))
                    for c in range(NC):
                        mm = nc.tensor.transpose(wk[:, h, tile(c)], em[:, h, tile(c)], ident[:, :])
                    mm.then_inc(tr_mm.sem, 1)
                chain_x(hp, b, 1)
                level(hp, b, 1)
                prep_q(hp, b + 1)
                chain_u(hp, b, 1)
                times_t(hp, b, 1)
                chain_o(hp, b, 1)
                level(hp, b, 2)
                prep_k(hp, b + 1)
                chain_x(hp, b, 2)
                t_times(hp, b, 1)
                chain_u(hp, b, 2)
                turn_t(hp, b, 1)
                times_t(hp, b, 2)
                chain_o(hp, b, 2)
                level(hp, b, 3)
                prep_a(hp, b + 1)
                chain_x(hp, b, 3)
                t_times(hp, b, 2)
                chain_u(hp, b, 3)
                turn_t(hp, b, 2)
                times_t(hp, b, 3)
                chain_o(hp, b, 3)
                level(hp, b, 4)
                t_times(hp, b, 3)
                prep_ssq(hp, b + 1)
                turn_t(hp, b, 3)
                times_t(hp, b, 4)
                level(hp, b, 5)
                t_times(hp, b, 4)
                prep_v(hp, b + 1)
                turn_t(hp, b, 4)
                times_t(hp, b, 5)
                level(hp, b, 6)
                t_times(hp, b, 5)
                prep_bb(hp, b + 1)
                turn_t(hp, b, 5)
                pe.wait_ge(y_norm.sem, y_norm.at(hp, b))
                pe.wait_ge(kab_done.sem, kab_done.at(hp, b + 1))
                for c in range(NC):
                    mm = nc.tensor.transpose(pj[:, tile(c)], yn[:, c, :], ident[:, :])
                mm.then_inc(yT_mm.sem, 1)
                times_t(hp, b, 6)
                project(hp, b)
                t_times(hp, b, 6)
                pe.wait_ge(kr_up.sem, kr_up.at(hp, b))
                pe.wait_ge(acc_done.sem, acc_done.at(hp, b))
                for c in range(NC):
                    mm = nc.tensor.transpose(pj[:, tile(c)], kr[:, tile(c)], ident[:, :])
                mm.then_inc(kh_mm.sem, 1)

            def project(hp, b):
                pe.wait_ge(yT_copy.sem, yT_copy.at(hp, b))
                if b <= 1:
                    pe.wait_ge(woc_ready, hp + 1 + b)
                nc.tensor.matmul(pj[:, :], woc[:, :], yT[:, :], start=True, stop=True).then_inc(out_mm.sem, 1)

            for prepare in (prep_q, prep_k, prep_a, prep_ssq, prep_v, prep_bb):
                prepare(0, 0)
            with pe.Fori(0, HP) as hp:
                for b in range(B):
                    step(hp, b)
            hp, b = HP, 0
            chain_u(hp, b, 0)
            chain_o(hp, b, 0)
            for c in range(1, NC):
                chain_x(hp, b, c)
                chain_u(hp, b, c)
                chain_o(hp, b, c)
            pe.wait_ge(y_norm.sem, y_norm.at(hp, b))
            for c in range(NC):
                mm = nc.tensor.transpose(pj[:, tile(c)], yn[:, c, :], ident[:, :])
            mm.then_inc(yT_mm.sem, 1)
            project(hp, b)

        @block.scalar
        def _(act):
            for s in act_signals:
                act.sem_inc(s.sem, s.per)

            def copy_u(hp, b, c):
                act.wait_ge(u_mm.sem, u_mm.at(hp, b, c + 1))
                act.wait_ge(o_mm.sem, o_mm.at(hp, b, c))
                nc.scalar.activation(us[:, :, :], cu[:, 0:P].rearrange("p (h d) -> p h d", h=2),
                                     ACT.Copy).then_inc(u_copy.sem, 1)

            def copy_y(hp, b, l):
                for h in range(2):
                    act.wait_ge(y_mm.sem, y_mm.at(hp, b, 2 * (l - 1) + h + 1))
                    nc.scalar.activation(ysb[:, h, :], wk[:, h, :], ACT.Copy).then_inc(y_copy.sem, 1)

            def copy_tT(hp, b, l):
                for h in range(2):
                    act.wait_ge(turn_mm.sem, turn_mm.at(hp, b, 2 * (l - 1) + h + 1))
                    nc.scalar.activation(tt[b % 2][:, h, 1, :], wk[:, 1 + h, :], ACT.Copy).then_inc(tT_copy.sem, 1)

            def rms(hp, b):
                act.wait_ge(y_sum.sem, y_sum.at(hp, b))
                nc.scalar.activation(ysd[:, :], yss[:, :], ACT.Sqrt, bias=keep["rms_eps"][:, :],
                                     scale=1.0 / DK).then_inc(rms_sqrt.sem, 1)

            def copy_yT(hp, b):
                act.wait_ge(yT_mm.sem, yT_mm.at(hp, b))
                act.wait_ge(out_mm.sem, out_mm.at(hp, b - 1))
                nc.scalar.activation(yT[:, :], pj[:, :], ACT.Copy).then_inc(yT_copy.sem, 1)

            def read_q(hp, b):
                act.wait_ge(q_mm.sem, q_mm.at(hp, b))
                act.wait_ge(ssq_mm.sem, ssq_mm.at(hp, b - 1))
                nc.scalar.activation(sqb[:, 0, :], pj[:, :], ACT.Square).then_inc(q_read.sem, 1)
                act.wait_ge(kq_start.sem, kq_start.at(hp, b - 1))
                act.wait_ge(diag_mm.sem, diag_mm.at(hp, b - 1))
                nc.scalar.activation(qs[:, :], pj[:, :], ACT.Copy).then_inc(q_read.sem, 1)

            def read_k(hp, b):
                act.wait_ge(k_mm.sem, k_mm.at(hp, b))
                nc.scalar.activation(sqb[:, 1, :], pj[:, :], ACT.Square).then_inc(k_read.sem, 1)
                nc.scalar.activation(kr2[b % 2][:, :], pj[:, :], ACT.Copy).then_inc(k_read.sem, 1)

            def read_a(hp, b):
                act.wait_ge(a_mm.sem, a_mm.at(hp, b))
                if b == B:
                    act.wait_ge(wc_ready, hp * 2 + 4)
                act.wait_ge(kq_up.sem, kq_up.at(hp, b - 1, 1))
                act.wait_ge(tot_up.sem, tot_up.at(hp, b - 1, 1))
                nc.scalar.activation(al[:, :], pj[:, :], ACT.Sigmoid, bias=abc[:, :]).then_inc(alpha_done.sem, 1)

            def read_ssq(hp, b):
                act.wait_ge(ssq_mm.sem, ssq_mm.at(hp, b))
                act.wait_ge(norm_steps.sem, norm_steps.at(hp, b - 1))
                nc.scalar.activation(nrm[:, :, :, :].rearrange("p i c h -> p (i c h)"), pj[:, 0:4 * NC],
                                     ACT.Sqrt).then_inc(norm_sqrt.sem, 1)

            def step(hp, b):
                copy_u(hp, b, 0)
                read_q(hp, b + 1)
                copy_u(hp, b, 1)
                copy_y(hp, b, 1)
                read_k(hp, b + 1)
                copy_u(hp, b, 2)
                copy_tT(hp, b, 1)
                copy_y(hp, b, 2)
                read_a(hp, b + 1)
                copy_u(hp, b, 3)
                copy_tT(hp, b, 2)
                copy_y(hp, b, 3)
                read_ssq(hp, b + 1)
                copy_tT(hp, b, 3)
                copy_y(hp, b, 4)
                rms(hp, b)
                copy_tT(hp, b, 4)
                copy_y(hp, b, 5)
                copy_tT(hp, b, 5)
                copy_yT(hp, b)
                copy_y(hp, b, 6)
                act.wait_ge(kh_mm.sem, kh_mm.at(hp, b))
                nc.scalar.activation(kh[b % 2][:, :, :], pj[:, :].rearrange("p (c d) -> p c d", c=NC),
                                     ACT.Copy).then_inc(kh_copy.sem, 1)

            act.wait_ge(wc_ready, 2)
            for read in (read_q, read_k, read_a, read_ssq):
                read(0, 0)
            with act.Fori(0, HP) as hp:
                for b in range(B):
                    step(hp, b)
            for c in range(NC):
                copy_u(HP, 0, c)
            rms(HP, 0)
            copy_yT(HP, 0)

        @block.vector
        def _(dve):
            for s in dve_signals:
                dve.sem_inc(s.sem, s.per)

            def take_o(hp, b, c):
                p = 1 - b % 2
                dve.wait_ge(o_mm.sem, o_mm.at(hp, b, c + 1))
                if c == 0:
                    dve.wait_ge(y_norm.sem, y_norm.at(hp, b - 1))
                nc.vector.tensor_tensor(yt[:, c], cx[:, P:2 * P].rearrange("p (h d) -> p h d", h=2),
                                        view(rn[p], c * 2, [[1, 2], [0, DK]]), ALU.mult).then_inc(o_done.sem, 1)

            def take_s(hp, b, c):
                p = 1 - b % 2
                dve.wait_ge(su_mm.sem, su_mm.at(hp, b, c + 1))
                if c == 0:
                    dve.wait_ge(o_mm.sem, o_mm.at(hp, b - 1))
                    dve.wait_ge(tot_up.sem, tot_up.at(hp, b - 1))
                for h in range(2):
                    add = cu[rows(h), P + h * DK:P + (h + 1) * DK]
                    if c == 0:
                        nc.vector.tensor_copy(st[rows(h), rows(h)], add).then_inc(s_done.sem, 1)
                    else:
                        nc.vector.scalar_tensor_tensor(out=st[rows(h), rows(h)], in0=st[rows(h), rows(h)],
                                                       scalar=totc[p][rows(h), c:c + 1], in1=add,
                                                       op0=ALU.mult, op1=ALU.add).then_inc(s_done.sem, 1)

            def take_x(hp, b, c):
                p = 1 - b % 2
                dve.wait_ge(x_mm.sem, x_mm.at(hp, b, c))
                dve.wait_ge(u_mm.sem, u_mm.at(hp, b, c))
                nc.vector.tensor_tensor(xsb[:, :, :], bv[p][:, c], cx[:, 0:P].rearrange("p (h d) -> p h d", h=2), ALU.subtract).then_inc(x_done.sem, 1)

            def take_level(hp, b, l):
                n = 1 << l
                mask = view(masks, l * NC * HALF, [[0, 2], [n, T // 2 // n], [1, n]])
                for h in range(2):
                    dve.wait_ge(lvl_mm.sem, lvl_mm.at(hp, b, 2 * l + h + 1))
                    if h == 0:
                        if l == 0:
                            dve.wait_ge(tr_mm.sem, tr_mm.at(hp, b - 1))
                            dve.wait_ge(tT_start.sem, tT_start.at(hp, b - 1))
                        else:
                            dve.wait_ge(y_mm.sem, y_mm.at(hp, b - 1, 2 * l))
                        if l < 2:
                            dve.wait_ge(mt_up.sem, mt_up.at(hp, b - 1))
                        else:
                            dve.wait_ge(mt_up.sem, mt_up.at(hp, b, 2 * l - 2))
                    nc.vector.tensor_tensor(
                        halves(em, (2 * l + h) * T, n, True, T, [(m_slot(l, h) - 2 * l - h) * T, 2]),
                        view(lv, h * 512, [[NC * HALF, 2], [n, T // 2 // n], [1, n]]), mask,
                        ALU.mult).then_inc(lvl_done.sem, 1)

            def grow_kq(hp, b, l):
                n, q = 1 << l, kq[b % 2]
                dve.wait_ge(lvl_mm.sem, lvl_mm.at(hp, b, 2 * l + 2))
                if l == 0:
                    dve.wait_ge(kq_start.sem, kq_start.at(hp, b))
                else:
                    dve.wait_ge(kq_up.sem, kq_up.at(hp, b, l))
                    dve.wait_ge(tot_up.sem, tot_up.at(hp, b, l))
                v = halves(q, 0, n, True, T, [T, 2])
                nc.vector.tensor_tensor(v, v, block_products(l, b % 2, False, 2, n), ALU.mult).then_inc(kq_up.sem, 1)

            def take_t(hp, b, l):
                n, last = 1 << l, l == LEVELS - 1
                for h in range(2):
                    dve.wait_ge(z_mm.sem, z_mm.at(hp, b, 2 * (l - 1) + h + 1))
                    v = halves(tt[b % 2], (h * 2 + last) * T, n, last, T)
                    z = halves(wk, (h if last else 2 - 2 * h) * 512, n, last, T)
                    nc.vector.tensor_tensor(v, v, z, ALU.subtract).then_inc(t_up.sem, 1)

            def sum_y(hp, b):
                dve.wait_ge(y_sq.sem, y_sq.at(hp, b))
                dve.wait_ge(rms_sqrt.sem, rms_sqrt.at(hp, b - 1))
                nc.vector.tensor_reduce(yss[:, :], ysq[:, :, :, :].rearrange("p c h d -> p (c h) d"), AX.X,
                                        ALU.add).then_inc(y_sum.sem, 1)

            def invert_y(hp, b):
                dve.wait_ge(rms_sqrt.sem, rms_sqrt.at(hp, b))
                dve.wait_ge(y_norm.sem, y_norm.at(hp, b - 1))
                nc.vector.reciprocal(yr[:, :], ysd[:, :]).then_inc(y_recip.sem, 1)

            def add_out(hp, b):
                dve.wait_ge(out_mm.sem, out_mm.at(hp, b))
                a = acc[:, (b - 1) % B, :]
                nc.vector.tensor_tensor(a, a, pj[:, :], ALU.add).then_inc(acc_done.sem, 1)

            def norms(hp, b):
                r = rn[b % 2]
                dve.wait_ge(norm_sqrt.sem, norm_sqrt.at(hp, b))
                nc.vector.tensor_scalar(nre[:], nrm[:], RMS_EPS, None, ALU.add).then_inc(norm_steps.sem, 1)
                dve.wait_ge(norm_steps.sem, norm_steps.at(hp, b, 1))
                nc.vector.reciprocal(r[:], nre[:]).then_inc(norm_steps.sem, 1)
                dve.wait_ge(norm_steps.sem, norm_steps.at(hp, b, 2))
                heads = bass.ds((hp + b // B) * 2, 2)
                nc.vector.tensor_tensor(bk[:, :, :], beta[:, b % B, :, heads], r[:, 1], ALU.mult).then_inc(norm_steps.sem, 1)
                dve.wait_ge(norm_steps.sem, norm_steps.at(hp, b, 3))
                dve.wait_ge(bb_mm.sem, bb_mm.at(hp, b - 1))
                nc.vector.tensor_tensor(
                    bk2[:, :, :].rearrange("p c (h d) -> p (c h) d", h=2), view(bk, 0, [[1, 2 * NC], [0, DK]]),
                    view(r, 2 * NC, [[1, 2 * NC], [0, DK]]), ALU.mult).then_inc(norm_steps.sem, 1)

            def scale_v(hp, b):
                dve.wait_ge(v_mm.sem, v_mm.at(hp, b))
                dve.wait_ge(norm_steps.sem, norm_steps.at(hp, b, 3))
                nc.vector.tensor_tensor(
                    bv[b % 2][:, :, :, :].rearrange("p c h d -> p (c h) d"),
                    pj[:, :].rearrange("p (c d) -> p c d", d=DK), view(bk, 0, [[1, 2 * NC], [0, DK]]),
                    ALU.mult).then_inc(bv_done.sem, 1)

            def scale_alpha(hp, b):
                dve.wait_ge(bb_mm.sem, bb_mm.at(hp, b))
                dve.wait_ge(alpha_done.sem, alpha_done.at(hp, b))
                nc.vector.tensor_tensor(ka[:, :], pj[:, :], al[:, :], ALU.mult).then_inc(kab_done.sem, 1)

            def start_kq(hp, b):
                q = kq[b % 2]
                dve.wait_ge(q_read.sem, q_read.at(hp, b))
                nc.vector.tensor_tensor(q[:, 1, :], qs[:, :], al[:, :], ALU.mult).then_inc(kq_start.sem, 1)
                dve.wait_ge(kab_done.sem, kab_done.at(hp, b))
                dve.wait_ge(k_read.sem, k_read.at(hp, b))
                nc.vector.tensor_tensor(q[:, 0, :], ka[:, :], kr2[b % 2][:, :], ALU.mult).then_inc(kq_start.sem, 1)

            def step(hp, b):
                for h in range(2):
                    dve.wait_ge(diag_mm.sem, diag_mm.at(hp, b, h + 1))
                    nc.vector.tensor_tensor(mt[b % 2][:, h, :], lv[:, h, :], ident4[:, :],
                                            ALU.mult).then_inc(diag_done.sem, 1)
                take_level(hp, b, 0)
                grow_kq(hp, b, 0)
                take_s(hp, b, 0)
                take_o(hp, b, 0)
                for h in range(2):
                    dve.wait_ge(tr_mm.sem, tr_mm.at(hp, b, h + 1))
                    nc.vector.tensor_tensor(tt[b % 2][:, h, 0, :], ident4[:, :], wk[:, h, :],
                                            ALU.subtract).then_inc(t_start.sem, 1)
                take_x(hp, b, 1)
                take_level(hp, b, 1)
                grow_kq(hp, b, 1)
                take_s(hp, b, 1)
                take_o(hp, b, 1)
                take_level(hp, b, 2)
                grow_kq(hp, b, 2)
                take_x(hp, b, 2)
                take_t(hp, b, 1)
                take_s(hp, b, 2)
                take_o(hp, b, 2)
                take_level(hp, b, 3)
                grow_kq(hp, b, 3)
                take_x(hp, b, 3)
                take_t(hp, b, 2)
                take_o(hp, b, 3)
                take_level(hp, b, 4)
                grow_kq(hp, b, 4)
                take_t(hp, b, 3)
                norms(hp, b + 1)
                sum_y(hp, b)
                take_level(hp, b, 5)
                grow_kq(hp, b, 5)
                take_t(hp, b, 4)
                scale_v(hp, b + 1)
                invert_y(hp, b)
                take_level(hp, b, 6)
                grow_kq(hp, b, 6)
                take_t(hp, b, 5)
                scale_alpha(hp, b + 1)
                start_kq(hp, b + 1)
                add_out(hp, b)
                take_t(hp, b, 6)

            for prepare in (norms, scale_v, scale_alpha, start_kq):
                prepare(0, 0)
            with dve.Fori(0, HP) as hp:
                for b in range(B):
                    step(hp, b)
            for c in range(NC):
                if c > 0:
                    take_x(HP, 0, c)
                if c < NC - 1:
                    take_s(HP, 0, c)
                take_o(HP, 0, c)
            sum_y(HP, 0)
            invert_y(HP, 0)
            add_out(HP, 0)

        @block.gpsimd
        def _(pool):
            for s in pool_signals:
                pool.sem_inc(s.sem, s.per)
            pool.sem_inc(woc_ready, 1)

            def add_m(hp, b, l):
                n, m = 1 << l, mt[b % 2]
                for h in range(2):
                    pool.wait_ge(lvl_done.sem, lvl_done.at(hp, b, 2 * l + h + 1))
                    if l > 0:
                        pool.wait_ge(mt_up.sem, mt_up.at(hp, b, 2 * (l - 1) + h + 1))
                    v = halves(m, h * T, n, True, T)
                    nc.gpsimd.tensor_tensor(v, v, halves(em, m_slot(l, h) * T, n, True, T),
                                            ALU.add).then_inc(mt_up.sem, 1)

            def grow_kr(hp, b, l):
                n = 1 << l
                pool.wait_ge(lvl_mm.sem, lvl_mm.at(hp, b, 2 * l + 2))
                if l == 0:
                    pool.wait_ge(alpha_done.sem, alpha_done.at(hp, b))
                    pool.wait_ge(kq_start.sem, kq_start.at(hp, b))
                else:
                    pool.wait_ge(kr_up.sem, kr_up.at(hp, b, l))
                    pool.wait_ge(tot_up.sem, tot_up.at(hp, b, l))
                v = halves(kr2[b % 2], 0, n, False, T)
                nc.gpsimd.tensor_tensor(v, v, block_products(l, b % 2, True, None, n), ALU.mult).then_inc(kr_up.sem, 1)
                out = view(tot, tot_at[l + 1], [[1, T >> (l + 1)]]) if l < LEVELS - 1 else totc[b % 2][:, :]
                pool.wait_ge(kq_up.sem, kq_up.at(hp, b - 1))
                nc.gpsimd.tensor_tensor(out, block_products(l, b % 2, False, None, 1),
                                        block_products(l, b % 2, True, None, 1), ALU.mult).then_inc(tot_up.sem, 1)

            def square_y(hp, b):
                pool.wait_ge(o_done.sem, o_done.at(hp, b))
                pool.wait_ge(y_sum.sem, y_sum.at(hp, b - 1))
                nc.gpsimd.tensor_tensor(ysq[:], yt[:], yt[:], ALU.mult).then_inc(y_sq.sem, 1)

            def norm_y(hp, b):
                pool.wait_ge(y_recip.sem, y_recip.at(hp, b))
                pool.wait_ge(yT_mm.sem, yT_mm.at(hp, b - 1))
                nc.gpsimd.tensor_tensor(yn[:, :, :].rearrange("p c (h d) -> p (c h) d", h=2),
                                        yt[:, :, :, :].rearrange("p c h d -> p (c h) d"),
                                        view(yr, 0, [[1, 2 * NC], [0, DK]]), ALU.mult).then_inc(y_norm.sem, 1)

            def step(hp, b):
                if b == B - 1:
                    pool.wait_ge(a_mm.sem, a_mm.at(hp, b))
                    pool.wait_ge(alpha_done.sem, alpha_done.at(hp, b))
                    nc.gpsimd.tensor_copy(wc[:, :, :], wqka[:, :, hp + 1, :]).then_inc(wc_ready, 1)
                    nc.gpsimd.tensor_copy(abc[:, :], ab[:, bass.ds(hp + 1, 1)]).then_inc(wc_ready, 1)
                grow_kr(hp, b, 0)
                for h in range(2):
                    pool.wait_ge(lvl_done.sem, lvl_done.at(hp, b, h + 1))
                    nc.gpsimd.tensor_tensor(tt[b % 2][:, h, 1, :], ident4[:, :], em[:, h, :],
                                            ALU.subtract).then_inc(tT_start.sem, 1)
                add_m(hp, b, 0)
                for l in range(1, LEVELS):
                    grow_kr(hp, b, l)
                    add_m(hp, b, l)
                    if l == 3:
                        square_y(hp, b)
                    if l == 5:
                        norm_y(hp, b)
                if b == 0:
                    pool.wait_ge(out_mm.sem, out_mm.at(hp, b))
                    nc.gpsimd.tensor_copy(woc[:, :], wo[:, hp, :]).then_inc(woc_ready, 1)

            nc.gpsimd.tensor_copy(wc[:, :, :], wqka[:, :, 0, :]).then_inc(wc_ready, 1)
            nc.gpsimd.tensor_copy(abc[:, :], ab[:, 0:1]).then_inc(wc_ready, 1)
            with pool.Fori(0, HP) as hp:
                for b in range(B):
                    step(hp, b)
            square_y(HP, 0)
            norm_y(HP, 0)


def loop_at(s, b, k=None):
    return b * s.per + (s.per + (s.per if k is None else k))


def stage_c(nc, io, keep):
    with ExitStack() as ctx:
        sb = lambda n, s: ctx.enter_context(nc.sbuf_tensor("c_" + n, s, F32))
        ps = lambda n, s: ctx.enter_context(nc.psum_tensor("c_" + n, s, F32))
        sig = lambda n, per=1: Signal(ctx, nc, "c_" + n, per)
        at = loop_at
        xT, xnT, gateT, acc, mean_w = (keep[k] for k in ("xT", "xnT", "gateT", "acc", "mean_w"))
        NF = 512 // P
        ffn_w = sb("ffn_w", [P, 1]); w1 = sb("w1", [P, NF, P]); w3 = sb("w3", [P, NF, P]); w2 = sb("w2", [P, NF, D])
        tg = sb("tg", [P, T]); y1 = sb("y1", [P, T]); sq = sb("sq", [P, T]); sd = sb("sd", [P, T]); rs = sb("rs", [P, T])
        y2 = sb("y2", [P, T]); sl = sb("sl", [P, 2, T]); g = sb("g", [P, 2, T]); y3 = sb("y3", [P, T])
        x2 = sb("x2", [P, T]); xm = sb("xm", [P, T])
        pM = ps("pM", [P, T]); p1 = ps("p1", [P, 2, T]); p3 = ps("p3", [P, 2, T]); pO = ps("pO", [P, T]); pV = ps("pV", [P, T])
        weights_in = ctx.enter_context(nc.semaphore("c_weights_in"))
        ms_mm, w1_mm, w3_mm, w2_mm, mean_mm, var_mm = (
            sig("ms_mm"), sig("w1_mm", NF), sig("w3_mm", NF), sig("w2_mm", NF), sig("mean_mm"), sig("var_mm"))
        sq_ms, sd_ms, silu_done, sq_var, sd_var = sig("sq_ms"), sig("sd_ms"), sig("silu_done", NF), sig("sq_var"), sig("sd_var")
        y_sum, r_ms, y_norm, g_done, y_ff, x_sum, centred, r_var, x_norm = (
            sig("y_sum"), sig("r_ms"), sig("y_norm"), sig("g_done", NF), sig("y_ff"), sig("x_sum"), sig("centred"),
            sig("r_var"), sig("x_norm"))
        gated, kept = sig("gated"), sig("kept")
        loads = [(ffn_w[:, :], io["ff_norm_w"].rearrange("(p o) -> p o", o=1)),
                 (w1[:, :, :], io["ff_w1"].rearrange("d (m n) -> d m n", n=P)),
                 (w3[:, :, :], io["ff_w3"].rearrange("d (m n) -> d m n", n=P)),
                 (w2[:, :, :], io["ff_w2"].rearrange("(m p) d -> p m d", p=P))]
        block = ctx.enter_context(nc.Block())

        @block.sync
        def _(sp):
            for dst, src in loads:
                sp.dma_start(dst, src).then_inc(weights_in, 16)

        @block.gpsimd
        def _(pool):
            for s in (gated, kept):
                pool.sem_inc(s.sem, s.per)
            with pool.Fori(0, B) as b:
                pool.wait_ge(y_sum.sem, at(y_sum, b, 0))
                nc.gpsimd.tensor_tensor(tg[:, :], acc[:, b, :], gateT[:, b, :], ALU.mult).then_inc(gated.sem, 1)
                pool.wait_ge(x_sum.sem, at(x_sum, b))
                nc.gpsimd.tensor_copy(xT[:, b, :], x2[:, :]).then_inc(kept.sem, 1)

        @block.tensor
        def _(pe):
            for s in (ms_mm, w1_mm, w3_mm, w2_mm, mean_mm, var_mm):
                pe.sem_inc(s.sem, s.per)
            pe.wait_ge(weights_in, 16 * len(loads))
            with pe.Fori(0, B) as b:
                pe.wait_ge(sq_ms.sem, at(sq_ms, b))
                pe.wait_ge(centred.sem, at(centred, b, 0))
                nc.tensor.matmul(pM[:, :], mean_w[:, :], sq[:, :], start=True, stop=True).then_inc(ms_mm.sem, 1)
                pe.wait_ge(y_norm.sem, at(y_norm, b))

                def ff_in(m):
                    pe.wait_ge(g_done.sem, at(g_done, b, m - 1) if m else at(g_done, b, 0))
                    nc.tensor.matmul(p1[:, m % 2, :], w1[:, m, :], y2[:, :], start=True, stop=True).then_inc(w1_mm.sem, 1)
                    nc.tensor.matmul(p3[:, m % 2, :], w3[:, m, :], y2[:, :], start=True, stop=True).then_inc(w3_mm.sem, 1)

                ff_in(0)
                for m in range(NF):
                    if m + 1 < NF:
                        ff_in(m + 1)
                    pe.wait_ge(g_done.sem, at(g_done, b, m + 1))
                    if m == 0:
                        pe.wait_ge(y_ff.sem, at(y_ff, b, 0))
                    nc.tensor.matmul(pO[:, :], w2[:, m, :], g[:, m % 2, :], start=(m == 0),
                                     stop=(m == NF - 1)).then_inc(w2_mm.sem, 1)
                pe.wait_ge(x_sum.sem, at(x_sum, b))
                pe.wait_ge(sd_ms.sem, at(sd_ms, b))
                nc.tensor.matmul(pM[:, :], mean_w[:, :], x2[:, :], start=True, stop=True).then_inc(mean_mm.sem, 1)
                pe.wait_ge(sq_var.sem, at(sq_var, b))
                nc.tensor.matmul(pV[:, :], mean_w[:, :], sq[:, :], start=True, stop=True).then_inc(var_mm.sem, 1)

        @block.scalar
        def _(act):
            for s in (sq_ms, sd_ms, silu_done, sq_var, sd_var):
                act.sem_inc(s.sem, s.per)
            with act.Fori(0, B) as b:
                act.wait_ge(y_sum.sem, at(y_sum, b))
                nc.scalar.activation(sq[:, :], y1[:, :], ACT.Square).then_inc(sq_ms.sem, 1)
                act.wait_ge(ms_mm.sem, at(ms_mm, b))
                nc.scalar.activation(sd[:, :], pM[:, :], ACT.Sqrt, bias=keep["rms_eps"][:, :]).then_inc(sd_ms.sem, 1)
                for m in range(NF):
                    act.wait_ge(w1_mm.sem, at(w1_mm, b, m + 1))
                    act.wait_ge(g_done.sem, at(g_done, b, max(m - 1, 0)))
                    nc.scalar.activation(sl[:, m % 2, :], p1[:, m % 2, :], ACT.Silu).then_inc(silu_done.sem, 1)
                act.wait_ge(centred.sem, at(centred, b))
                nc.scalar.activation(sq[:, :], xm[:, :], ACT.Square).then_inc(sq_var.sem, 1)
                act.wait_ge(var_mm.sem, at(var_mm, b))
                act.wait_ge(r_ms.sem, at(r_ms, b))
                nc.scalar.activation(sd[:, :], pV[:, :], ACT.Sqrt, bias=keep["ln_eps"][:, :]).then_inc(sd_var.sem, 1)

        @block.vector
        def _(dve):
            for s in (y_sum, r_ms, y_norm, g_done, y_ff, x_sum, centred, r_var, x_norm):
                dve.sem_inc(s.sem, s.per)
            dve.wait_ge(weights_in, 16 * len(loads))
            with dve.Fori(0, B) as b:
                dve.wait_ge(gated.sem, at(gated, b))
                nc.vector.tensor_tensor(y1[:, :], tg[:, :], xnT[:, b, :], ALU.add).then_inc(y_sum.sem, 1)
                dve.wait_ge(sd_ms.sem, at(sd_ms, b))
                dve.wait_ge(x_norm.sem, at(x_norm, b, 0))
                nc.vector.reciprocal(rs[:, :], sd[:, :]).then_inc(r_ms.sem, 1)
                dve.wait_ge(r_ms.sem, at(r_ms, b))
                dve.wait_ge(w3_mm.sem, at(w3_mm, b, 0))
                dve.wait_ge(y_sum.sem, at(y_sum, b))
                nc.vector.scalar_tensor_tensor(out=y2[:, :], in0=y1[:, :], scalar=ffn_w[:, 0:1], in1=rs[:, :],
                                               op0=ALU.mult, op1=ALU.mult).then_inc(y_norm.sem, 1)
                for m in range(NF):
                    dve.wait_ge(silu_done.sem, at(silu_done, b, m + 1))
                    dve.wait_ge(w3_mm.sem, at(w3_mm, b, m + 1))
                    dve.wait_ge(w2_mm.sem, at(w2_mm, b, max(m - 1, 0)))
                    nc.vector.tensor_tensor(g[:, m % 2, :], sl[:, m % 2, :], p3[:, m % 2, :], ALU.mult).then_inc(g_done.sem, 1)
                dve.wait_ge(w2_mm.sem, at(w2_mm, b))
                nc.vector.tensor_tensor(y3[:, :], y1[:, :], pO[:, :], ALU.add).then_inc(y_ff.sem, 1)
                dve.wait_ge(y_ff.sem, at(y_ff, b))
                dve.wait_ge(kept.sem, at(kept, b, 0))
                nc.vector.tensor_tensor(x2[:, :], y3[:, :], xT[:, b, :], ALU.add).then_inc(x_sum.sem, 1)
                dve.wait_ge(mean_mm.sem, at(mean_mm, b))
                dve.wait_ge(x_sum.sem, at(x_sum, b))
                nc.vector.tensor_tensor(xm[:, :], x2[:, :], pM[:, :], ALU.subtract).then_inc(centred.sem, 1)
                dve.wait_ge(sd_var.sem, at(sd_var, b))
                nc.vector.reciprocal(rs[:, :], sd[:, :]).then_inc(r_var.sem, 1)
                dve.wait_ge(r_var.sem, at(r_var, b))
                dve.wait_ge(centred.sem, at(centred, b))
                nc.vector.tensor_tensor(xnT[:, b, :], xm[:, :], rs[:, :], ALU.mult).then_inc(x_norm.sem, 1)


AH = 8
AP2 = AH // 2
INNER = AH * DK
WINDOW = 64
LAYERS = 2
HID = int(D * 4 * 2 / 3)
HM = [128, 128, HID - 256]
NEG = -3.0e38


def rotary_tables():
    half = np.arange(0, DK, 2, dtype=np.float32)
    inv_freq = (1.0 / 10000.0 ** (half / DK)).astype(np.float32)
    t = np.arange(T, dtype=np.float32)
    fr = (t[:, None] * inv_freq[None, :]).astype(np.float32).astype(np.float64)
    base = ((half + 0.4 * DK) / (1.4 * DK)).astype(np.float64)
    power = (t.astype(np.float64) - T // 2) / (WINDOW // 2)
    scale = base[None, :] ** power[:, None]
    cos, sin = np.cos(fr), np.sin(fr)
    q_scale = 8.0

    def pack(f, signed):
        lo, hi = (-f, f) if signed else (f, f)
        q = np.concatenate([lo * scale, hi * scale], -1) * q_scale
        k = np.concatenate([lo / scale, hi / scale], -1)
        return np.stack([q, k], 1)

    def lay(a):
        return np.ascontiguousarray(a.reshape(NC, C, 2, DK).transpose(1, 0, 2, 3)).astype(np.float32)

    return lay(pack(cos, False)), lay(pack(sin, True))


def attention_mask():
    i = np.arange(C)[:, None] + C
    j = np.arange(2 * C)[None, :]
    window = (i // WINDOW) * WINDOW
    ok = (j <= i) & (j + WINDOW >= i) & (j >= window - WINDOW)
    return np.where(ok, 0.0, NEG).astype(np.float32)


def stage_d(nc, io, keep, out):
    with ExitStack() as ctx:
        nm_ = "d_"
        sb = lambda n, s: ctx.enter_context(nc.sbuf_tensor(nm_ + n, s, F32))
        ps = lambda n, s: ctx.enter_context(nc.psum_tensor(nm_ + n, s, F32))
        signals = {"pe": [], "act": [], "dve": [], "pool": [], "sp": []}

        def sig(by, n, per=1):
            s = Signal(ctx, nc, nm_ + n, per)
            signals[by].append(s)
            return s

        xdT, x2T, ident, mean_w = keep["xnT"], keep["xT"], keep["ident"], keep["mean_w"]
        wqkv = sb("wqkv", [P, 3, INNER]); wo = sb("wo", [P, AP2, D]); w1 = sb("w1", [P, 2, HID]); w2 = sb("w2", [P, 3, D])
        b1 = sb("b1", [P, 2, 3]); b2 = sb("b2", [P, 1]); lg = sb("lg", [P, 1]); lb = sb("lb", [P, 1])
        mask = sb("mask", [P, 2 * C]); tcos = sb("tcos", [P, NC, 2, DK]); tsin = sb("tsin", [P, NC, 2, DK])
        sc = sb("sc", [P, 2, DK])
        xb = sb("xb", [P, T]); hs = sb("hs", [P, T]); sq = sb("sq", [P, 2, INNER]); ssq = sb("ssq", [P, 16])
        nrm = sb("nrm", [P, 16]); nmx = sb("nmx", [P, 16]); rn = sb("rn", [P, 16])
        qn = sb("qn", [P, 2, AH, DK]); qc = sb("qc", [P, 2, AH, DK]); qx = sb("qx", [P, 2, AH, DK]); qr = sb("qr", [P, 2 * INNER])
        vs = sb("vs", [P, NC, INNER]); qT = sb("qT", [P, AP2, C]); kT = sb("kT", [P, AP2, T])
        sm = sb("sm", [P, AH, 2 * C]); mx = sb("mx", [P, AH]); ex = sb("ex", [P, AH, 2 * C]); den = sb("den", [P, AH])
        rd = sb("rd", [P, AH]); pT = sb("pT", [P, AH, 2 * C]); o = sb("o", [P, INNER]); oT = sb("oT", [P, AP2, T])
        x1 = sb("x1", [P, T]); xm = sb("xm", [P, T]); sq1 = sb("sq1", [P, T]); sd = sb("sd", [P, T]); rs = sb("rs", [P, T])
        hn = sb("hn", [P, T]); hf = sb("hf", [P, T]); gl = sb("gl", [P, T]); hm = sb("hm", [P, 2, T]); xo = sb("xo", [P, T])
        pqk = ps("pqk", [P, 2, 512]); pv = ps("pv", [P, 512]); psm = ps("psm", [P, 4, 512]); po = ps("po", [P, 512])

        weights_in = ctx.enter_context(nc.semaphore(nm_ + "weights_in"))
        prepared = ctx.enter_context(nc.semaphore(nm_ + "prepared"))
        stored = ctx.enter_context(nc.semaphore(nm_ + "stored"))
        shifted, kept = sig("dve", "shifted", 2), sig("pool", "kept")
        cos_done = sig("pool", "cos_done", NC)
        q_mm, k_mm, v_mm, qkT_mm, o_mm, oT_mm = (
            sig("pe", n, NC) for n in ("q_mm", "k_mm", "v_mm", "qkT_mm", "o_mm", "oT_mm"))
        s_mm, pT_mm = sig("pe", "s_mm", 2 * NC), sig("pe", "pT_mm", 2 * NC)
        wo_mm, mean_mm, var_mm, a_mm, g_mm, w2_mm, out_mm = (
            sig("pe", "wo_mm"), sig("pe", "mean_mm"), sig("pe", "var_mm"), sig("pe", "a_mm", 3), sig("pe", "g_mm", 3),
            sig("pe", "w2_mm", 3), sig("pe", "out_mm"))
        squared, v_copy, norm_sqrt, qT_copy, exped, pT_copy, oT_copy = (
            sig("act", "squared", 2 * NC), sig("act", "v_copy", NC), sig("act", "norm_sqrt", NC), sig("act", "qT_copy", NC),
            sig("act", "exped", 2 * NC), sig("act", "pT_copy", NC), sig("act", "oT_copy", NC))
        sq_var, sd_var, gelu_done, out_copy = (sig("act", "sq_var"), sig("act", "sd_var"), sig("act", "gelu_done", 3),
                                               sig("act", "out_copy"))
        q_sum, norm_steps, q_norm, rot, q_rot, kT_copy, masked, maxed, r_den, p_half, o_norm = (
            sig("dve", "q_sum", NC), sig("dve", "norm_steps", 2 * NC), sig("dve", "q_norm", NC), sig("dve", "rot", 2 * NC),
            sig("dve", "q_rot", NC), sig("dve", "kT_copy", NC), sig("dve", "masked", 2 * NC), sig("dve", "maxed", 2 * NC),
            sig("dve", "r_den", NC), sig("dve", "p_half", NC), sig("dve", "o_norm", NC))
        hf_zero = sig("dve", "hf_zero", 3)
        x_sum, centred, r_var, normed, scaled, mid, x_done, total = (
            sig("dve", "x_sum"), sig("dve", "centred"), sig("dve", "r_var"), sig("dve", "normed"), sig("dve", "scaled"),
            sig("dve", "mid", 3), sig("dve", "x_done"), sig("dve", "total"))
        x_out = sig("sp", "x_out")

        def tile(c):
            return slice(c * C, (c + 1) * C)

        def ff_bank(m, i):
            return psm[:, 2 + i, :] if m == 1 else pqk[:, i, :]

        last_only = (out_mm, out_copy, total)

        def credit(eng, by, layer):
            for s in signals[by]:
                if s in last_only and layer == LAYERS - 1:
                    eng.sem_inc(s.sem, B * (LAYERS - 1) * s.per)
                if layer == 0:
                    eng.sem_inc(s.sem, s.per)

        def run_layer(layer):
            last_layer = layer == LAYERS - 1

            def at(s, b, k=None):
                return b * s.per + (layer * B * s.per + s.per + (s.per if k is None else k))

            col = lambda a: a.rearrange("(p o) -> p o", o=1)
            loads = [(wqkv[:, :, :], io["wqkv"][layer].rearrange("d (i n) -> d i n", i=3)),
                     (wo[:, :, :], io["wo"][layer].rearrange("(m p) d -> p m d", p=P)),
                     (w1[:, :, :], io["w1"][layer].rearrange("d (i n) -> d i n", i=2)),
                     (w2[:, 0:2, :], io["w2"][layer][0:256].rearrange("(m p) d -> p m d", p=P)),
                     (w2[0:HM[2], 2, :], io["w2"][layer][256:HID]),
                     (b2[:, :], col(io["b2"][layer])), (lg[:, :], col(io["ln_g"][layer])), (lb[:, :], col(io["ln_b"][layer])),
                     (mask[:, :], io["mask"]), (tcos[:, :, :, :], io["tcos"]), (tsin[:, :, :, :], io["tsin"]),
                     (sc[:, 0, :], io["q_scale"][layer].rearrange("(o d) -> o d", o=1).to_broadcast([P, DK])),
                     (sc[:, 1, :], io["k_scale"][layer].rearrange("(o d) -> o d", o=1).to_broadcast([P, DK]))]
            for i in range(2):
                for m in range(3):
                    lo = i * HID + m * P
                    loads.append((b1[0:HM[m], i, m:m + 1], col(io["b1"][layer][lo:lo + HM[m]])))

            with nc.Block() as block:
                @block.sync
                def _(sp):
                    with nc.allow_non_contiguous_dma(reason="small per-channel vectors"):
                        for dst, src in loads:
                            sp.dma_start(dst, src).then_inc(weights_in, 16)

                @block.vector
                def _(dve):
                    nc.vector.memset(hs[:, :], 0.0)
                    dve.wait_ge(weights_in, 16 * len(loads) * (layer + 1))
                    for c in range(NC):
                        nc.vector.tensor_tensor(tcos[:, c], tcos[:, c], sc[:, :, :], ALU.mult).then_inc(prepared, 1)
                        for d in range(2):
                            a = tsin[:, c, :, d * 32:d * 32 + 32]
                            nc.vector.tensor_tensor(a, a, sc[:, :, 32 - d * 32:64 - d * 32], ALU.mult).then_inc(prepared, 1)

            with nc.Block() as block:

                @block.gpsimd
                def _(pool):
                    credit(pool, "pool", layer)

                    def turn_cos(b, c):
                        pool.wait_ge(q_norm.sem, at(q_norm, b, c + 1))
                        pool.wait_ge(q_rot.sem, at(q_rot, b, c))
                        nc.gpsimd.tensor_tensor(qc[:, :, :, :], qn[:, :, :, :],
                                                view(tcos, c * 2 * DK, [[DK, 2], [0, AH], [1, DK]]), ALU.mult).then_inc(cos_done.sem, 1)

                    def batch(b, ahead):
                        pool.wait_ge(x_sum.sem, at(x_sum, b, 0))
                        nc.gpsimd.tensor_copy(xb[:, :], xdT[:, b, :]).then_inc(kept.sem, 1)
                        for c in range(1, NC):
                            turn_cos(b, c)
                        if ahead:
                            turn_cos(b + 1, 0)

                    turn_cos(0, 0)
                    with pool.Fori(0, B - 1) as b:
                        batch(b, True)
                    batch(B - 1, False)

                @block.tensor
                def _(pe):
                    credit(pe, "pe", layer)
                    def project(b, c):
                        pe.wait_ge(qT_copy.sem, at(qT_copy, b, c))
                        pe.wait_ge(kT_copy.sem, at(kT_copy, b, c))
                        if c == 0:
                            pe.wait_ge(shifted.sem, at(shifted, b))
                        if c == 1:
                            pe.wait_ge(gelu_done.sem, at(gelu_done, b, 0))
                            pe.wait_ge(mid.sem, at(mid, b, 0))
                        nc.tensor.matmul(pqk[:, 0, :], hs[:, tile(c)], wqkv[:, 0, :], start=True, stop=True).then_inc(q_mm.sem, 1)
                        nc.tensor.matmul(pqk[:, 1, :], hs[:, tile(c)], wqkv[:, 1, :], start=True, stop=True).then_inc(k_mm.sem, 1)
                        pe.wait_ge(v_copy.sem, at(v_copy, b, c))
                        if c == 1:
                            pe.wait_ge(x_done.sem, at(x_done, b, 0))
                        nc.tensor.matmul(pv[:, :], hs[:, tile(c)], wqkv[:, 2, :], start=True, stop=True).then_inc(v_mm.sem, 1)

                    def turn(b, c):
                        pe.wait_ge(q_rot.sem, at(q_rot, b, c + 1))
                        for i in range(2):
                            for m in range(AP2):
                                mm = nc.tensor.transpose(pqk[:, i, tile(m)], qr[:, (i * AP2 + m) * P:(i * AP2 + m + 1) * P], ident[:, :])
                        mm.then_inc(qkT_mm.sem, 1)

                    def score(b, c):
                        pe.wait_ge(qT_copy.sem, at(qT_copy, b, c + 1))
                        pe.wait_ge(kT_copy.sem, at(kT_copy, b, c + 1))
                        lo = 0 if c else C
                        pe.wait_ge(pT_copy.sem, at(pT_copy, b, c))
                        pe.wait_ge(p_half.sem, at(p_half, b, c))
                        if c == 0:
                            pe.wait_ge(x_sum.sem, at(x_sum, b, 0))
                            pe.wait_ge(centred.sem, at(centred, b, 0))
                            pe.wait_ge(sd_var.sem, at(sd_var, b, 0))
                        for e in range(2):
                            r = slice(e * DK, e * DK + DK)
                            for m in range(AP2):
                                mm = nc.tensor.matmul(psm[:, e * 2 + m // 2, (m % 2) * 256 + lo:(m % 2) * 256 + 256], qT[r, m, :],
                                                      kT[r, m, (c - 1) * C + lo:(c + 1) * C], start=True, stop=True)
                            mm.then_inc(s_mm.sem, 1)

                    def turn_p(b, c):
                        for g in range(2):
                            pe.wait_ge(exped.sem, at(exped, b, 2 * c + g + 1))
                            for hd in range(4 * g, 4 * g + 4):
                                for w in range(1 if c == 0 else 0, 2):
                                    mm = nc.tensor.transpose(psm[:, hd // 2, (hd % 2) * 256 + w * C:(hd % 2) * 256 + w * C + C],
                                                             ex[:, hd, w * C:(w + 1) * C], ident[:, :])
                            mm.then_inc(pT_mm.sem, 1)

                    def mix(b, c):
                        pe.wait_ge(p_half.sem, at(p_half, b, c + 1))
                        pe.wait_ge(v_copy.sem, at(v_copy, b, c + 1))
                        pe.wait_ge(oT_copy.sem, at(oT_copy, b, c))
                        if c == 0 and last_layer:
                            pe.wait_ge(out_copy.sem, at(out_copy, b, 0))
                        for hd in range(AH):
                            if hd == AH // 2:
                                pe.wait_ge(pT_copy.sem, at(pT_copy, b, c + 1))
                            for w in range(1 if c == 0 else 0, 2):
                                mm = nc.tensor.matmul(po[:, hd * DK:(hd + 1) * DK], pT[:, hd, w * C:(w + 1) * C],
                                                      vs[:, c - 1 + w, slot_cols(hd)], start=(w == 0 or c == 0), stop=(w == 1))
                        mm.then_inc(o_mm.sem, 1)

                    def turn_o(b, c):
                        pe.wait_ge(o_norm.sem, at(o_norm, b, c + 1))
                        for m in range(AP2):
                            mm = nc.tensor.transpose(po[:, tile(m)], o[:, tile(m)], ident[:, :])
                        mm.then_inc(oT_mm.sem, 1)

                    def batch(b, ahead):
                        for c in range(NC):
                            nxt = (b, c + 1) if c + 1 < NC else (b + 1, 0)
                            go = ahead or c + 1 < NC
                            score(b, c)
                            if go:
                                project(*nxt)
                            turn_p(b, c)
                            mix(b, c)
                            if go:
                                turn(*nxt)
                            turn_o(b, c)
                        pe.wait_ge(oT_copy.sem, at(oT_copy, b))
                        for m in range(AP2):
                            mm = nc.tensor.matmul(psm[:, 0, :], wo[:, m, :], oT[:, m, :], start=(m == 0), stop=(m == AP2 - 1))
                        mm.then_inc(wo_mm.sem, 1)
                        pe.wait_ge(hf_zero.sem, at(hf_zero, b))
                        nc.tensor.matmul(psm[:, 1, :], mean_w[:, :], hf[:, :], start=True, stop=True).then_inc(mean_mm.sem, 1)
                        pe.wait_ge(sq_var.sem, at(sq_var, b))
                        nc.tensor.matmul(psm[:, 2, :], mean_w[:, :], sq1[:, :], start=True, stop=True).then_inc(var_mm.sem, 1)
                        pe.wait_ge(scaled.sem, at(scaled, b))
                        if ahead:
                            pe.wait_ge(qT_copy.sem, at(qT_copy, b + 1, 1))
                            pe.wait_ge(kT_copy.sem, at(kT_copy, b + 1, 1))
                            pe.wait_ge(v_copy.sem, at(v_copy, b + 1, 1))

                        def ff_in(m):
                            n = HM[m]
                            nc.tensor.matmul(ff_bank(m, 0)[0:n, :], w1[:, 0, m * P:m * P + n], hn[:, :], start=True, stop=True).then_inc(a_mm.sem, 1)
                            nc.tensor.matmul(ff_bank(m, 1)[0:n, :], w1[:, 1, m * P:m * P + n], hn[:, :], start=True, stop=True).then_inc(g_mm.sem, 1)

                        ff_in(0)
                        ff_in(1)
                        for m in range(3):
                            n = HM[m]
                            pe.wait_ge(mid.sem, at(mid, b, m + 1))
                            if m == 0:
                                pe.wait_ge(gelu_done.sem, at(gelu_done, b, 1))
                                ff_in(2)
                            nc.tensor.matmul(pv[:, :], w2[0:n, m, :], hm[0:n, m % 2, :], start=(m == 0), stop=(m == 2)).then_inc(w2_mm.sem, 1)
                        if last_layer:
                            pe.wait_ge(total.sem, at(total, b))
                            for c in range(NC):
                                mm = nc.tensor.transpose(po[:, tile(c)], xo[:, tile(c)], ident[:, :])
                            mm.then_inc(out_mm.sem, 1)

                    project(0, 0)
                    turn(0, 0)
                    with pe.Fori(0, B - 1) as b:
                        batch(b, True)
                    batch(B - 1, False)

                @block.scalar
                def _(act):
                    credit(act, "act", layer)
                    def square(b, c):
                        act.wait_ge(q_sum.sem, at(q_sum, b, c))
                        for i, s in enumerate((q_mm, k_mm)):
                            act.wait_ge(s.sem, at(s, b, c + 1))
                            nc.scalar.activation(sq[:, i, :], pqk[:, i, :], ACT.Square).then_inc(squared.sem, 1)
                        act.wait_ge(v_mm.sem, at(v_mm, b, c + 1))
                        if c < 2:
                            act.wait_ge(o_mm.sem, at(o_mm, b, 2 - NC if c == 0 else 0))
                        nc.scalar.activation(vs[:, c, :], pv[:, :], ACT.Copy).then_inc(v_copy.sem, 1)

                    def root(b, c):
                        act.wait_ge(q_sum.sem, at(q_sum, b, c + 1))
                        act.wait_ge(norm_steps.sem, at(norm_steps, b, 2 * c))
                        nc.scalar.activation(nrm[:, :], ssq[:, :], ACT.Sqrt).then_inc(norm_sqrt.sem, 1)

                    def copy_q(b, c):
                        act.wait_ge(qkT_mm.sem, at(qkT_mm, b, c + 1))
                        act.wait_ge(s_mm.sem, at(s_mm, b, 2 * c))
                        nc.scalar.activation(qT[:, :, :], pqk[:, 0, :].rearrange("p (m t) -> p m t", m=AP2), ACT.Copy).then_inc(qT_copy.sem, 1)

                    def exponent(b, c):
                        act.wait_ge(pT_mm.sem, at(pT_mm, b, 2 * c))
                        act.wait_ge(r_den.sem, at(r_den, b, c))
                        lo = 0 if c else C
                        for g in range(2):
                            act.wait_ge(maxed.sem, at(maxed, b, 2 * c + g + 1))
                            for hd in range(4 * g, 4 * g + 4):
                                a = nc.scalar.activation(ex[:, hd, lo:], sm[:, hd, lo:], ACT.Exp, bias=mx[:, hd:hd + 1],
                                                         accum_out=den[:, hd:hd + 1])
                            a.then_inc(exped.sem, 1)

                    def copy_p(b, c):
                        lo = 0 if c else C
                        act.wait_ge(pT_mm.sem, at(pT_mm, b, 2 * c + 2))
                        act.wait_ge(o_mm.sem, at(o_mm, b, c))
                        nc.scalar.activation(pT[:, 4:8, lo:], psm[:, 2:4, :].rearrange("p e (m j) -> p (e m) j", m=2)[:, :, lo:], ACT.Copy).then_inc(pT_copy.sem, 1)

                    def copy_o(b, c):
                        act.wait_ge(oT_mm.sem, at(oT_mm, b, c + 1))
                        if c == 0:
                            act.wait_ge(wo_mm.sem, at(wo_mm, b, 0))
                        nc.scalar.activation(oT[:, :, tile(c)], po[:, :].rearrange("p (m t) -> p m t", m=AP2), ACT.Copy).then_inc(oT_copy.sem, 1)

                    def batch(b, ahead):
                        for c in range(NC):
                            nxt = (b, c + 1) if c + 1 < NC else (b + 1, 0)
                            go = ahead or c + 1 < NC
                            if go:
                                square(*nxt)
                            exponent(b, c)
                            if go:
                                root(*nxt)
                            copy_p(b, c)
                            if go:
                                copy_q(*nxt)
                            copy_o(b, c)
                        act.wait_ge(centred.sem, at(centred, b))
                        act.wait_ge(var_mm.sem, at(var_mm, b, 0))
                        nc.scalar.activation(sq1[:, :], xm[:, :], ACT.Square).then_inc(sq_var.sem, 1)
                        act.wait_ge(var_mm.sem, at(var_mm, b))
                        act.wait_ge(r_var.sem, at(r_var, b, 0))
                        nc.scalar.activation(sd[:, :], psm[:, 2, :], ACT.Sqrt, bias=keep["ln_eps"][:, :]).then_inc(sd_var.sem, 1)
                        for m in range(3):
                            n = HM[m]
                            act.wait_ge(g_mm.sem, at(g_mm, b, m + 1))
                            act.wait_ge(mid.sem, at(mid, b, m))
                            nc.scalar.activation(gl[0:n, :], ff_bank(m, 1)[0:n, :], ACT.Gelu, bias=b1[0:n, 1, m:m + 1]).then_inc(gelu_done.sem, 1)
                        if last_layer:
                            act.wait_ge(out_mm.sem, at(out_mm, b))
                            act.wait_ge(x_out.sem, b * 16 + 1)
                            nc.scalar.activation(hf[:, :], po[:, :], ACT.Copy).then_inc(out_copy.sem, 1)

                    square(0, 0)
                    root(0, 0)
                    copy_q(0, 0)
                    with act.Fori(0, B - 1) as b:
                        batch(b, True)
                    batch(B - 1, False)

                @block.vector
                def _(dve):
                    credit(dve, "dve", layer)
                    def shift(b):
                        dve.wait_ge(v_mm.sem, at(v_mm, b, 0))
                        nc.vector.tensor_copy(hs[0:DK, :], xdT[0:DK, b, :]).then_inc(shifted.sem, 1)
                        nc.vector.tensor_copy(hs[DK:P, 1:T], xdT[DK:P, b, 0:T - 1]).then_inc(shifted.sem, 1)

                    def sum_squares(b, c):
                        dve.wait_ge(squared.sem, at(squared, b, 2 * c + 2))
                        dve.wait_ge(norm_sqrt.sem, at(norm_sqrt, b, c))
                        nc.vector.tensor_reduce(ssq[:, :], sq[:, :, :].rearrange("p i (h d) -> p (i h) d", d=DK), AX.X, ALU.add).then_inc(q_sum.sem, 1)

                    def normalise(b, c):
                        dve.wait_ge(norm_sqrt.sem, at(norm_sqrt, b, c + 1))
                        nc.vector.tensor_scalar(nmx[:, :], nrm[:, :], 1e-12, None, ALU.max).then_inc(norm_steps.sem, 1)
                        dve.wait_ge(norm_steps.sem, at(norm_steps, b, 2 * c + 1))
                        nc.vector.reciprocal(rn[:, :], nmx[:, :]).then_inc(norm_steps.sem, 1)
                        dve.wait_ge(norm_steps.sem, at(norm_steps, b, 2 * c + 2))
                        dve.wait_ge(cos_done.sem, at(cos_done, b, c))
                        dve.wait_ge(k_mm.sem, at(k_mm, b, c + 1))
                        nc.vector.tensor_tensor(qn[:, :, :, :].rearrange("p i h d -> p (i h) d"),
                                                pqk[:, :, :].rearrange("p i (h d) -> p (i h) d", d=DK),
                                                view(rn, 0, [[1, 16], [0, DK]]), ALU.mult).then_inc(q_norm.sem, 1)

                    def rotate(b, c):
                        dve.wait_ge(q_norm.sem, at(q_norm, b, c + 1))
                        for d in range(2):
                            nc.vector.tensor_tensor(qx[:, :, :, d * 32:d * 32 + 32], qn[:, :, :, 32 - d * 32:64 - d * 32],
                                                    view(tsin, c * 2 * DK + d * 32, [[DK, 2], [0, AH], [1, 32]]), ALU.mult).then_inc(rot.sem, 1)
                        dve.wait_ge(rot.sem, at(rot, b, 2 * c + 2))
                        dve.wait_ge(cos_done.sem, at(cos_done, b, c + 1))
                        dve.wait_ge(qkT_mm.sem, at(qkT_mm, b, c))
                        nc.vector.tensor_tensor(qr[:, :], qc[:, :, :, :].rearrange("p i h d -> p (i h d)"),
                                                qx[:, :, :, :].rearrange("p i h d -> p (i h d)"), ALU.add).then_inc(q_rot.sem, 1)

                    def copy_k(b, c):
                        dve.wait_ge(qkT_mm.sem, at(qkT_mm, b, c + 1))
                        nc.vector.tensor_copy(kT[:, :, tile(c)], pqk[:, 1, :].rearrange("p (m t) -> p m t", m=AP2)).then_inc(kT_copy.sem, 1)

                    def mask_max(b, c):
                        lo = 0 if c else C
                        dve.wait_ge(exped.sem, at(exped, b, 2 * c))
                        for g in range(2):
                            hd = slice(4 * g, 4 * g + 4)
                            dve.wait_ge(s_mm.sem, at(s_mm, b, 2 * c + g + 1))
                            nc.vector.tensor_tensor(sm[:, hd, lo:], psm[:, 2 * g:2 * g + 2, :].rearrange("p e (m j) -> p (e m) j", m=2)[:, :, lo:],
                                                    view(mask, lo, [[0, 4], [1, 2 * C - lo]]), ALU.add).then_inc(masked.sem, 1)
                            dve.wait_ge(masked.sem, at(masked, b, 2 * c + g + 1))
                            nc.vector.tensor_reduce(mx[:, hd], sm[:, hd, lo:], AX.X, ALU.max, negate=True).then_inc(maxed.sem, 1)

                    def invert_sum(b, c):
                        dve.wait_ge(exped.sem, at(exped, b, 2 * c + 2))
                        dve.wait_ge(o_norm.sem, at(o_norm, b, c))
                        nc.vector.reciprocal(rd[:, :], den[:, :]).then_inc(r_den.sem, 1)

                    def copy_p(b, c):
                        lo = 0 if c else C
                        dve.wait_ge(pT_mm.sem, at(pT_mm, b, 2 * c + 1))
                        dve.wait_ge(o_mm.sem, at(o_mm, b, c))
                        nc.vector.tensor_copy(pT[:, 0:4, lo:], psm[:, 0:2, :].rearrange("p e (m j) -> p (e m) j", m=2)[:, :, lo:]).then_inc(p_half.sem, 1)

                    def scale_o(b, c):
                        dve.wait_ge(o_mm.sem, at(o_mm, b, c + 1))
                        dve.wait_ge(r_den.sem, at(r_den, b, c + 1))
                        dve.wait_ge(oT_mm.sem, at(oT_mm, b, c))
                        for e in range(2):
                            ins = nc.vector.tensor_tensor(
                                view(o, e * DK, [[2 * DK, AP2], [1, DK]]), view(po, e * 4 * DK, [[DK, AP2], [1, DK]]),
                                view(rd, e * 4, [[1, AP2], [0, DK]]), ALU.mult)
                        ins.then_inc(o_norm.sem, 1)

                    def batch(b, ahead):
                        for c in range(NC):
                            nxt = (b, c + 1) if c + 1 < NC else (b + 1, 0)
                            go = ahead or c + 1 < NC
                            if go and c == NC - 1:
                                shift(b + 1)
                            mask_max(b, c)
                            if go:
                                sum_squares(*nxt)
                            copy_p(b, c)
                            invert_sum(b, c)
                            if go:
                                normalise(*nxt)
                            if go:
                                rotate(*nxt)
                            scale_o(b, c)
                            if go:
                                copy_k(*nxt)
                        dve.wait_ge(wo_mm.sem, at(wo_mm, b))
                        dve.wait_ge(kept.sem, at(kept, b))
                        nc.vector.tensor_tensor(x1[:, :], xb[:, :], psm[:, 0, :], ALU.add).then_inc(x_sum.sem, 1)
                        dve.wait_ge(x_sum.sem, at(x_sum, b))
                        if last_layer:
                            dve.wait_ge(x_out.sem, b * 16 + 1)
                        nc.vector.memset(hf[DK:P, 0:1], 0.0).then_inc(hf_zero.sem, 1)
                        nc.vector.tensor_copy(hf[0:DK, :], x1[0:DK, :]).then_inc(hf_zero.sem, 1)
                        nc.vector.tensor_copy(hf[DK:P, 1:T], x1[DK:P, 0:T - 1]).then_inc(hf_zero.sem, 1)
                        dve.wait_ge(mean_mm.sem, at(mean_mm, b))
                        dve.wait_ge(hf_zero.sem, at(hf_zero, b))
                        nc.vector.tensor_tensor(xm[:, :], hf[:, :], psm[:, 1, :], ALU.subtract).then_inc(centred.sem, 1)
                        dve.wait_ge(sd_var.sem, at(sd_var, b))
                        nc.vector.reciprocal(rs[:, :], sd[:, :]).then_inc(r_var.sem, 1)
                        dve.wait_ge(r_var.sem, at(r_var, b))
                        dve.wait_ge(g_mm.sem, at(g_mm, b, 0))
                        dve.wait_ge(centred.sem, at(centred, b))
                        nc.vector.tensor_tensor(rs[:, :], xm[:, :], rs[:, :], ALU.mult).then_inc(normed.sem, 1)
                        dve.wait_ge(normed.sem, at(normed, b))
                        nc.vector.tensor_scalar(hn[:, :], rs[:, :], lg[:, 0:1], lb[:, 0:1], ALU.mult, ALU.add).then_inc(scaled.sem, 1)
                        for m in range(3):
                            n = HM[m]
                            dve.wait_ge(a_mm.sem, at(a_mm, b, m + 1))
                            dve.wait_ge(gelu_done.sem, at(gelu_done, b, m + 1))
                            dve.wait_ge(w2_mm.sem, at(w2_mm, b, max(m - 1, 0)))
                            nc.vector.scalar_tensor_tensor(out=hm[0:n, m % 2, :], in0=ff_bank(m, 0)[0:n, :], scalar=b1[0:n, 0, m:m + 1],
                                                           in1=gl[0:n, :], op0=ALU.add, op1=ALU.mult).then_inc(mid.sem, 1)
                        dve.wait_ge(w2_mm.sem, at(w2_mm, b))
                        if last_layer:
                            dve.wait_ge(out_mm.sem, at(out_mm, b, 0))
                        xnew = xo[:, :] if last_layer else xdT[:, b, :]
                        nc.vector.scalar_tensor_tensor(out=xnew, in0=pv[:, :], scalar=b2[:, 0:1], in1=x1[:, :],
                                                       op0=ALU.add, op1=ALU.add).then_inc(x_done.sem, 1)
                        if last_layer:
                            dve.wait_ge(x_done.sem, at(x_done, b))
                            nc.vector.tensor_tensor(xo[:, :], xo[:, :], x2T[:, b, :], ALU.add).then_inc(total.sem, 1)

                    shift(0)
                    sum_squares(0, 0)
                    normalise(0, 0)
                    rotate(0, 0)
                    copy_k(0, 0)
                    with dve.Fori(0, B - 1) as b:
                        batch(b, True)
                    batch(B - 1, False)

                if last_layer:
                    out_v = out.rearrange("b (c p) d -> b p c d", p=P)

                    @block.sync
                    def _(sp):
                        sp.sem_inc(x_out.sem, 1)
                        with sp.Fori(0, B) as b:
                            sp.wait_ge(out_copy.sem, at(out_copy, b))
                            sp.dma_start(out_v[b], hf[:, :].rearrange("p (c d) -> p c d", c=NC)).then_inc(x_out.sem, 16)
                        sp.wait_ge(x_out.sem, 16 * B + 1)

        for layer in range(LAYERS):
            run_layer(layer)


def slot_cols(slot):
    head = 2 * (slot % 4) + slot // 4
    return slice(head * DK, (head + 1) * DK)


def build(nc, io, outs):
    with ExitStack() as ctx:
        sb = lambda n, s: ctx.enter_context(nc.sbuf_tensor(n, s, F32))
        keep = dict(ident=sb("ident", [P, P]), mean_w=sb("mean_w", [P, P]), xT=sb("xT", [P, B, T]),
                    xnT=sb("xnT", [P, B, T]), hT=sb("hT", [P, B, T]), gateT=sb("gateT", [P, B, T]),
                    acc=sb("acc", [P, B, T]), beta=sb("beta", [P, B, NC, H + 2]),
                    ln_eps=sb("ln_eps", [P, 1]), rms_eps=sb("rms_eps", [P, 1]))
        with nc.Block() as block:
            @block.vector
            def _(dve):
                nc.vector.memset(keep["ln_eps"][:, :], LN_EPS)
                nc.vector.memset(keep["rms_eps"][:, :], RMS_EPS)
        stage_a(nc, io, keep, None)
        stage_b(nc, io, keep)
        stage_c(nc, io, keep)
        stage_d(nc, io, keep, outs)


_INS = {'x': 'L0_attn_x', 'norm_in_w': 'L0_attn_norm_in_w', 'conv_w': 'L0_attn_conv_w', 'conv_b': 'L0_attn_conv_b',
        'q_w': 'L0_attn_q_w', 'k_w': 'L0_attn_k_w', 'v_w': 'L0_attn_v_w', 'out_w': 'L0_attn_out_w',
        'alpha_w': 'L0_attn_alpha_w', 'alpha_b': 'L0_attn_alpha_b', 'beta_w': 'L0_attn_beta_w',
        'beta_b': 'L0_attn_beta_b', 'head_norm_w': 'L0_attn_head_norm_w', 'u1_w': 'L0_attn_u1_w',
        'u1_b': 'L0_attn_u1_b', 'u2_w': 'L0_attn_u2_w', 'u2_b': 'L0_attn_u2_b',
        'ff_norm_w': 'L0_attn_ff_norm_w', 'ff_w1': 'L0_attn_ff_w1', 'ff_w3': 'L0_attn_ff_w3', 'ff_w2': 'L0_attn_ff_w2',
        'wqkv': 'L0_ffn_wqkv', 'q_scale': 'L0_ffn_q_scale', 'k_scale': 'L0_ffn_k_scale', 'wo': 'L0_ffn_wo',
        'ln_g': 'L0_ffn_ln_g', 'ln_b': 'L0_ffn_ln_b', 'w1': 'L0_ffn_w1', 'b1': 'L0_ffn_b1', 'w2': 'L0_ffn_w2',
        'b2': 'L0_ffn_b2'}


def kernel(**inputs):
    import concourse.bacc as _bacc
    from concourse.bass_utils import run_bass_kernel_spmd as _run

    nc = _bacc.Bacc("TRN2", target_bir_lowering=False, num_devices=1)
    arrays, io = {}, {}
    host = {k: np.ascontiguousarray(inputs[v]) for k, v in _INS.items()}
    host["ident"] = np.eye(P, dtype=np.float32)
    host["mean_w"] = np.full((P, P), 1.0 / D, np.float32)
    host["masks"] = level_consts()
    host["tcos"], host["tsin"] = rotary_tables()
    host["mask"] = attention_mask()
    host["sel"] = (np.arange(P)[:, None] // DK == np.arange(2)[None, :]).astype(np.float32)
    for name, a in host.items():
        arrays[f"in_{name}_dram"] = a
        io[name] = nc.dram_tensor(f"in_{name}_dram", a.shape, mybir.dt.from_np(a.dtype), kind="ExternalInput").ap()
    out = nc.dram_tensor("out_0_dram", (B, T, D), F32, kind="ExternalOutput").ap()
    build(nc, io, out)
    r = _run(nc, [arrays], core_ids=[0])
    return r.results[0]["out_0_dram"]
```
